# Optimizing a Trainium2 kernel written in Bass

```python
import numpy as np
import jax
import jax.numpy as jnp

def _softmax(x, axis=-1):
    return jax.nn.softmax(x, axis=axis)

def _gelu(x):
    return jax.nn.gelu(x, approximate=True)

def _silu(x):
    return jax.nn.silu(x)

def _sigmoid(x):
    return jax.nn.sigmoid(x)

def _layernorm(x, axis=-1, eps=1e-05):
    m = jnp.mean(x, axis=axis, keepdims=True)
    v = jnp.var(x, axis=axis, keepdims=True)
    return (x - m) / jnp.sqrt(v + eps)

def _scatter_add(tgt, idx, src, axis=0):
    return tgt.at[idx].add(src)

def _segment_sum(src, seg, n):
    return jax.ops.segment_sum(src, seg, n)
kernel_name = 'mk_vit_tower_cls_d4_tok_img256_r4_d806f5'

def setup_inputs(seed: int=0):
    np.random.seed(seed)
    _w = jnp.asarray

    def _rec_inputs():
        import jax
        import jax.numpy as jnp
        _rk = jax.random.key(seed)
        x = 7.22013e-05 + 1.00017 * jax.random.normal(jax.random.fold_in(_rk, 1), (8, 1, 1024, 64), jnp.float32)
        cls_tok = 0.02 * jax.random.normal(jax.random.fold_in(_rk, 5), (1, 1, 64), jnp.float32)
        return (x, cls_tok)
    x, cls_tok = _rec_inputs()

    def _L0_tok_setup():
        import jax, jax.numpy as jnp
        import numpy as np
        T, D_IN, D_INT, D_OUT, B = (1024, 64, 64, 64, 8)
        key = jax.random.key(seed)
        ks = jax.random.split(key, 12)
        s_in = 1.0 / np.sqrt(D_IN)
        s_int = 1.0 / np.sqrt(D_INT)
        return {'x_batched': jax.random.normal(ks[0], (B, 1, T, D_IN), dtype=jnp.float32), 'd_gamma_batched': jax.random.uniform(ks[1], (T, T), dtype=jnp.float32), 'Wq': jax.random.uniform(ks[2], (D_IN, D_INT), jnp.float32, -s_in, s_in), 'bq': jax.random.uniform(ks[3], (D_INT,), jnp.float32, -s_in, s_in), 'Wk': jax.random.uniform(ks[4], (D_IN, D_INT), jnp.float32, -s_in, s_in), 'bk': jax.random.uniform(ks[5], (D_INT,), jnp.float32, -s_in, s_in), 'Wv': jax.random.uniform(ks[6], (D_IN, D_INT), jnp.float32, -s_in, s_in), 'bv': jax.random.uniform(ks[7], (D_INT,), jnp.float32, -s_in, s_in), 'Wo': jax.random.uniform(ks[8], (D_INT, D_OUT), jnp.float32, -s_int, s_int), 'bo': jax.random.uniform(ks[9], (D_OUT,), jnp.float32, -s_int, s_int), 'prelu_a': jnp.float32(0.25)}
    _L0_tok_all = _L0_tok_setup()
    _L0_tok_in = {k: v for k, v in _L0_tok_all.items() if k in ('d_gamma_batched', 'Wq', 'bq', 'Wk', 'bk', 'Wv', 'bv', 'Wo', 'bo', 'prelu_a')}
    del _L0_tok_all

    def _L0_attn_setup():
        import jax, jax.numpy as jnp
        import numpy as np
        import math
        H = 8
        DH = 16
        DEPTH = 1
        LAMBDA_INIT = 0.8 - 0.6 * math.exp(-0.3 * DEPTH)
        LN_EPS = 1e-05
        key = jax.random.key(seed)
        ks = jax.random.split(key, 12)
        dim = 64
        inner = 2 * H * DH
        b, n = (2, 512)
        s = lambda fan_in: 1.0 / math.sqrt(fan_in)
        return {'x': jax.random.normal(ks[0], (b, n, dim), jnp.float32), 'Wq': jax.random.normal(ks[1], (dim, inner), jnp.float32) * s(dim), 'Wkv': jax.random.normal(ks[2], (dim, 2 * inner), jnp.float32) * s(dim), 'Wout': jax.random.normal(ks[3], (inner, dim), jnp.float32) * s(inner), 'bout': jnp.zeros((dim,), jnp.float32), 'Wg': jax.random.normal(ks[4], (dim, inner), jnp.float32) * s(dim), 'bg': jnp.ones((inner,), jnp.float32), 'lq1': jax.random.normal(ks[5], (DH,), jnp.float32) * 0.1, 'lk1': jax.random.normal(ks[6], (DH,), jnp.float32) * 0.1, 'lq2': jax.random.normal(ks[7], (DH,), jnp.float32) * 0.1, 'lk2': jax.random.normal(ks[8], (DH,), jnp.float32) * 0.1, 'ln_gamma': jnp.ones((2 * DH,), jnp.float32), 'ln_beta': jnp.zeros((2 * DH,), jnp.float32)}
    _L0_attn_all = _L0_attn_setup()
    _L0_attn_in = {k: v for k, v in _L0_attn_all.items() if k in ('Wq', 'Wkv', 'Wout', 'bout', 'Wg', 'bg', 'lq1', 'lk1', 'lq2', 'lk2', 'ln_gamma', 'ln_beta')}
    del _L0_attn_all

    def _L0_ffn_setup():
        import jax, jax.numpy as jnp
        import numpy as np
        B, S, D = (8, 1024, 64)
        H = 4 * D
        CAPACITY = 0.5
        key = jax.random.key(seed)
        ks = jax.random.split(key, 6)
        x = jax.random.normal(ks[0], (B, S, D), dtype=jnp.float32)
        attention_mask = jnp.zeros((B, 1, 1, S), dtype=jnp.float32)
        wr = jax.random.normal(ks[1], (D, 1), dtype=jnp.float32) * 0.02
        br = jnp.zeros((1,), dtype=jnp.float32)
        w1 = jax.random.normal(ks[2], (D, H), dtype=jnp.float32) * 0.02
        b1 = jnp.zeros((H,), dtype=jnp.float32)
        w2 = jax.random.normal(ks[3], (H, D), dtype=jnp.float32) * 0.02
        b2 = jnp.zeros((D,), dtype=jnp.float32)
        return {'x': x, 'attention_mask': attention_mask, 'wr': wr, 'br': br, 'w1': w1, 'b1': b1, 'w2': w2, 'b2': b2}
    _L0_ffn_all = _L0_ffn_setup()
    _L0_ffn_in = {k: v for k, v in _L0_ffn_all.items() if k in ('attention_mask', 'wr', 'br', 'w1', 'b1', 'w2', 'b2')}
    del _L0_ffn_all

    def _L1_attn_setup():
        import jax, jax.numpy as jnp
        import numpy as np
        HEAD_SIZE = 64
        HEAD_SIZE_R = HEAD_SIZE // 4
        HEAD_SIZE_C = HEAD_SIZE - HEAD_SIZE_R
        N_EMBD = 64

        def rope(x, start_pos=0):
            B, T, d = x.shape
            half = d // 2
            theta = 1.0 / 10000.0 ** (jnp.arange(half, dtype=x.dtype) / half)
            idx = jnp.arange(start_pos, start_pos + T, dtype=x.dtype)[:, None] * theta[None, :]
            sin, cos = (jnp.sin(idx), jnp.cos(idx))
            xs = x.reshape(B, T, half, 2)
            x1, x2 = (xs[..., 0], xs[..., 1])
            rot = jnp.stack([x1 * cos - x2 * sin, x1 * sin + x2 * cos], axis=-1)
            return rot.reshape(B, T, d)

        def _reference_tuple_inner(x, Wq_comp, Wkv_comp, Wqc, Wqr, Wkc, Wkr, Wv):
            c_q = x @ Wq_comp
            c_kv = x @ Wkv_comp
            q_c = c_q @ Wqc
            q_r = rope(c_q @ Wqr, start_pos=0)
            q = jnp.concatenate([q_c, q_r], axis=-1)
            k_c = c_kv @ Wkc
            k_r = rope(c_kv @ Wkr, start_pos=0)
            k = jnp.concatenate([k_c, k_r], axis=-1)
            v = c_kv @ Wv
            scale = 1.0 / jnp.sqrt(jnp.asarray(HEAD_SIZE, dtype=x.dtype))
            wei = jnp.einsum('bqd,bkd->bqk', q, k) * scale
            T_q = q.shape[1]
            mask = jnp.tril(jnp.ones((T_q, T_q), dtype=bool))
            wei = jnp.where(mask, wei, jnp.asarray(-jnp.inf, dtype=wei.dtype))
            wei = jax.nn.softmax(wei, axis=-1)
            out = jnp.einsum('bqk,bkd->bqd', wei, v)
            return (out, (k, v))
        key = jax.random.key(seed)
        ks = jax.random.split(key, 8)
        B, T = (32, 512)
        s = 0.05
        return {'x': jax.random.normal(ks[0], (B, T, N_EMBD), dtype=jnp.float32), 'Wq_comp': jax.random.normal(ks[1], (N_EMBD, N_EMBD), dtype=jnp.float32) * s, 'Wkv_comp': jax.random.normal(ks[2], (N_EMBD, N_EMBD), dtype=jnp.float32) * s, 'Wqc': jax.random.normal(ks[3], (N_EMBD, HEAD_SIZE_C), dtype=jnp.float32) * s, 'Wqr': jax.random.normal(ks[4], (N_EMBD, HEAD_SIZE_R), dtype=jnp.float32) * s, 'Wkc': jax.random.normal(ks[5], (N_EMBD, HEAD_SIZE_C), dtype=jnp.float32) * s, 'Wkr': jax.random.normal(ks[6], (N_EMBD, HEAD_SIZE_R), dtype=jnp.float32) * s, 'Wv': jax.random.normal(ks[7], (N_EMBD, HEAD_SIZE), dtype=jnp.float32) * s}
    _L1_attn_all = _L1_attn_setup()
    _L1_attn_in = {k: v for k, v in _L1_attn_all.items() if k in ('Wq_comp', 'Wkv_comp', 'Wqc', 'Wqr', 'Wkc', 'Wkr', 'Wv')}
    del _L1_attn_all

    def _L1_ffn_setup():
        import jax, jax.numpy as jnp
        import numpy as np
        B, H, E, IN, OUT = (1024, 1, 8, 64, 64)

        @jax.custom_vjp
        def bin_active(x):
            return jnp.sign(x)

        def _ba_fwd(x):
            return (jnp.sign(x), x)

        def _ba_bwd(x, g):
            return (g * (jnp.abs(x) <= 1.0).astype(g.dtype),)
        bin_active.defvjp(_ba_fwd, _ba_bwd)

        @jax.custom_vjp
        def bin_gate(x):
            return (x > 0.5).astype(x.dtype)

        def _bg_fwd(x):
            return ((x > 0.5).astype(x.dtype), None)

        def _bg_bwd(_, g):
            return (g,)
        bin_gate.defvjp(_bg_fwd, _bg_bwd)
        key = jax.random.key(seed)
        k1, k2, k3, k4, k5 = jax.random.split(key, 5)
        x = jax.random.normal(k1, (B, H, IN), dtype=jnp.float32)
        weight = jax.random.normal(k2, (H, E, IN, OUT), dtype=jnp.float32) * 0.05
        proj_w = jax.random.normal(k3, (E, IN), dtype=jnp.float32) * 0.05
        proj_b = jax.random.normal(k4, (E,), dtype=jnp.float32) * 0.05
        scale = jax.random.normal(k5, (H, 1, OUT), dtype=jnp.float32) * 0.1
        return {'x': x, 'weight': weight, 'proj_w': proj_w, 'proj_b': proj_b, 'scale': scale}
    _L1_ffn_all = _L1_ffn_setup()
    _L1_ffn_in = {k: v for k, v in _L1_ffn_all.items() if k in ('weight', 'proj_w', 'proj_b', 'scale')}
    del _L1_ffn_all

    def _L2_attn_setup():
        import jax, jax.numpy as jnp
        import numpy as np
        B, N, C, H = (1024, 64, 64, 8)
        key = jax.random.key(seed)
        ks = jax.random.split(key, 6)
        return {'x': jax.random.normal(ks[0], (B, N, C), dtype=jnp.float32), 'qkv_w': jax.random.normal(ks[1], (C, 3 * C), dtype=jnp.float32) * 0.02, 'qkv_b': jax.random.normal(ks[2], (3 * C,), dtype=jnp.float32) * 0.02, 'proj_w': jax.random.normal(ks[3], (C, C), dtype=jnp.float32) * 0.02, 'proj_b': jax.random.normal(ks[4], (C,), dtype=jnp.float32) * 0.02, 'rpb_table': jax.random.normal(ks[5], (2 * N - 1, H), dtype=jnp.float32) * 0.02}
    _L2_attn_all = _L2_attn_setup()
    _L2_attn_in = {k: v for k, v in _L2_attn_all.items() if k in ('qkv_w', 'qkv_b', 'proj_w', 'proj_b', 'rpb_table')}
    del _L2_attn_all

    def _L2_ffn_setup():
        import jax, jax.numpy as jnp
        import numpy as np
        TOP_K = 2
        key = jax.random.key(seed)
        ks = jax.random.split(key, 4)
        B, L, D, H, E = (8, 1024, 64, 256, 8)
        s = 0.02
        return {'x': jax.random.normal(ks[0], (B, L, D), jnp.float32), 'Wg': jax.random.normal(ks[1], (D, E), jnp.float32) * s, 'bg': jnp.zeros((E,), jnp.float32), 'W1': jax.random.normal(ks[2], (E, D, H), jnp.float32) * s, 'b1': jnp.zeros((E, H), jnp.float32), 'W2': jax.random.normal(ks[3], (E, H, D), jnp.float32) * s, 'b2': jnp.zeros((E, D), jnp.float32)}
    _L2_ffn_all = _L2_ffn_setup()
    _L2_ffn_in = {k: v for k, v in _L2_ffn_all.items() if k in ('Wg', 'bg', 'W1', 'b1', 'W2', 'b2')}
    del _L2_ffn_all

    def _L3_attn_setup():
        import jax, jax.numpy as jnp
        import numpy as np
        import math
        B, N, D = (4, 1024, 64)
        key = jax.random.key(seed)
        k0, k1, k2, k3 = jax.random.split(key, 4)
        bound = math.sqrt(6.0 / D)
        return {'x': jax.random.normal(k0, (B, N, D), dtype=jnp.float32), 'Wq': jax.random.uniform(k1, (D, D), dtype=jnp.float32, minval=-bound, maxval=bound), 'Wk': jax.random.uniform(k2, (D, D), dtype=jnp.float32, minval=-bound, maxval=bound), 'Wv': jax.random.uniform(k3, (D, D), dtype=jnp.float32, minval=-bound, maxval=bound)}
    _L3_attn_all = _L3_attn_setup()
    _L3_attn_in = {k: v for k, v in _L3_attn_all.items() if k in ('Wq', 'Wk', 'Wv')}
    del _L3_attn_all

    def _L3_ffn_setup():
        import jax, jax.numpy as jnp
        import numpy as np
        B, T, C = (64, 96, 64)
        NH, NKV = (4, 2)
        HD = C // NH
        NREP = NH // NKV
        NE, TOPK = (8, 2)
        HID = int(8 / 3 * C)
        EPS_RMS = 1e-06

        def _rope_tables(t_len):
            inv_freq = 1.0 / 10000.0 ** (np.arange(0, HD, 2, dtype=np.float32) / HD)
            t = np.arange(t_len, dtype=np.float32)
            freqs = np.outer(t, inv_freq)
            emb = np.concatenate([freqs, freqs], axis=-1)
            return (jnp.asarray(np.cos(emb)), jnp.asarray(np.sin(emb)))

        def _rotate_half(x):
            h = x.shape[-1] // 2
            return jnp.concatenate([-x[..., h:], x[..., :h]], axis=-1)

        def _rmsnorm(v, w):
            return v * jax.lax.rsqrt(jnp.mean(v * v, axis=-1, keepdims=True) + EPS_RMS) * w
        key = jax.random.key(seed)
        ks = jax.random.split(key, 10)
        s = lambda k, shape: jax.random.normal(k, shape, jnp.float32) * 0.02
        return {'x': jax.random.normal(ks[0], (B, T, C), jnp.float32), 'ln1_w': jnp.ones((C,), jnp.float32), 'ln2_w': jnp.ones((C,), jnp.float32), 'wq': s(ks[1], (NH * HD, C)), 'wk': s(ks[2], (NKV * HD, C)), 'wv': s(ks[3], (NKV * HD, C)), 'wo': s(ks[4], (C, C)), 'router_w': s(ks[5], (NE, C)), 'w1': s(ks[6], (NE, HID, C)), 'w2': s(ks[7], (NE, C, HID)), 'w3': s(ks[8], (NE, HID, C))}
    _L3_ffn_all = _L3_ffn_setup()
    _L3_ffn_in = {k: v for k, v in _L3_ffn_all.items() if k in ('ln1_w', 'ln2_w', 'wq', 'wk', 'wv', 'wo', 'router_w', 'w1', 'w2', 'w3')}
    del _L3_ffn_all
    return {'x': x, 'cls_tok': cls_tok, 'L0_tok_d_gamma_batched': _L0_tok_in['d_gamma_batched'], 'L0_tok_Wq': _L0_tok_in['Wq'], 'L0_tok_bq': _L0_tok_in['bq'], 'L0_tok_Wk': _L0_tok_in['Wk'], 'L0_tok_bk': _L0_tok_in['bk'], 'L0_tok_Wv': _L0_tok_in['Wv'], 'L0_tok_bv': _L0_tok_in['bv'], 'L0_tok_Wo': _L0_tok_in['Wo'], 'L0_tok_bo': _L0_tok_in['bo'], 'L0_tok_prelu_a': _L0_tok_in['prelu_a'], 'L0_attn_Wq': _L0_attn_in['Wq'], 'L0_attn_Wkv': _L0_attn_in['Wkv'], 'L0_attn_Wout': _L0_attn_in['Wout'], 'L0_attn_bout': _L0_attn_in['bout'], 'L0_attn_Wg': _L0_attn_in['Wg'], 'L0_attn_bg': _L0_attn_in['bg'], 'L0_attn_lq1': _L0_attn_in['lq1'], 'L0_attn_lk1': _L0_attn_in['lk1'], 'L0_attn_lq2': _L0_attn_in['lq2'], 'L0_attn_lk2': _L0_attn_in['lk2'], 'L0_attn_ln_gamma': _L0_attn_in['ln_gamma'], 'L0_attn_ln_beta': _L0_attn_in['ln_beta'], 'L0_ffn_attention_mask': _L0_ffn_in['attention_mask'], 'L0_ffn_wr': _L0_ffn_in['wr'], 'L0_ffn_br': _L0_ffn_in['br'], 'L0_ffn_w1': _L0_ffn_in['w1'], 'L0_ffn_b1': _L0_ffn_in['b1'], 'L0_ffn_w2': _L0_ffn_in['w2'], 'L0_ffn_b2': _L0_ffn_in['b2'], 'L1_attn_Wq_comp': _L1_attn_in['Wq_comp'], 'L1_attn_Wkv_comp': _L1_attn_in['Wkv_comp'], 'L1_attn_Wqc': _L1_attn_in['Wqc'], 'L1_attn_Wqr': _L1_attn_in['Wqr'], 'L1_attn_Wkc': _L1_attn_in['Wkc'], 'L1_attn_Wkr': _L1_attn_in['Wkr'], 'L1_attn_Wv': _L1_attn_in['Wv'], 'L1_ffn_weight': _L1_ffn_in['weight'], 'L1_ffn_proj_w': _L1_ffn_in['proj_w'], 'L1_ffn_proj_b': _L1_ffn_in['proj_b'], 'L1_ffn_scale': _L1_ffn_in['scale'], 'L2_attn_qkv_w': _L2_attn_in['qkv_w'], 'L2_attn_qkv_b': _L2_attn_in['qkv_b'], 'L2_attn_proj_w': _L2_attn_in['proj_w'], 'L2_attn_proj_b': _L2_attn_in['proj_b'], 'L2_attn_rpb_table': _L2_attn_in['rpb_table'], 'L2_ffn_Wg': _L2_ffn_in['Wg'], 'L2_ffn_bg': _L2_ffn_in['bg'], 'L2_ffn_W1': _L2_ffn_in['W1'], 'L2_ffn_b1': _L2_ffn_in['b1'], 'L2_ffn_W2': _L2_ffn_in['W2'], 'L2_ffn_b2': _L2_ffn_in['b2'], 'L3_attn_Wq': _L3_attn_in['Wq'], 'L3_attn_Wk': _L3_attn_in['Wk'], 'L3_attn_Wv': _L3_attn_in['Wv'], 'L3_ffn_ln1_w': _L3_ffn_in['ln1_w'], 'L3_ffn_ln2_w': _L3_ffn_in['ln2_w'], 'L3_ffn_wq': _L3_ffn_in['wq'], 'L3_ffn_wk': _L3_ffn_in['wk'], 'L3_ffn_wv': _L3_ffn_in['wv'], 'L3_ffn_wo': _L3_ffn_in['wo'], 'L3_ffn_router_w': _L3_ffn_in['router_w'], 'L3_ffn_w1': _L3_ffn_in['w1'], 'L3_ffn_w2': _L3_ffn_in['w2'], 'L3_ffn_w3': _L3_ffn_in['w3']}

def reference(x, cls_tok, L0_tok_d_gamma_batched, L0_tok_Wq, L0_tok_bq, L0_tok_Wk, L0_tok_bk, L0_tok_Wv, L0_tok_bv, L0_tok_Wo, L0_tok_bo, L0_tok_prelu_a, L0_attn_Wq, L0_attn_Wkv, L0_attn_Wout, L0_attn_bout, L0_attn_Wg, L0_attn_bg, L0_attn_lq1, L0_attn_lk1, L0_attn_lq2, L0_attn_lk2, L0_attn_ln_gamma, L0_attn_ln_beta, L0_ffn_attention_mask, L0_ffn_wr, L0_ffn_br, L0_ffn_w1, L0_ffn_b1, L0_ffn_w2, L0_ffn_b2, L1_attn_Wq_comp, L1_attn_Wkv_comp, L1_attn_Wqc, L1_attn_Wqr, L1_attn_Wkc, L1_attn_Wkr, L1_attn_Wv, L1_ffn_weight, L1_ffn_proj_w, L1_ffn_proj_b, L1_ffn_scale, L2_attn_qkv_w, L2_attn_qkv_b, L2_attn_proj_w, L2_attn_proj_b, L2_attn_rpb_table, L2_ffn_Wg, L2_ffn_bg, L2_ffn_W1, L2_ffn_b1, L2_ffn_W2, L2_ffn_b2, L3_attn_Wq, L3_attn_Wk, L3_attn_Wv, L3_ffn_ln1_w, L3_ffn_ln2_w, L3_ffn_wq, L3_ffn_wk, L3_ffn_wv, L3_ffn_wo, L3_ffn_router_w, L3_ffn_w1, L3_ffn_w2, L3_ffn_w3):
    import jax
    import jax.numpy as jnp

    def _L0_tok_ref(x_batched, d_gamma_batched, Wq, bq, Wk, bk, Wv, bv, Wo, bo, prelu_a):
        import jax, jax.numpy as jnp
        import numpy as np
        T, D_IN, D_INT, D_OUT, B = (1024, 64, 64, 64, 8)
        x = x_batched.reshape(x_batched.shape[0], T, D_IN)
        q = x @ Wq + bq
        k = x @ Wk + bk
        v = x @ Wv + bv
        scores = jnp.einsum('btd,bsd->bts', q, k)
        retained = jnp.einsum('bts,bsd->btd', d_gamma_batched * scores, v)
        y = retained @ Wo + bo
        out = jnp.where(y >= 0, y, prelu_a * y)
        return out

    def _L0_attn_ref(x, Wq, Wkv, Wout, bout, Wg, bg, lq1, lk1, lq2, lk2, ln_gamma, ln_beta):
        import jax, jax.numpy as jnp
        import numpy as np
        import math
        H = 8
        DH = 16
        DEPTH = 1
        LAMBDA_INIT = 0.8 - 0.6 * math.exp(-0.3 * DEPTH)
        LN_EPS = 1e-05
        b, n, dim = x.shape
        scale = DH ** (-0.5)
        q = x @ Wq
        kv = x @ Wkv
        k, v = jnp.split(kv, 2, axis=-1)
        q = q.reshape(b, n, 2 * H, DH).transpose(0, 2, 1, 3) * scale
        k = k.reshape(b, n, 2 * H, DH).transpose(0, 2, 1, 3)
        v = v.reshape(b, n, H, 2 * DH).transpose(0, 2, 1, 3)
        dots = jnp.einsum('bhid,bhjd->bhij', q, k)
        attn = jax.nn.softmax(dots, axis=-1)
        lam1 = jnp.exp(jnp.sum(lq1 * lk1))
        lam2 = jnp.exp(jnp.sum(lq2 * lk2))
        lam = lam1 - lam2 + LAMBDA_INIT
        attn = attn.reshape(b, H, 2, n, n)
        attn = attn[:, :, 0] - lam * attn[:, :, 1]
        out = jnp.einsum('bhij,bhjd->bhid', attn, v)
        mu = jnp.mean(out, axis=-1, keepdims=True)
        var = jnp.var(out, axis=-1, keepdims=True)
        out = (out - mu) * jax.lax.rsqrt(var + LN_EPS) * ln_gamma + ln_beta
        out = out * (1.0 - LAMBDA_INIT)
        out = out.transpose(0, 2, 1, 3).reshape(b, n, H * 2 * DH)
        gates = x @ Wg + bg
        out = out * jax.nn.sigmoid(gates)
        return out @ Wout + bout

    def _L0_ffn_ref(x, attention_mask, wr, br, w1, b1, w2, b2):
        import jax, jax.numpy as jnp
        import numpy as np
        B, S, D = (8, 1024, 64)
        H = 4 * D
        CAPACITY = 0.5
        b, s, d = x.shape
        weights = (jnp.einsum('bsd,do->bso', x, wr) + br)[..., 0]
        k = max(1, int(CAPACITY * s))
        kk = k - 1 if k > 1 else 1
        _, idx = jax.lax.top_k(weights, k)
        sel_idx = idx[:, :kk]
        sel = jnp.take_along_axis(x, sel_idx[:, :, None], axis=1)
        h = jax.nn.gelu(jnp.einsum('bkd,dh->bkh', sel, w1) + b1)
        y = jnp.einsum('bkh,hd->bkd', h, w2) + b2
        w_sel = jnp.take_along_axis(weights, sel_idx, axis=1)
        y = y * w_sel[..., None]
        batch_idx = jnp.arange(b)[:, None]
        processed = jnp.zeros_like(x).at[batch_idx, sel_idx].set(y)
        return processed + x

    def _L1_attn_ref(x, Wq_comp, Wkv_comp, Wqc, Wqr, Wkc, Wkr, Wv):
        import jax, jax.numpy as jnp
        import numpy as np
        HEAD_SIZE = 64
        HEAD_SIZE_R = HEAD_SIZE // 4
        HEAD_SIZE_C = HEAD_SIZE - HEAD_SIZE_R
        N_EMBD = 64

        def rope(x, start_pos=0):
            B, T, d = x.shape
            half = d // 2
            theta = 1.0 / 10000.0 ** (jnp.arange(half, dtype=x.dtype) / half)
            idx = jnp.arange(start_pos, start_pos + T, dtype=x.dtype)[:, None] * theta[None, :]
            sin, cos = (jnp.sin(idx), jnp.cos(idx))
            xs = x.reshape(B, T, half, 2)
            x1, x2 = (xs[..., 0], xs[..., 1])
            rot = jnp.stack([x1 * cos - x2 * sin, x1 * sin + x2 * cos], axis=-1)
            return rot.reshape(B, T, d)

        def _reference_tuple_inner(x, Wq_comp, Wkv_comp, Wqc, Wqr, Wkc, Wkr, Wv):
            c_q = x @ Wq_comp
            c_kv = x @ Wkv_comp
            q_c = c_q @ Wqc
            q_r = rope(c_q @ Wqr, start_pos=0)
            q = jnp.concatenate([q_c, q_r], axis=-1)
            k_c = c_kv @ Wkc
            k_r = rope(c_kv @ Wkr, start_pos=0)
            k = jnp.concatenate([k_c, k_r], axis=-1)
            v = c_kv @ Wv
            scale = 1.0 / jnp.sqrt(jnp.asarray(HEAD_SIZE, dtype=x.dtype))
            wei = jnp.einsum('bqd,bkd->bqk', q, k) * scale
            T_q = q.shape[1]
            mask = jnp.tril(jnp.ones((T_q, T_q), dtype=bool))
            wei = jnp.where(mask, wei, jnp.asarray(-jnp.inf, dtype=wei.dtype))
            wei = jax.nn.softmax(wei, axis=-1)
            out = jnp.einsum('bqk,bkd->bqd', wei, v)
            return (out, (k, v))
        return _reference_tuple_inner(x, Wq_comp, Wkv_comp, Wqc, Wqr, Wkc, Wkr, Wv)[0]

    def _L1_ffn_ref(x, weight, proj_w, proj_b, scale):
        import jax, jax.numpy as jnp
        import numpy as np
        B, H, E, IN, OUT = (1024, 1, 8, 64, 64)

        @jax.custom_vjp
        def bin_active(x):
            return jnp.sign(x)

        def _ba_fwd(x):
            return (jnp.sign(x), x)

        def _ba_bwd(x, g):
            return (g * (jnp.abs(x) <= 1.0).astype(g.dtype),)
        bin_active.defvjp(_ba_fwd, _ba_bwd)

        @jax.custom_vjp
        def bin_gate(x):
            return (x > 0.5).astype(x.dtype)

        def _bg_fwd(x):
            return ((x > 0.5).astype(x.dtype), None)

        def _bg_bwd(_, g):
            return (g,)
        bin_gate.defvjp(_bg_fwd, _bg_bwd)
        xh = jnp.transpose(x, (1, 0, 2))
        gate = jax.nn.sigmoid(jnp.einsum('hbi,ei->hbe', xh, proj_w) + proj_b)
        gate = bin_gate(gate)
        w = jnp.einsum('hbe,heio->hbio', gate, weight)
        xb = bin_active(xh)
        wb = bin_active(w)
        y = jnp.einsum('hbi,hbio->hbo', xb, wb)
        y = y * scale
        return jnp.transpose(y, (1, 0, 2))

    def _L2_attn_ref(x, qkv_w, qkv_b, proj_w, proj_b, rpb_table):
        import jax, jax.numpy as jnp
        import numpy as np
        B, N, C, H = (1024, 64, 64, 8)
        Bw, Nw, Cd = x.shape
        nh = rpb_table.shape[1]
        dh = Cd // nh
        scale = dh ** (-0.5)
        qkv = (x @ qkv_w + qkv_b).reshape(Bw, Nw, 3, nh, dh)
        q, k, v = (qkv[:, :, 0], qkv[:, :, 1], qkv[:, :, 2])
        attn = jnp.einsum('bnhd,bmhd->bhnm', q * scale, k)
        coords = jnp.arange(Nw)
        rel_idx = coords[:, None] - coords[None, :] + (Nw - 1)
        bias = jnp.transpose(rpb_table[rel_idx], (2, 0, 1))
        attn = jax.nn.softmax(attn + bias[None], axis=-1)
        out = jnp.einsum('bhnm,bmhd->bnhd', attn, v).reshape(Bw, Nw, Cd)
        return out @ proj_w + proj_b

    def _L2_ffn_ref(x, Wg, bg, W1, b1, W2, b2):
        import jax, jax.numpy as jnp
        import numpy as np
        TOP_K = 2
        B, L, D = x.shape
        E = W1.shape[0]
        xf = x.reshape(-1, D)
        gate_logits = xf @ Wg + bg
        top_w, top_i = jax.lax.top_k(gate_logits, TOP_K)
        top_w = jax.nn.softmax(top_w, axis=-1)
        w_dense = jnp.sum(jax.nn.one_hot(top_i, E, dtype=xf.dtype) * top_w[..., None], axis=1)
        out = jnp.zeros_like(xf)
        for e in range(E):
            h = jax.nn.gelu(xf @ W1[e] + b1[e], approximate=False)
            out = out + w_dense[:, e:e + 1] * (h @ W2[e] + b2[e])
        return out.reshape(B, L, D)

    def _L3_attn_ref(x, Wq, Wk, Wv):
        import jax, jax.numpy as jnp
        import numpy as np
        import math
        B, N, D = (4, 1024, 64)
        q = x @ Wq.T
        k = x @ Wk.T
        v = x @ Wv.T
        n = x.shape[1]
        d_k = x.shape[2]
        mask = jnp.triu(jnp.ones((n, n), dtype=x.dtype), k=1)
        scale = jnp.asarray(1.0 / math.sqrt(d_k), dtype=x.dtype)
        s = (jnp.einsum('bnd,bmd->bnm', q, k) - (1.0 - mask) * 10000000000.0) * scale
        s = jax.nn.softmax(s, axis=1)
        return jnp.einsum('bnm,bmd->bnd', s, v)

    def _L3_ffn_ref(x, ln1_w, ln2_w, wq, wk, wv, wo, router_w, w1, w2, w3):
        import jax, jax.numpy as jnp
        import numpy as np
        B, T, C = (64, 96, 64)
        NH, NKV = (4, 2)
        HD = C // NH
        NREP = NH // NKV
        NE, TOPK = (8, 2)
        HID = int(8 / 3 * C)
        EPS_RMS = 1e-06

        def _rope_tables(t_len):
            inv_freq = 1.0 / 10000.0 ** (np.arange(0, HD, 2, dtype=np.float32) / HD)
            t = np.arange(t_len, dtype=np.float32)
            freqs = np.outer(t, inv_freq)
            emb = np.concatenate([freqs, freqs], axis=-1)
            return (jnp.asarray(np.cos(emb)), jnp.asarray(np.sin(emb)))

        def _rotate_half(x):
            h = x.shape[-1] // 2
            return jnp.concatenate([-x[..., h:], x[..., :h]], axis=-1)

        def _rmsnorm(v, w):
            return v * jax.lax.rsqrt(jnp.mean(v * v, axis=-1, keepdims=True) + EPS_RMS) * w
        Bx, Tx, Cx = x.shape
        h = _rmsnorm(x, ln1_w)
        q = (h @ wq.T).reshape(Bx, Tx, NH, HD).transpose(0, 2, 1, 3)
        k = (h @ wk.T).reshape(Bx, Tx, NKV, HD).transpose(0, 2, 1, 3)
        v = (h @ wv.T).reshape(Bx, Tx, NKV, HD).transpose(0, 2, 1, 3)
        cos, sin = _rope_tables(Tx)
        cos, sin = (cos[None, None], sin[None, None])
        q = q * cos + _rotate_half(q) * sin
        k = k * cos + _rotate_half(k) * sin
        k = jnp.repeat(k, NREP, axis=1)
        v = jnp.repeat(v, NREP, axis=1)
        scores = jnp.einsum('bhtd,bhsd->bhts', q, k) / jnp.sqrt(jnp.float32(HD))
        causal = jnp.tril(jnp.ones((Tx, Tx), dtype=bool))
        scores = jnp.where(causal[None, None], scores, jnp.float32(-1e+30))
        att = jax.nn.softmax(scores, axis=-1)
        y = jnp.einsum('bhts,bhsd->bhtd', att, v).transpose(0, 2, 1, 3).reshape(Bx, Tx, Cx)
        x = x + y @ wo.T
        flat = _rmsnorm(x, ln2_w).reshape(-1, Cx)
        probs = jax.nn.softmax(flat @ router_w.T, axis=-1)
        tp, ti = jax.lax.top_k(probs, TOPK)
        tp = tp / (jnp.sum(tp, axis=-1, keepdims=True) + 1e-09)
        weights = jnp.sum(tp[..., None] * jax.nn.one_hot(ti, NE, dtype=flat.dtype), axis=1)
        out = jnp.zeros_like(flat)
        for e in range(NE):
            hh = jax.nn.silu(flat @ w1[e].T) * (flat @ w3[e].T)
            out = out + weights[:, e:e + 1] * (hh @ w2[e].T)
        return x + out.reshape(Bx, Tx, Cx)
    h = _L0_tok_ref(x, L0_tok_d_gamma_batched, L0_tok_Wq, L0_tok_bq, L0_tok_Wk, L0_tok_bk, L0_tok_Wv, L0_tok_bv, L0_tok_Wo, L0_tok_bo, L0_tok_prelu_a)
    h = jnp.concatenate([jnp.broadcast_to(cls_tok, (h.shape[0], 1, h.shape[2])), h], axis=1)
    h = h + _L0_attn_ref(_layernorm(h, axis=-1), L0_attn_Wq, L0_attn_Wkv, L0_attn_Wout, L0_attn_bout, L0_attn_Wg, L0_attn_bg, L0_attn_lq1, L0_attn_lk1, L0_attn_lq2, L0_attn_lk2, L0_attn_ln_gamma, L0_attn_ln_beta)
    h = h + _L0_ffn_ref(_layernorm(h, axis=-1), L0_ffn_attention_mask, L0_ffn_wr, L0_ffn_br, L0_ffn_w1, L0_ffn_b1, L0_ffn_w2, L0_ffn_b2)
    h = h + _L1_attn_ref(_layernorm(h, axis=-1), L1_attn_Wq_comp, L1_attn_Wkv_comp, L1_attn_Wqc, L1_attn_Wqr, L1_attn_Wkc, L1_attn_Wkr, L1_attn_Wv)
    h = h + _L1_ffn_ref(_layernorm(h, axis=-1), L1_ffn_weight, L1_ffn_proj_w, L1_ffn_proj_b, L1_ffn_scale)
    h = h + _L2_attn_ref(_layernorm(h, axis=-1), L2_attn_qkv_w, L2_attn_qkv_b, L2_attn_proj_w, L2_attn_proj_b, L2_attn_rpb_table)
    h = h + _L2_ffn_ref(_layernorm(h, axis=-1), L2_ffn_Wg, L2_ffn_bg, L2_ffn_W1, L2_ffn_b1, L2_ffn_W2, L2_ffn_b2)
    h = h + _L3_attn_ref(_layernorm(h, axis=-1), L3_attn_Wq, L3_attn_Wk, L3_attn_Wv)
    h = h + _L3_ffn_ref(_layernorm(h, axis=-1), L3_ffn_ln1_w, L3_ffn_ln2_w, L3_ffn_wq, L3_ffn_wk, L3_ffn_wv, L3_ffn_wo, L3_ffn_router_w, L3_ffn_w1, L3_ffn_w2, L3_ffn_w3)
    return h

_drawn_inputs = setup_inputs


def setup_inputs(seed=0):
    import zlib

    import numpy as np

    out = dict(_drawn_inputs(seed))
    spreads = {'L0_attn_bout': (0.0, 0.8),
     'L0_attn_bg': (1.0, 0.6),
     'L0_attn_ln_gamma': (1.0, 0.6),
     'L0_attn_ln_beta': (0.0, 0.8),
     'L0_ffn_b1': (0.0, 0.8),
     'L0_ffn_b2': (0.0, 0.8),
     'L2_ffn_bg': (0.0, 0.8),
     'L2_ffn_b1': (0.0, 2.0),
     'L2_ffn_b2': (0.0, 2.0),
     'L3_ffn_ln1_w': (1.0, 0.6),
     'L3_ffn_ln2_w': (1.0, 0.6)}
    factors = {'cls_tok': 8.0,
     'L0_tok_bo': 8.0,
     'L0_attn_Wq': 4.893,
     'L0_attn_Wkv': 4.495,
     'L0_attn_Wout': 4.595,
     'L0_attn_Wg': 8.0,
     'L0_attn_lq1': 8.0,
     'L0_attn_lk1': 8.0,
     'L0_attn_lq2': 8.0,
     'L0_attn_lk2': 8.0,
     'L0_ffn_wr': 8.0,
     'L0_ffn_w1': 8.0,
     'L0_ffn_w2': 8.0,
     'L1_attn_Wq_comp': 8.0,
     'L1_attn_Wkv_comp': 8.0,
     'L1_attn_Wqc': 8.0,
     'L1_attn_Wqr': 8.0,
     'L1_attn_Wkc': 8.0,
     'L1_attn_Wkr': 8.0,
     'L1_attn_Wv': 8.0,
     'L1_ffn_weight': 3.42,
     'L1_ffn_proj_w': 4.339,
     'L1_ffn_proj_b': 7.977,
     'L1_ffn_scale': 3.285,
     'L2_attn_qkv_w': 27.49,
     'L2_attn_qkv_b': 64.0,
     'L2_attn_proj_w': 26.514,
     'L2_attn_proj_b': 64.0,
     'L2_attn_rpb_table': 200.0,
     'L2_ffn_Wg': 8.0,
     'L2_ffn_W1': 8.0,
     'L2_ffn_W2': 8.0,
     'L3_attn_Wq': 2.701,
     'L3_ffn_wq': 8.0,
     'L3_ffn_wk': 8.0,
     'L3_ffn_wv': 8.0,
     'L3_ffn_wo': 8.0,
     'L3_ffn_router_w': 8.0,
     'L3_ffn_w1': 8.0,
     'L3_ffn_w2': 8.0,
     'L3_ffn_w3': 8.0}
    for name, (base, spread) in spreads.items():
        noise = np.random.default_rng([zlib.crc32(name.encode()), seed]).standard_normal(out[name].shape)
        drawn = base * np.exp(spread * noise) if base else spread * noise
        out[name] = jnp.asarray(drawn.astype(out[name].dtype))
    for name, factor in factors.items():
        out[name] = (out[name] * factor).astype(out[name].dtype)
    return out
```

```python
import math
from contextlib import ExitStack, contextmanager

import concourse.bass as bass
from concourse import mybir

B, T0, D = 8, 1024, 64
T = T0 + 1
PT, NT = 114, 9
TP = PT * NT
NC, CW = 3, 342
TPB = 8
LAMBDA_INIT = 0.8 - 0.6 * math.exp(-0.3)
CAPACITY = T // 2 - 1
NEG = -1e30
RPB = 127
RPB0 = T - 1 - (RPB - 1)
SPLITS_Q = (0, 0, 0, 1, 1, 2)
SPLITS_K = (0, 1, 2, 0, 1, 0)
LAST = 9


def build(nc, A, scratch, out, stop_after=LAST):
    fp32, bf16 = mybir.dt.float32, mybir.dt.bfloat16
    ALU, ACT, AX = mybir.AluOpType, mybir.ActivationFunctionType, mybir.AxisListType
    stack = ExitStack()

    pool_sems = [stack.enter_context(nc.semaphore(f"step_{n}")) for n in range(8)]
    assert pool_sems[-1].num - pool_sems[0].num == 7

    def sb(name, shape, dt=fp32):
        return stack.enter_context(nc.sbuf_tensor(name, shape, dt))

    @contextmanager
    def step(*names):
        used = pool_sems[0:len(names)]
        with nc.Block() as block:
            yield (block, *used)
        nc.all_engine_barrier(sems_to_clear=range(used[0].num, used[-1].num + 1))

    def chain(eng, sem):
        count = [0]

        def link(ins):
            count[0] += 1
            ins.then_inc(sem, 1)
            eng.wait_ge(sem, count[0])
        return link

    with stack:
        PS = stack.enter_context(nc.psum_tensor("PS", [128, 8, 512], fp32))

        ident = sb("ident", [128, 128])
        ident_bf = sb("ident_bf", [128, 128], bf16)
        flip = sb("flip", [PT, PT])
        mask_q = sb("mask_q", [PT, CW], bf16)
        mask_k = sb("mask_k", [PT, PT], bf16)
        mask_cols = sb("mask_cols", [PT, TP])
        mask_diag = sb("mask_diag", [PT, CW])
        earlier = sb("earlier", [PT, 2 * TP], bf16)
        select_o = sb("select_o", [128, 128], bf16)
        minus_half = sb("minus_half", [PT, NT])
        ones_row = sb("ones_row", [1, PT])
        real_row = sb("real_row", [PT, 1])
        split1 = sb("split1", [24, 1])
        split2 = sb("split2", [24, 1])
        gammaT = sb("gammaT", [128, 8, T0])
        bias_q = sb("bias_q", [PT, 2, 8, RPB])
        bias_k = sb("bias_k", [PT, 2, 8, 128])
        wsign = sb("wsign", [24, 64 * 64], bf16)
        W = {}
        for name, cols in (("tWq", 64), ("tWk", 64), ("tWv", 64), ("tWo", 64), ("aWg", 256), ("wr", 1), ("rWg", 8),
                           ("qkv", 192), ("wproj", 64)):
            W[name] = sb("w_" + name, [65, cols])
        for name, cols in (("aWq", 256), ("aWk", 256), ("aWv", 256), ("cq", 64), ("ckv", 64), ("lq", 64), ("lqs", 64),
                           ("lk", 64), ("lks", 64), ("lv", 64), ("gWq", 64), ("gWk", 64), ("gWv", 64), ("fq", 64),
                           ("fqs", 64), ("fk", 32), ("fks", 32), ("fv", 32), ("fo", 64), ("router", 8)):
            W[name] = sb("w_" + name, [64, cols])
        gate_w = sb("gate_w", [65, 24])
        aWout = sb("aWout", [128, 2, 64])
        aBout = sb("aBout", [1, 64])
        lam_in = sb("lam_in", [PT, 4, 16])
        lam = sb("lam", [PT, 8])
        ln_g = sb("ln_g", [PT, 32])
        ln_b = sb("ln_b", [PT, 32])
        prelu = sb("prelu", [64, 1])
        bscale = sb("bscale", [64, 1])
        rms1 = sb("rms1", [64, 1])
        rms2 = sb("rms2", [64, 1])
        rope = sb("rope", [64, 4, TP])
        wr_b = sb("wr_b", [65, PT])
        h = sb("h", [PT, NT, D])
        xn = sb("xn", [PT, NT, D])
        sq = sb("sq", [PT, NT, D])
        stat = sb("stat", [PT, 4, 72])
        xT = sb("xT", [65, TP])
        FA = sb("FA", [128, 2, TP])
        FB = sb("FB", [128, 2, TP])
        parts = sb("parts", [128, 3, 2 * TP], bf16)
        qs = sb("qs", [128, 2, TP], bf16)
        ks = sb("ks", [128, 2, TP], bf16)
        q65 = sb("q65", [65, TP])
        k65 = sb("k65", [65, TP])
        vv = sb("vv", [PT, NT, 8 * 33])
        P = sb("P", [128, 2, TP])
        att = sb("att", [PT, NT, 256])
        gates = sb("gates", [PT, NT, 256])
        tmp = sb("tmp", [PT, NT, 256])
        negmax = sb("negmax", [PT, 16, NT])
        mparts = sb("mparts", [16, 3, TP], bf16)
        wd = sb("wd", [PT, 8, NT])
        w1 = sb("w1", [65, 2, 256])
        w2 = sb("w2", [128, 2, D])
        b2 = sb("b2", [1, D])
        lg = sb("lg", [PT, 5, NT, 8])
        cmp8 = tmp[:, :, 0:64].rearrange("p t (a b) -> p t a b", b=8)
        x_tok = FB[:, 0, 0:8 * D].rearrange("p (t d) -> p t d", d=D)
        mreg = P

        scr_qa, scr_ka, scr_qb, scr_kb, scr_qc, scr_kc, scr_m, scr_t = scratch

        def bcast(ap, n):
            return ap.unsqueeze(2).to_broadcast([ap.shape[0], ap.shape[1], n])

        loads = [(W["tWq"][0:64, :], A["L0_tok_Wq"]), (W["tWq"][64:65, :], A["L0_tok_bq"]),
                 (W["tWk"][0:64, :], A["L0_tok_Wk"]), (W["tWk"][64:65, :], A["L0_tok_bk"]),
                 (W["tWv"][0:64, :], A["L0_tok_Wv"]), (W["tWv"][64:65, :], A["L0_tok_bv"]),
                 (W["tWo"][0:64, :], A["L0_tok_Wo"]), (W["tWo"][64:65, :], A["L0_tok_bo"]),
                 (W["aWq"][:, :], A["L0_attn_Wq"]), (W["aWk"][:, :], A["L0_attn_Wkv"][:, 0:256]),
                 (W["aWv"][:, :], A["L0_attn_Wkv"][:, 256:512]),
                 (W["aWg"][0:64, :], A["L0_attn_Wg"]), (W["aWg"][64:65, :], A["L0_attn_bg"]),
                 (W["wr"][0:64, :], A["L0_ffn_wr"]), (W["wr"][64:65, :], A["L0_ffn_br"]),
                 (W["rWg"][0:64, :], A["L2_ffn_Wg"]), (W["rWg"][64:65, :], A["L2_ffn_bg"]),
                 (W["qkv"][0:64, :], A["L2_attn_qkv_w"]), (W["qkv"][64:65, :], A["L2_attn_qkv_b"]),
                 (W["wproj"][0:64, :], A["L2_attn_proj_w"]), (W["wproj"][64:65, :], A["L2_attn_proj_b"]),
                 (W["cq"][:, :], A["L1_attn_Wq_comp"]), (W["ckv"][:, :], A["L1_attn_Wkv_comp"]),
                 (W["lq"][:, 0:48], A["L1_attn_Wqc"]), (W["lq"][:, 48:64], A["L1_attn_Wqr"]),
                 (W["lqs"][:, 0:48], A["L1_attn_Wqc"]), (W["lqs"][:, 48:64], A["L1_attn_Wqr_swapped"]),
                 (W["lk"][:, 0:48], A["L1_attn_Wkc"]), (W["lk"][:, 48:64], A["L1_attn_Wkr"]),
                 (W["lks"][:, 0:48], A["L1_attn_Wkc"]), (W["lks"][:, 48:64], A["L1_attn_Wkr_swapped"]),
                 (W["lv"][:, :], A["L1_attn_Wv"]),
                 (W["gWq"][:, :], A["L3_attn_WqT"]), (W["gWk"][:, :], A["L3_attn_WkT"]), (W["gWv"][:, :], A["L3_attn_WvT"]),
                 (W["fq"][:, :], A["L3_ffn_wqT"]), (W["fqs"][:, :], A["L3_ffn_wqT_rotated"]),
                 (W["fk"][:, :], A["L3_ffn_wkT"]), (W["fks"][:, :], A["L3_ffn_wkT_rotated"]),
                 (W["fv"][:, :], A["L3_ffn_wvT"]), (W["fo"][:, :], A["L3_ffn_woT"]), (W["router"][:, :], A["L3_ffn_routerT"]),
                 (aWout[:, :, :], A["L0_attn_Wout"].rearrange("(g p) n -> p g n", p=128)), (aBout[:, :], A["L0_attn_bout"]),
                 (ln_g[:, :], A["L0_attn_ln_gamma"].to_broadcast([PT, 32])),
                 (ln_b[:, :], A["L0_attn_ln_beta"].to_broadcast([PT, 32])),
                 (prelu[:, :], A["L0_tok_prelu_a"].to_broadcast([64, 1])),
                 (bscale[:, :], A["L1_ffn_scale"]), (rms1[:, :], A["L3_ffn_ln1_w"]), (rms2[:, :], A["L3_ffn_ln2_w"]),
                 (rope[:, :, :], A["rope"])]
        loads += [(lam_in[:, n, :], A["L0_attn_" + v].to_broadcast([PT, 16])) for n, v in enumerate(("lq1", "lk1", "lq2", "lk2"))]
        for part in range(3):
            loads += [(gate_w[0:64, 8 * part:8 * part + 8], A["L1_ffn_proj_wT"]), (gate_w[64:65, 8 * part:8 * part + 8], A["L1_ffn_proj_b"])]

        with step("weights_loaded", "zeroed", "made") as (block, weights_loaded, zeroed, made):
            @block.sync
            def _(sp):
                for dst, src in loads:
                    sp.dma_start(dst, src).then_inc(weights_loaded, 16)
                sp.wait_ge(weights_loaded, 16 * len(loads))

            @block.gpsimd
            def _(pool):
                cleared = [(t, 0.0) for t in (ident, ident_bf, flip, mask_q, mask_k, mask_diag, mask_cols, select_o)]
                cleared += [(t, 1.0) for t in (earlier, real_row, split1, split2, ones_row)] + [(minus_half, -0.5)]
                clear = chain(pool, zeroed)
                for t, value in cleared:
                    clear(nc.gpsimd.memset(t[tuple(slice(None) for _ in t.shape)], value))
                clear(nc.gpsimd.memset(xT[64:65, :], 1.0))
                clear(nc.gpsimd.memset(k65[64:65, :], 1.0))
                link = chain(pool, made)

                def where(ap, compare, fill, base, pattern, channel):
                    link(nc.gpsimd.affine_select(out=ap, in_=ap, compare_op=compare, fill=fill, base=base,
                                                 pattern=pattern, channel_multiplier=channel))
                for m in (ident, ident_bf):
                    where(m[:, :], ALU.not_equal, 1.0, 0, [[-1, 128]], 1)
                where(flip[:, :], ALU.not_equal, 1.0, 1 - PT, [[1, PT]], 1)
                where(mask_q[:, :], ALU.is_ge, NEG, 0, [[-1, CW]], 1)
                where(mask_k[:, :], ALU.is_ge, NEG, 0, [[1, PT]], -1)
                where(mask_cols[:, :], ALU.is_gt, -1e10, 0, [[-1, TP]], 1)
                where(mask_cols[:, T:TP], ALU.is_gt, NEG, -1, [[-1, 1]], 0)
                where(mask_diag[:, :], ALU.is_gt, -1e10, 0, [[-1, CW]], 1)
                where(mask_diag[:, :], ALU.is_gt, NEG, PT, [[-1, CW]], 0)
                where(earlier[:, :], ALU.is_gt, 0.0, TP, [[-1, 2 * TP]], 1)
                where(real_row[:, :], ALU.is_gt, 0.0, PT - 1, [[0, 1]], -1)
                where(split1[:, :], ALU.is_ge, 0.0, -8, [[0, 1]], 1)
                where(split2[:, :], ALU.is_ge, 0.0, -16, [[0, 1]], 1)
                link(nc.gpsimd.memset(select_o[0:64, 62:63], 1.0))
                link(nc.gpsimd.memset(select_o[64:128, 63:64], 1.0))

        with step("made", "raised", "loaded", "stored") as (block, made, raised, loaded, stored):
            table = FA[0:8, 0, 0:384]
            flipped = FA[0:8, 1, 0:384]
            raw = FB[0:8, 0, 0:2 * RPB + 1]

            @block.sync
            def _(sp):
                sp.dma_start(raw[:, 0:RPB], A["rpbT"]).then_inc(loaded, 16)
                sp.dma_start(raw[:, RPB:2 * RPB], A["rpbT_flipped"]).then_inc(loaded, 16)
                sp.wait_ge(made, 11)
                sp.dma_start(scr_t[0], table).then_inc(stored, 16)
                sp.dma_start(scr_t[1], flipped).then_inc(stored, 16)
                sp.wait_ge(stored, 32)

            @block.vector
            def _(dve):
                link = chain(dve, made)
                link(nc.vector.tensor_tensor(lam_in[:, 0, :], lam_in[:, 0, :], lam_in[:, 1, :], ALU.mult))
                link(nc.vector.tensor_tensor(lam_in[:, 2, :], lam_in[:, 2, :], lam_in[:, 3, :], ALU.mult))
                link(nc.vector.reduce_sum(lam[:, 0:1], lam_in[:, 0, :], AX.X))
                link(nc.vector.reduce_sum(lam[:, 1:2], lam_in[:, 2, :], AX.X))
                link(nc.vector.memset(FA[0:8, :, 0:384], 0.0))
                dve.wait_ge(loaded, 32)
                link(nc.vector.tensor_scalar(table[:, 1:1 + RPB], raw[:, 0:RPB], raw[:, RPB - 1:RPB], None, ALU.subtract))
                link(nc.vector.tensor_scalar(flipped[:, 227:227 + RPB], raw[:, RPB:2 * RPB], raw[:, RPB - 1:RPB], None, ALU.subtract))
                link(nc.vector.tensor_scalar_mul(ln_g[:, :], ln_g[:, :], 1.0 - LAMBDA_INIT))
                link(nc.vector.tensor_scalar_mul(ln_b[:, :], ln_b[:, :], 1.0 - LAMBDA_INIT))
                link(nc.vector.memset(wr_b[:, :], 1.0))
                link(nc.vector.tensor_scalar_mul(wr_b[:, :], wr_b[:, :], W["wr"][:, :]))
                dve.wait_ge(raised, 1)
                link(nc.vector.tensor_tensor(lam[:, 4:5], lam[:, 3:4], lam[:, 2:3], ALU.subtract))
                link(nc.vector.tensor_scalar_add(lam[:, 5:6], lam[:, 4:5], -LAMBDA_INIT))

            @block.scalar
            def _(act):
                act.wait_ge(made, 4)
                nc.scalar.activation(lam[:, 2:4], lam[:, 0:2], ACT.Exp).then_inc(raised, 1)

        with step("loaded", "split") as (block, loaded, split):
            whole = FB[0:24, :, :].rearrange("p a n -> p (a n)")

            @block.sync
            def _(sp):
                for half in range(2):
                    for part in range(3):
                        sp.dma_start(P[8 * part:8 * part + 8, half, 0:1024], A["L1_ffn_weightT"][:, 2048 * half:2048 * half + 1024]).then_inc(loaded, 16)
                        sp.dma_start(FA[8 * part:8 * part + 8, half, 0:1024], A["L1_ffn_weightT"][:, 2048 * half + 1024:2048 * half + 2048]).then_inc(loaded, 16)
                for tile in range(2):
                    for head in range(8):
                        q0 = 227 - PT * tile
                        sp.dma_start(bias_q[:, tile, head, :], diagonal(scr_t, 1, head, q0, RPB)).then_inc(loaded, 16)
                        k0 = 1 + T - 1 - PT * (7 + tile)
                        sp.dma_start(bias_k[:, tile, head, :], diagonal(scr_t, 0, head, k0, 128)).then_inc(loaded, 16)
                sp.wait_ge(loaded, 16 * (12 + 32))

            @block.vector
            def _(dve):
                dve.wait_ge(loaded, 16 * (12 + 32))
                link = chain(dve, split)
                for q, buf in enumerate((P[0:24, 0, 0:1024], FA[0:24, 0, 0:1024], P[0:24, 1, 0:1024], FA[0:24, 1, 0:1024])):
                    dst = wsign[:, 1024 * q:1024 * q + 1024]
                    work = FB[0:24, 0, 0:1024]
                    for mask in (split1, split2):
                        link(nc.vector.tensor_copy(dst, buf))
                        link(nc.vector.tensor_scalar_mul(work, dst, mask[:, :]))
                        link(nc.vector.tensor_tensor(buf, buf, work, ALU.subtract))
                    link(nc.vector.tensor_copy(dst, buf))
                link(nc.vector.memset(bias_k[0:1, 1, :, :], 0.0))

        with step("loaded_even", "loaded_odd", "transposed", "copied") as (block, loaded_even, loaded_odd, transposed, copied):
            loaded = (loaded_even, loaded_odd)

            @block.sync
            def _(sp):
                for t in range(8):
                    if t >= 2:
                        sp.wait_ge(transposed, t - 1)
                    sp.dma_start(P[:, t % 2, 0:T0], A["L0_tok_d_gamma_batched"][128 * t:128 * t + 128, :]).then_inc(loaded[t % 2], 16)

            @block.tensor
            def _(pe):
                for t in range(8):
                    pe.wait_ge(loaded[t % 2], 16 * (t // 2 + 1))
                    if t >= 2:
                        pe.wait_ge(copied, t - 1)
                    for s in range(8):
                        last = nc.tensor.transpose(PS[:, 2 * (t % 2) + s // 4, 128 * (s % 4):128 * (s % 4) + 128],
                                                   P[:, t % 2, 128 * s:128 * s + 128], ident[:, :])
                    last.then_inc(transposed, 1)

            @block.scalar
            def _(act):
                for t in range(8):
                    act.wait_ge(transposed, t + 1)
                    nc.scalar.activation(gammaT[:, :, 128 * t:128 * t + 128].rearrange("p (a s) n -> p a s n", a=2),
                                         PS[:, 2 * (t % 2):2 * (t % 2) + 2, :].rearrange("p a (s n) -> p a s n", n=128),
                                         ACT.Copy).then_inc(copied, 1)

        def feature_products(groups, terms, consume, on="vector"):
            with step("product", "consumed") as (block, product, consumed):
                @block.tensor
                def _(pe):
                    for g in range(groups):
                        for c in range(NC):
                            pairs = terms(g, c)
                            for n, (lhsT, rhs) in enumerate(pairs):
                                last = nc.tensor.matmul(PS[0:lhsT.shape[-1], 3 * g + c, 0:CW], lhsT, rhs,
                                                        start=(n == 0), stop=(n == len(pairs) - 1))
                            last.then_inc(product, 1)

                def program(eng):
                    for g in range(groups):
                        for c in range(NC):
                            eng.wait_ge(product, 3 * g + c + 1)
                            consume(g, c, PS[:, 3 * g + c, 0:CW]).then_inc(consumed, 1)
                (block.vector if on == "vector" else block.scalar)(program)

        def token_products(width, terms, consume, on="vector"):
            per = min(512 // width, NT)
            banks = -(-NT // per)
            with step("product", "consumed") as (block, product, consumed):
                @block.tensor
                def _(pe):
                    for t in range(NT):
                        pairs = terms(t)
                        for n, (lhsT, rhs) in enumerate(pairs):
                            last = nc.tensor.matmul(PS[0:PT, t // per, width * (t % per):width * (t % per) + width], lhsT, rhs,
                                                    start=(n == 0), stop=(n == len(pairs) - 1))
                        if t % per == per - 1 or t == NT - 1:
                            last.then_inc(product, 1)

                def program(eng):
                    for b in range(banks):
                        t0, t1 = b * per, min(NT, b * per + per)
                        eng.wait_ge(product, b + 1)
                        consume(t0, t1, PS[0:PT, b, 0:width * (t1 - t0)].rearrange("p (t n) -> p t n", n=width)).then_inc(consumed, 1)
                (block.vector if on == "vector" else block.scalar)(program)

        def tile(ap, t):
            return ap[:, PT * t:PT * t + PT]

        def chunk(ap, c):
            return ap[:, CW * c:CW * c + CW]

        def normalise(src, dst, layer, eps):
            with step("linked", "variance", "rstd") as (block, linked, variance, rstd):
                @block.vector
                def _(dve):
                    link = chain(dve, linked)
                    base = src
                    if layer:
                        link(nc.vector.reduce_sum(stat[:, 0, 0:NT], src, AX.X))
                        link(nc.vector.tensor_scalar_mul(stat[:, 1, 0:NT], stat[:, 0, 0:NT], -1.0 / D))
                        link(nc.vector.tensor_tensor(dst, src, bcast(stat[:, 1, 0:NT], D), ALU.add))
                        base = dst
                    link(nc.vector.tensor_tensor(sq[:, :, :], base, base, ALU.mult))
                    link(nc.vector.reduce_sum(stat[:, 2, 0:NT], sq[:, :, :], AX.X))
                    nc.vector.tensor_scalar(stat[:, 3, 0:NT], stat[:, 2, 0:NT], 1.0 / D, eps, ALU.mult, ALU.add).then_inc(variance, 1)
                    dve.wait_ge(rstd, 1)
                    link(nc.vector.tensor_tensor(dst, base, bcast(stat[:, 0, 0:NT], D), ALU.mult))

                @block.gpsimd
                def _(pool):
                    pool.wait_ge(variance, 1)
                    nc.gpsimd.tensor_tensor(stat[:, 0, 0:NT], stat[:, 3, 0:NT], minus_half[:, :], ALU.pow).then_inc(rstd, 1)

        def to_features(src, rows, dst, pad=True, scale=None):
            with step("transposed", "copied") as (block, transposed, copied):
                @block.tensor
                def _(pe):
                    for g, s in enumerate(src):
                        for t in range(NT):
                            last = nc.tensor.transpose(PS[0:rows, 3 * g + t // 3, PT * (t % 3):PT * (t % 3) + PT], s[:, t, :],
                                                       ident[0:PT, 0:PT])
                            if t % 3 == 2:
                                last.then_inc(transposed, 1)

                @block.vector
                def _(dve):
                    for g, d in enumerate(dst):
                        for c in range(NC):
                            dve.wait_ge(transposed, 3 * g + c + 1)
                            if scale is None:
                                nc.vector.tensor_copy(chunk(d, c), PS[0:rows, 3 * g + c, 0:CW]).then_inc(copied, 1)
                            else:
                                nc.vector.tensor_scalar_mul(chunk(d, c), PS[0:rows, 3 * g + c, 0:CW], scale).then_inc(copied, 1)
                    if pad:
                        dve.wait_ge(copied, 3 * len(dst))
                        for d in dst:
                            nc.vector.tensor_copy(d[:, T:TP], d[:, 0:1]).then_inc(copied, 1)

        def add_to_h(t0, t1, tiles):
            return nc.vector.tensor_tensor(h[:, t0:t1, :], h[:, t0:t1, :], tiles, ALU.add)

        def copy_chunk(dst, rows):
            return lambda g, c, bank: nc.scalar.activation(chunk(dst[g], c), bank[0:rows, :], ACT.Copy)

        def store_stacked(x, rows, groups, scr, splits, scale=1.0):
            flat = x[0:rows, 0:groups, :].rearrange("p g n -> p (g n)")
            P1, P2, P3 = (parts[0:rows, s, 0:groups * TP] for s in range(3))
            with step("linked", "stored") as (block, linked, stored):
                @block.vector
                def _(dve):
                    link = chain(dve, linked)
                    if scale != 1.0:
                        link(nc.vector.tensor_scalar_mul(flat, flat, scale))
                    link(nc.vector.tensor_copy(P1, flat))
                    link(nc.vector.tensor_tensor(flat, flat, P1, ALU.subtract))
                    link(nc.vector.tensor_copy(P2, flat))
                    link(nc.vector.tensor_tensor(P3, flat, P2, ALU.subtract))

                @block.sync
                def _(sp):
                    count = 0
                    for slot, part in sorted(enumerate(splits), key=lambda sp_: sp_[1]):
                        sp.wait_ge(linked, (0, 1, 3, 4)[part + 1] + (scale != 1.0))
                        for g in range(groups):
                            sp.dma_start(scr.rearrange("h r s n -> (h r) s n")[rows * g:rows * g + rows, slot, :],
                                         parts[0:rows, part, TP * g:TP * g + TP]).then_inc(stored, 16)
                            count += 1
                    sp.wait_ge(stored, 16 * count)

        def maxima_pass(block, heads, K, causal, bias, ready, scores, taken):
            @block.tensor
            def _(pe):
                for u, (q, k, head) in enumerate(heads):
                    for n_in, sem in ready[u]:
                        pe.wait_ge(sem, n_in)
                    for t in range(NT):
                        n = NT * u + t
                        if n >= 2:
                            pe.wait_ge(taken, n - 1)
                        b0 = 3 * (n % 2)
                        nb = t // 3 + 1 if causal else NC
                        for c in range(nb):
                            masked = causal and c == nb - 1
                            biased = bias and t < 2 and c == 2
                            last = nc.tensor.matmul(PS[0:PT, b0 + c, 0:CW], tile(q[0:K], t), chunk(k[0:K], c),
                                                    start=True, stop=not (masked or biased))
                            if masked:
                                r = PT * (t % 3)
                                last = nc.tensor.matmul(PS[0:PT, b0 + c, r:CW], ident_bf[0:PT, 0:PT], mask_q[:, 0:CW - r],
                                                        start=False, stop=True)
                            if biased:
                                k0 = RPB0 - 2 * CW
                                last = nc.tensor.matmul(PS[0:PT, b0 + c, k0:k0 + RPB], flip[:, :],
                                                        bias_q[:, t, head, :], start=False, stop=True)
                        last.then_inc(scores, 1)

            @block.vector
            def _(dve):
                for u, (q, k, head) in enumerate(heads):
                    for t in range(NT):
                        n = NT * u + t
                        b0 = 3 * (n % 2)
                        nb = t // 3 + 1 if causal else NC
                        dve.wait_ge(scores, n + 1)
                        nc.vector.tensor_reduce(negmax[:, head, t:t + 1], PS[0:PT, b0:b0 + nb, 0:CW], AX.XY, ALU.max,
                                                negate=True).then_inc(taken, 1)

        def values_pass(block, heads, K, causal, bias, width, ready, scores, raised, summed, combine, exp_scale=1.0):
            spans = {}
            for j in range(NT):
                c0, r = (j // 3, PT * (j % 3)) if causal else (0, 0)
                spans[j] = (c0, r)

            @block.tensor
            def _(pe):
                def weigh(n):
                    u, j = divmod(n, NT)
                    pe.wait_ge(raised, n + 1)
                    for t in range(j if causal else 0, NT):
                        last = nc.tensor.matmul(PS[0:PT, 6 + u, width * t:width * t + width], tile(P[0:PT, n % 2], t), heads[u][3](j),
                                                start=(j == 0 and t == 0), stop=(j == (t if causal else NT - 1)), skip_group_check=True)
                    last.then_inc(summed, 1)
                for n in range(NT * len(heads)):
                    u, j = divmod(n, NT)
                    q, k, head = heads[u][0:3]
                    if j == 0:
                        for n_in, sem in ready[u]:
                            pe.wait_ge(sem, n_in)
                    if n >= 2:
                        pe.wait_ge(raised, n - 1)
                    b0 = 3 * (n % 2)
                    c0, r = spans[j]
                    for c in range(c0, NC):
                        first = r if c == c0 else 0
                        masked = causal and c == c0
                        biased = bias and j >= 7 and c == 0
                        last = nc.tensor.matmul(PS[0:PT, b0 + c, first:CW], tile(k[0:K], j), q[0:K][:, CW * c + first:CW * c + CW],
                                                start=True, stop=not (masked or biased))
                        if masked:
                            last = nc.tensor.matmul(PS[0:PT, b0 + c, first:first + PT], ident_bf[0:PT, 0:PT], mask_k[:, :],
                                                    start=False, stop=True)
                        if biased:
                            last = nc.tensor.matmul(PS[0:PT, b0, 0:128], flip[:, :], bias_k[:, j - 7, head, :],
                                                    start=False, stop=True)
                    last.then_inc(scores, 1)
                    if n:
                        weigh(n - 1)
                weigh(NT * len(heads) - 1)

            @block.scalar
            def _(act):
                for n in range(NT * len(heads)):
                    u, j = divmod(n, NT)
                    b0 = 3 * (n % 2)
                    c0, r = spans[j]
                    act.wait_ge(scores, n + 1)
                    if n >= 2:
                        act.wait_ge(summed, n - 1)
                    row = P[0:PT, n % 2, :]
                    if r:
                        last = nc.scalar.activation(row[:, CW * c0 + r:CW * c0 + CW], PS[0:PT, b0 + c0, r:CW], ACT.Exp)
                        c0 += 1
                    if c0 < NC:
                        last = nc.scalar.activation(row[:, CW * c0:TP].rearrange("p (c n) -> p c n", n=CW),
                                                    PS[0:PT, b0 + c0:b0 + NC, 0:CW], ACT.Exp)
                    last.then_inc(raised, 1)

            @block.vector
            def _(dve):
                for u in range(len(heads)):
                    dve.wait_ge(summed, NT * (u + 1))
                    combine(dve, u, PS[0:PT, 6 + u, 0:NT * width].rearrange("p (t n) -> p t n", n=width))

        def stacked_attention(nh, d, scr_q, scr_k, shared, width, v_of, causal, bias, combine):
            K = 6 * d
            with step("ones_written") as (block, ones_written):
                @block.gpsimd
                def _(pool):
                    base = K // 32 * 32
                    nc.gpsimd.memset(ks[base:base + 32, :, :], 1.0).then_inc(ones_written, 1)

            def load(sp, i, sems, with_max):
                for u in range(2):
                    head = i * 2 + u
                    sp.dma_start(qs[0:K, u, :], scr_q.rearrange("h r s n -> h (r s) n")[head]).then_inc(sems[u], 16)
                    sp.dma_start(ks[0:K, u, :], scr_k.rearrange("h r s n -> h (r s) n")[i if shared else head]).then_inc(sems[u], 16)
                    if with_max:
                        sp.dma_start(qs[K:K + 3, u, :], scr_m[head]).then_inc(sems[u], 16)

            def ops(i):
                return [(qs[:, u, :], ks[:, u, :], i * 2 + u) for u in range(2)]

            with nc.Fori(0, nh // 2) as i:
                with step("loaded_even", "loaded_odd", "scores", "taken") as (block, l0, l1, scores, taken):
                    @block.sync
                    def _(sp):
                        load(sp, i, (l0, l1), False)
                    maxima_pass(block, ops(i), K, causal, bias, [[(32, l0)], [(32, l1)]], scores, taken)

            with step("transposed", "linked", "stored") as (block, transposed, linked, stored):
                rows = PS[0:nh, 0:3, 0:CW]

                @block.tensor
                def _(pe):
                    for t in range(NT):
                        last = nc.tensor.transpose(PS[0:nh, t // 3, PT * (t % 3):PT * (t % 3) + PT], negmax[:, 0:nh, t], ident[0:PT, 0:PT])
                    last.then_inc(transposed, 1)

                @block.vector
                def _(dve):
                    link = chain(dve, linked)
                    p1, p2, p3 = (mparts[0:nh, s, :].rearrange("p (c n) -> p c n", n=CW) for s in range(3))
                    rest = mreg[0:nh, 0, :].rearrange("p (c n) -> p c n", n=CW)
                    dve.wait_ge(transposed, 1)
                    link(nc.vector.tensor_copy(p1, rows))
                    link(nc.vector.tensor_tensor(rest, rows, p1, ALU.subtract))
                    link(nc.vector.tensor_copy(p2, rest))
                    link(nc.vector.tensor_tensor(p3, rest, p2, ALU.subtract))

                @block.sync
                def _(sp):
                    sp.wait_ge(linked, 4)
                    sp.dma_start(scr_m[0:nh], mparts[0:nh, :, :]).then_inc(stored, 16)
                    sp.wait_ge(stored, 16)

            with nc.Fori(0, nh // 2) as i:
                with step("loaded_even", "loaded_odd", "scores", "raised", "summed", "linked") as (block, l0, l1, scores, raised, summed, linked):
                    @block.sync
                    def _(sp):
                        load(sp, i, (l0, l1), True)
                    heads = [(q, k, head, v_of(i, u)) for u, (q, k, head) in enumerate(ops(i))]
                    count = [0]

                    def divide(dve, u, O):
                        def link(ins):
                            count[0] += 1
                            ins.then_inc(linked, 1)
                            dve.wait_ge(linked, count[0])
                        combine(link, i, u, O)
                    values_pass(block, heads, K + 3, causal, bias, width, [[(48, l0)], [(48, l1)]], scores, raised, summed, divide)

        def mask_pad_values(ap):
            with step("masked") as (block, masked):
                @block.vector
                def _(dve):
                    nc.vector.tensor_scalar_mul(ap, ap, real_row[:, :]).then_inc(masked, 1)

        def set_ones(ap):
            with step("set") as (block, done):
                @block.gpsimd
                def _(pool):
                    nc.gpsimd.memset(ap, 1.0).then_inc(done, 1)

        def experts(count, hidden, func, w1_of, b1_of, w3_of, w2_of, b2_of):
            F = hidden // 2
            K = 65 if b1_of else 64
            n_loads = 2 + bool(b1_of) + bool(w3_of) + bool(b2_of)
            with nc.Fori(0, count) as e:
                with step("loaded", "hidden_ready", "activated", "gated", "output") as (block, loaded, hidden_ready, activated, gated, output):
                    @block.sync
                    def _(sp):
                        sp.dma_start(w1[0:64, 0, 0:hidden], w1_of(e)).then_inc(loaded, 16)
                        sp.dma_start(w2[0:F, :, :], w2_of(e)).then_inc(loaded, 16)
                        if b1_of:
                            sp.dma_start(w1[64:65, 0, 0:hidden], b1_of(e)).then_inc(loaded, 16)
                        if w3_of:
                            sp.dma_start(w1[0:64, 1, 0:hidden], w3_of(e)).then_inc(loaded, 16)
                        if b2_of:
                            sp.dma_start(b2[:, :], b2_of(e)).then_inc(loaded, 16)

                    @block.tensor
                    def _(pe):
                        pe.wait_ge(loaded, 16 * n_loads)
                        for j in range(2):
                            if w3_of and j:
                                pe.wait_ge(gated, 1)
                            b0 = 0 if w3_of else 3 * j
                            for c in range(NC):
                                last = nc.tensor.matmul(PS[0:F, b0 + c, 0:CW], w1[0:K, 0, F * j:F * j + F], chunk(xT[0:K], c), start=True, stop=True)
                                if w3_of:
                                    last = nc.tensor.matmul(PS[0:F, 3 + c, 0:CW], w1[0:64, 1, F * j:F * j + F], chunk(xT[0:64], c), start=True, stop=True)
                            last.then_inc(hidden_ready, 1)
                        pe.wait_ge(gated if w3_of else activated, 2)
                        for t in range(NT):
                            o = PS[0:PT, 6 + t // TPB, D * (t % TPB):D * (t % TPB) + D]
                            nc.tensor.matmul(o, tile(FA[0:F, 0], t), w2[0:F, 0, :], start=True, stop=False)
                            last = nc.tensor.matmul(o, tile(FA[0:F, 1], t), w2[0:F, 1, :], start=False, stop=not b2_of)
                            if b2_of:
                                last = nc.tensor.matmul(o, ones_row[:, :], b2[:, :], start=False, stop=True)
                        last.then_inc(output, 1)

                    @block.scalar
                    def _(act):
                        for j in range(2):
                            b0 = 0 if w3_of else 3 * j
                            act.wait_ge(hidden_ready, j + 1)
                            nc.scalar.activation(FA[0:F, j, :].rearrange("p (c n) -> p c n", n=CW), PS[0:F, b0:b0 + 3, 0:CW], func).then_inc(activated, 1)

                    @block.vector
                    def _(dve):
                        if w3_of:
                            for j in range(2):
                                dve.wait_ge(activated, j + 1)
                                row = FA[0:F, j, :].rearrange("p (c n) -> p c n", n=CW)
                                nc.vector.tensor_tensor(row, row, PS[0:F, 3:6, 0:CW], ALU.mult).then_inc(gated, 1)
                        dve.wait_ge(output, 1)
                        for t in range(NT):
                            nc.vector.scalar_tensor_tensor(h[:, t, :], PS[0:PT, 6 + t // TPB, D * (t % TPB):D * (t % TPB) + D],
                                                           wd[:, e, t:t + 1], h[:, t, :], ALU.mult, ALU.add).then_inc(gated, 1)

        def route_top2(weights, K, probabilities):
            logit, shifted, raised_, key, chosen = (lg[:, n, :, :] for n in range(5))
            token_products(8, lambda t: [(tile(xT[0:K], t), weights)],
                           lambda t0, t1, tiles: nc.vector.tensor_copy(logit[:, t0:t1, :], tiles))
            with step("linked", "shift_ready", "raised") as (block, linked, shift_ready, raised):
                @block.vector
                def _(dve):
                    link = chain(dve, linked)
                    link(nc.vector.reduce_max(stat[:, 0, 0:NT], logit, AX.X))
                    nc.vector.tensor_tensor(shifted, logit, bcast(stat[:, 0, 0:NT], 8), ALU.subtract).then_inc(shift_ready, 1)
                    dve.wait_ge(raised, 1)
                    score = logit
                    if probabilities:
                        link(nc.vector.reduce_sum(stat[:, 1, 0:NT], raised_, AX.X))
                        link(nc.vector.reciprocal(stat[:, 2, 0:NT], stat[:, 1, 0:NT]))
                        link(nc.vector.tensor_tensor(key, raised_, bcast(stat[:, 2, 0:NT], 8), ALU.mult))
                        score = key
                    value = score if probabilities else raised_
                    for e in range(8):
                        own = score[:, :, e:e + 1]
                        link(nc.vector.tensor_tensor(cmp8[:, :, 0:e + 1, e], own.to_broadcast([PT, NT, e + 1]), score[:, :, 0:e + 1], ALU.is_gt))
                        if e < 7:
                            link(nc.vector.tensor_tensor(cmp8[:, :, e + 1:8, e], own.to_broadcast([PT, NT, 7 - e]), score[:, :, e + 1:8], ALU.is_ge))
                    link(nc.vector.reduce_sum(chosen, cmp8[:, :, :, :], AX.X))
                    link(nc.vector.tensor_scalar(chosen, chosen, 2.0, None, ALU.is_lt))
                    link(nc.vector.tensor_tensor(chosen, chosen, value, ALU.mult))
                    link(nc.vector.reduce_sum(stat[:, 1, 0:NT], chosen, AX.X))
                    if probabilities:
                        link(nc.vector.tensor_scalar_add(stat[:, 1, 0:NT], stat[:, 1, 0:NT], 1e-9))
                    link(nc.vector.reciprocal(stat[:, 2, 0:NT], stat[:, 1, 0:NT]))
                    link(nc.vector.tensor_tensor(wd[:, :, :].rearrange("p e t -> p t e"), chosen, bcast(stat[:, 2, 0:NT], 8), ALU.mult))

                @block.scalar
                def _(act):
                    act.wait_ge(shift_ready, 1)
                    nc.scalar.activation(raised_, shifted, ACT.Exp).then_inc(raised, 1)

        def tokeniser(b):
            hT = FB[0:64, 1, :]
            q, k, ret = FA[0:64, 0, 0:T0], FA[0:64, 1, 0:T0], q65
            v = vv[:, :, 0:64]
            vt = x_tok
            with step("loaded", "transposed", "copied", "padded") as (block, loaded, transposed, copied, padded):
                @block.sync
                def _(sp):
                    sp.dma_start(x_tok[:, :, :], A["x"].rearrange("b o (t p) d -> b (o p) t d", p=128)[b]).then_inc(loaded, 16)
                    sp.dma_start(hT[:, 0:1], A["cls_tok"]).then_inc(loaded, 16)

                @block.tensor
                def _(pe):
                    pe.wait_ge(loaded, 32)
                    for t in range(8):
                        last = nc.tensor.transpose(PS[0:64, t // 4, 128 * (t % 4):128 * (t % 4) + 128], x_tok[:, t, :], ident[:, :])
                    last.then_inc(transposed, 1)

                @block.scalar
                def _(act):
                    act.wait_ge(transposed, 1)
                    nc.scalar.activation(xT[0:64, 0:T0].rearrange("p (a n) -> p a n", a=2), PS[0:64, 0:2, :], ACT.Copy).then_inc(copied, 1)

                @block.gpsimd
                def _(pool):
                    nc.gpsimd.memset(hT[:, T:TP], 0.0).then_inc(padded, 1)
                    pool.wait_ge(padded, 1)
                    nc.gpsimd.memset(q65[64:65, :], 1.0).then_inc(padded, 1)

            with step("product", "copied") as (block, product, copied):
                @block.tensor
                def _(pe):
                    for n, w in enumerate((W["tWq"], W["tWk"])):
                        for c in range(2):
                            nc.tensor.matmul(PS[0:64, 2 * n + c, :], w[:, :], xT[:, 512 * c:512 * c + 512], start=True, stop=True).then_inc(product, 1)
                    for t in range(8):
                        last = nc.tensor.matmul(PS[:, 4, D * t:D * t + D], xT[:, 128 * t:128 * t + 128], W["tWv"][:, :], start=True, stop=True)
                    last.then_inc(product, 1)

                @block.scalar
                def _(act):
                    for n, dst in enumerate((q, k)):
                        act.wait_ge(product, 2 * n + 2)
                        nc.scalar.activation(dst.rearrange("p (a n) -> p a n", a=2), PS[0:64, 2 * n:2 * n + 2, :], ACT.Copy).then_inc(copied, 1)

                @block.vector
                def _(dve):
                    dve.wait_ge(product, 5)
                    nc.vector.tensor_copy(vt[:, :, :], PS[:, 4, :].rearrange("p (t d) -> p t d", d=D)).then_inc(copied, 1)

            with step("scores", "decayed", "summed", "copied") as (block, scores, decayed, summed, copied):
                @block.tensor
                def _(pe):
                    def weigh(s):
                        pe.wait_ge(decayed, s + 1)
                        for c in range(2):
                            last = nc.tensor.matmul(PS[0:64, 6 + c, :], vt[:, s, :], P[:, s % 2, 512 * c:512 * c + 512], start=(s == 0), stop=(s == 7))
                        last.then_inc(summed, 1)
                    for s in range(8):
                        if s >= 2:
                            pe.wait_ge(decayed, s - 1)
                        for c in range(2):
                            last = nc.tensor.matmul(PS[:, 2 * (s % 2) + c, :], k[:, 128 * s:128 * s + 128], q[:, 512 * c:512 * c + 512], start=True, stop=True)
                        last.then_inc(scores, 1)
                        if s:
                            weigh(s - 1)
                    weigh(7)

                @block.vector
                def _(dve):
                    for s in range(8):
                        dve.wait_ge(scores, s + 1)
                        if s >= 2:
                            dve.wait_ge(summed, s - 1)
                        nc.vector.tensor_tensor(P[:, s % 2, 0:T0].rearrange("p (a n) -> p a n", a=2), gammaT[:, s, :].rearrange("p (a n) -> p a n", a=2),
                                                PS[:, 2 * (s % 2):2 * (s % 2) + 2, :], ALU.mult).then_inc(decayed, 1)

                @block.scalar
                def _(act):
                    act.wait_ge(summed, 8)
                    nc.scalar.activation(ret[0:64, 0:T0].rearrange("p (a n) -> p a n", a=2), PS[0:64, 6:8, :], ACT.Copy).then_inc(copied, 1)

            with step("product", "linked") as (block, product, linked):
                @block.tensor
                def _(pe):
                    for c in range(2):
                        last = nc.tensor.matmul(PS[0:64, c, :], W["tWo"][:, :], ret[:, 512 * c:512 * c + 512], start=True, stop=True)
                    last.then_inc(product, 1)

                @block.vector
                def _(dve):
                    link = chain(dve, linked)
                    y = PS[0:64, 0:2, :]
                    below = FA[0:64, 0, 0:T0].rearrange("p (a n) -> p a n", a=2)
                    dve.wait_ge(product, 1)
                    link(nc.vector.tensor_scalar(below, y, 0.0, prelu[:, :], ALU.min, ALU.mult))
                    link(nc.vector.scalar_tensor_tensor(hT[:, 1:T].rearrange("p (a n) -> p a n", a=2), y, 0.0, below, ALU.max, ALU.add))

            with step("transposed", "copied") as (block, transposed, copied):
                @block.tensor
                def _(pe):
                    for t in range(NT):
                        last = nc.tensor.transpose(PS[0:PT, t // TPB, D * (t % TPB):D * (t % TPB) + D], tile(hT, t), ident[0:64, 0:64])
                    last.then_inc(transposed, 1)

                @block.vector
                def _(dve):
                    dve.wait_ge(transposed, 1)
                    nc.vector.tensor_copy(h[:, 0:TPB, :], PS[0:PT, 0, :].rearrange("p (t d) -> p t d", d=D)).then_inc(copied, 1)
                    nc.vector.tensor_copy(h[:, TPB:NT, :], PS[0:PT, 1:2, 0:D]).then_inc(copied, 1)

        def normed(eps=1e-5):
            normalise(h[:, :, :], xn[:, :, :], True, eps)
            to_features([xn], 64, [xT[0:64, :]])

        def differential_attention():
            normed()
            x64 = xT[0:64]
            for w, dst in (("aWq", FA), ("aWk", FB)):
                feature_products(2, lambda g, c: [(W[w][:, 128 * g:128 * g + 128], chunk(x64, c))],
                                 copy_chunk([dst[:, 0, :], dst[:, 1, :]], 128), on="scalar")
            store_stacked(FA, 128, 2, scr_qa, SPLITS_Q, scale=0.25)
            store_stacked(FB, 128, 2, scr_ka, SPLITS_K)
            v = vv[:, :, :].rearrange("p t (h n) -> p t h n", n=33)
            set_ones(v[:, :, :, 32:33])
            token_products(256, lambda t: [(tile(x64, t), W["aWv"][:, :])],
                           lambda t0, t1, tiles: nc.scalar.activation(v[:, t0:t1, :, 0:32], tiles.rearrange("p t (h n) -> p t h n", n=32), ACT.Copy), on="scalar")
            mask_pad_values(vv[:, NT - 1, :])
            token_products(256, lambda t: [(tile(xT, t), W["aWg"][:, :])],
                           lambda t0, t1, tiles: nc.scalar.activation(gates[:, t0:t1, :], tiles, ACT.Sigmoid), on="scalar")

            def combine(link, i, u, O):
                rec, first = stat[:, u, 0:NT], tmp[:, :, 0:32]
                link(nc.vector.reciprocal(rec, O[:, :, 32]))
                if u == 0:
                    link(nc.vector.tensor_tensor(first, O[:, :, 0:32], bcast(rec, 32), ALU.mult))
                else:
                    link(nc.vector.tensor_scalar_mul(rec, rec, lam[:, 5:6]))
                    link(nc.vector.tensor_tensor(tmp[:, :, 32:64], O[:, :, 0:32], bcast(rec, 32), ALU.mult))
                    link(nc.vector.tensor_tensor(att[:, :, :].rearrange("p t (i n) -> p i t n", n=32)[:, i], first, tmp[:, :, 32:64], ALU.add))
            stacked_attention(16, 16, scr_qa, scr_ka, False, 33, lambda i, u: lambda j: vv[:, j, :].rearrange("p (h n) -> p h n", n=33)[:, i, :],
                              False, False, combine)

            with step("linked", "variance", "rstd") as (block, linked, variance, rstd):
                a3 = att[:, :, :].rearrange("p t (h n) -> p (t h) n", n=32)
                t3 = tmp[:, :, :].rearrange("p t (h n) -> p (t h) n", n=32)

                @block.vector
                def _(dve):
                    link = chain(dve, linked)
                    link(nc.vector.reduce_sum(stat[:, 0, :], a3, AX.X))
                    link(nc.vector.tensor_scalar_mul(stat[:, 1, :], stat[:, 0, :], -1.0 / 32))
                    link(nc.vector.tensor_tensor(a3, a3, bcast(stat[:, 1, :], 32), ALU.add))
                    link(nc.vector.tensor_tensor(t3, a3, a3, ALU.mult))
                    link(nc.vector.reduce_sum(stat[:, 2, :], t3, AX.X))
                    nc.vector.tensor_scalar(stat[:, 3, :], stat[:, 2, :], 1.0 / 32, 1e-5, ALU.mult, ALU.add).then_inc(variance, 1)
                    dve.wait_ge(rstd, 1)
                    link(nc.vector.tensor_tensor(a3, a3, bcast(stat[:, 0, :], 32), ALU.mult))
                    link(nc.vector.tensor_tensor(a3, a3, ln_g[:, :].unsqueeze(1).to_broadcast([PT, 72, 32]), ALU.mult))
                    link(nc.vector.tensor_tensor(a3, a3, ln_b[:, :].unsqueeze(1).to_broadcast([PT, 72, 32]), ALU.add))
                    link(nc.vector.tensor_tensor(att[:, :, :], att[:, :, :], gates[:, :, :], ALU.mult))

                @block.gpsimd
                def _(pool):
                    pool.wait_ge(variance, 1)
                    nc.gpsimd.tensor_tensor(stat[:, 0, :], stat[:, 3, :], minus_half[:, 0:1].to_broadcast([PT, 72]), ALU.pow).then_inc(rstd, 1)
            to_features([att[:, :, 0:128], att[:, :, 128:256]], 128, [FA[:, 0, :], FA[:, 1, :]], pad=False)
            token_products(64, lambda t: [(tile(FA[:, 0], t), aWout[:, 0, :]), (tile(FA[:, 1], t), aWout[:, 1, :]), (ones_row[:, :], aBout[:, :])], add_to_h)

        def mixture_of_depths():
            normed()
            with step("product", "copied", "linked") as (block, product, copied, linked):
                wb = P[0:PT, 0, :]

                @block.tensor
                def _(pe):
                    for c in range(NC):
                        last = nc.tensor.matmul(PS[0:PT, c, 0:CW], wr_b[:, :], chunk(xT, c), start=True, stop=True)
                    last.then_inc(product, 1)

                @block.scalar
                def _(act):
                    act.wait_ge(product, 1)
                    nc.scalar.activation(wb.rearrange("p (c n) -> p c n", n=CW), PS[0:PT, 0:3, 0:CW], ACT.Copy).then_inc(copied, 1)

                @block.vector
                def _(dve):
                    link = chain(dve, linked)
                    own, more, ties = stat[:, 0, 0:NT], stat[:, 1, 0:NT], stat[:, 2, 0:NT]
                    work = P[0:PT, 1, :]
                    dve.wait_ge(copied, 1)
                    link(nc.vector.tensor_tensor(work.rearrange("p (t n) -> p t n", n=PT), wb.rearrange("p (t n) -> p t n", n=PT),
                                                 ident[0:PT, 0:PT].unsqueeze(1).to_broadcast([PT, NT, PT]), ALU.mult))
                    link(nc.vector.reduce_sum(own, work.rearrange("p (t n) -> p t n", n=PT), AX.X))
                    for t in range(NT):
                        link(nc.vector.tensor_scalar(work[:, 0:T], wb[:, 0:T], own[:, t:t + 1], None, ALU.is_gt, ALU.add, accum_out=more[:, t:t + 1]))
                        link(nc.vector.scalar_tensor_tensor(work[:, 0:T], wb[:, 0:T], own[:, t:t + 1], earlier[:, TP - PT * t:TP - PT * t + T],
                                                            ALU.is_equal, ALU.mult, accum_out=ties[:, t:t + 1]))
                    link(nc.vector.tensor_tensor(more, more, ties, ALU.add))
                    link(nc.vector.tensor_scalar(more, more, float(CAPACITY), None, ALU.is_lt))
                    link(nc.vector.tensor_tensor(wd[:, 0, :], more, own, ALU.mult))
                    link(nc.vector.tensor_tensor(h[:, :, :], h[:, :, :], xn[:, :, :], ALU.add))
            experts(1, 256, ACT.Gelu_apprx_tanh, lambda e: A["L0_ffn_w1"], lambda e: A["L0_ffn_b1"], None,
                    lambda e: A["L0_ffn_w2"].rearrange("(g p) n -> p g n", g=2), lambda e: A["L0_ffn_b2"])

        def rotate(dst, main, swapped, rows, table, x, scale=1.0):
            def consume(g, c, bank):
                return nc.vector.tensor_tensor(chunk((dst, FB[0:rows, 1])[g], c), bank[0:rows, :],
                                               rope[0:rows, table + g, CW * c:CW * c + CW], ALU.mult)
            feature_products(2, lambda g, c: [((main, swapped)[g], chunk(x, c))], consume)
            with step("linked") as (block, linked):
                @block.vector
                def _(dve):
                    link = chain(dve, linked)
                    link(nc.vector.tensor_tensor(dst, dst, FB[0:rows, 1, :], ALU.add))
                    if scale != 1.0:
                        link(nc.vector.tensor_scalar_mul(dst, dst, scale))

        def latent_attention():
            normed()
            cq, ckv = FA[0:64, 0, :], FA[0:64, 1, :]
            feature_products(2, lambda g, c: [(W[("cq", "ckv")[g]][:, :], chunk(xT[0:64], c))], copy_chunk([cq, ckv], 64), on="scalar")
            rotate(q65[0:64], W["lq"][:, :], W["lqs"][:, :], 64, 0, cq, scale=0.125)
            rotate(k65[0:64], W["lk"][:, :], W["lks"][:, :], 64, 0, ckv)
            set_ones(vv[:, :, 64:65])
            token_products(64, lambda t: [(tile(ckv, t), W["lv"][:, :])],
                           lambda t0, t1, tiles: nc.vector.tensor_copy(vv[:, t0:t1, 0:64], tiles))
            mask_pad_values(vv[:, NT - 1, 0:65])
            with step("scores", "taken") as (block, scores, taken):
                maxima_pass(block, [(q65, k65, 0)], 64, True, False, [[]], scores, taken)
            with step("transposed", "copied") as (block, transposed, copied):
                @block.tensor
                def _(pe):
                    for t in range(NT):
                        last = nc.tensor.transpose(PS[0:1, t // 3, PT * (t % 3):PT * (t % 3) + PT], negmax[:, 0, t:t + 1], ident[0:PT, 0:PT])
                    last.then_inc(transposed, 1)

                @block.vector
                def _(dve):
                    dve.wait_ge(transposed, 1)
                    nc.vector.tensor_copy(q65[64:65, :].rearrange("p (c n) -> p c n", n=CW), PS[0:1, 0:3, 0:CW]).then_inc(copied, 1)
            wide_values_pass()

        def wide_values_pass():
            with step("scores", "raised", "summed", "linked") as (block, scores, raised, summed, linked):
                def O(t):
                    return PS[0:PT, 6 + t // 5, 65 * (t % 5):65 * (t % 5) + 65]

                @block.tensor
                def _(pe):
                    def weigh(j):
                        pe.wait_ge(raised, j + 1)
                        for t in range(j, NT):
                            last = nc.tensor.matmul(O(t), tile(P[0:PT, j % 2], t), vv[:, j, 0:65], start=(j == 0 and t in (0, 5)),
                                                    stop=(j == t), skip_group_check=True)
                        last.then_inc(summed, 1)
                    for j in range(NT):
                        if j >= 2:
                            pe.wait_ge(raised, j - 1)
                        b0, c0, r = 3 * (j % 2), j // 3, PT * (j % 3)
                        for c in range(c0, NC):
                            first = r if c == c0 else 0
                            last = nc.tensor.matmul(PS[0:PT, b0 + c, first:CW], tile(k65[0:65], j), q65[0:65, CW * c + first:CW * c + CW],
                                                    start=True, stop=(c != c0))
                            if c == c0:
                                last = nc.tensor.matmul(PS[0:PT, b0 + c, first:first + PT], ident_bf[0:PT, 0:PT], mask_k[:, :], start=False, stop=True)
                        last.then_inc(scores, 1)
                        if j:
                            weigh(j - 1)
                    weigh(NT - 1)

                @block.scalar
                def _(act):
                    for j in range(NT):
                        b0, c0, r = 3 * (j % 2), j // 3, PT * (j % 3)
                        act.wait_ge(scores, j + 1)
                        if j >= 2:
                            act.wait_ge(summed, j - 1)
                        if r:
                            last = nc.scalar.activation(P[0:PT, j % 2, CW * c0 + r:CW * c0 + CW], PS[0:PT, b0 + c0, r:CW], ACT.Exp)
                            c0 += 1
                        if c0 < NC:
                            last = nc.scalar.activation(P[0:PT, j % 2, CW * c0:TP].rearrange("p (c n) -> p c n", n=CW), PS[0:PT, b0 + c0:b0 + NC, 0:CW], ACT.Exp)
                        last.then_inc(raised, 1)

                @block.vector
                def _(dve):
                    link = chain(dve, linked)
                    dve.wait_ge(summed, NT)
                    for bank, t0, t1 in ((6, 0, 5), (7, 5, NT)):
                        o = PS[0:PT, bank, 0:65 * (t1 - t0)].rearrange("p (t n) -> p t n", n=65)
                        link(nc.vector.reciprocal(stat[:, 0, t0:t1], o[:, :, 64]))
                        link(nc.vector.tensor_tensor(sq[:, t0:t1, :], o[:, :, 0:64], bcast(stat[:, 0, t0:t1], 64), ALU.mult))
                    link(nc.vector.tensor_tensor(h[:, :, :], h[:, :, :], sq[:, :, :], ALU.add))

        def binary_experts():
            normed()
            gate = parts[0:24, 0, 0:TP]
            signs = parts[:, 1, 0:TP]
            feature_products(1, lambda g, c: [(gate_w[:, :], chunk(xT, c))],
                             lambda g, c, bank: nc.vector.tensor_scalar(chunk(gate, c), bank[0:24, :], 2.0 ** -23, None, ALU.is_gt))
            with step("signed") as (block, signed):
                @block.scalar
                def _(act):
                    for half in range(2):
                        nc.scalar.activation(signs[64 * half:64 * half + 64, :], xT[0:64, :], ACT.Sign).then_inc(signed, 1)
            pairs = D // 2
            with step("mixed", "signed", "multiplied", "summed", "scaled") as (block, mixed, signed, multiplied, summed, scaled):
                SLOTS = 4
                sg, pr = FA, FB
                sgb = FA[:, :, :].bitcast(bf16).rearrange("p a n -> p (a n)")
                prb = FB[:, :, :].bitcast(bf16).rearrange("p a n -> p (a n)")
                units = [(o, c) for o in range(pairs) for c in range(NC)]

                @block.tensor
                def _(pe):
                    def add_up(n):
                        o, c = units[n]
                        pe.wait_ge(multiplied, n + 1)
                        nc.tensor.matmul(PS[0:64, c, 0:CW], select_o[:, 62 - 2 * o:126 - 2 * o], prb[:, CW * (n % SLOTS):CW * (n % SLOTS) + CW],
                                         start=(o == 0), stop=(o == pairs - 1)).then_inc(summed, 1)
                    for n, (o, c) in enumerate(units):
                        if n >= SLOTS:
                            pe.wait_ge(signed, n - SLOTS + 1)
                        nc.tensor.matmul(PS[:, 3 + n % SLOTS, 0:CW], wsign[:, 128 * o:128 * o + 128], chunk(gate, c), start=True, stop=True).then_inc(mixed, 1)
                        if n >= 2:
                            add_up(n - 2)
                    add_up(len(units) - 2)
                    add_up(len(units) - 1)

                @block.scalar
                def _(act):
                    for n in range(len(units)):
                        act.wait_ge(mixed, n + 1)
                        if n >= SLOTS:
                            act.wait_ge(multiplied, n - SLOTS + 1)
                        nc.scalar.activation(sgb[:, CW * (n % SLOTS):CW * (n % SLOTS) + CW], PS[:, 3 + n % SLOTS, 0:CW], ACT.Sign).then_inc(signed, 1)

                @block.vector
                def _(dve):
                    for n, (o, c) in enumerate(units):
                        dve.wait_ge(signed, n + 1)
                        if n >= SLOTS:
                            dve.wait_ge(summed, n - SLOTS + 1)
                        nc.vector.tensor_tensor(prb[:, CW * (n % SLOTS):CW * (n % SLOTS) + CW], sgb[:, CW * (n % SLOTS):CW * (n % SLOTS) + CW],
                                                chunk(signs, c), ALU.mult).then_inc(multiplied, 1)
                    dve.wait_ge(summed, len(units))
                    nc.vector.tensor_scalar_mul(q65[0:64, :].rearrange("p (c n) -> p c n", n=CW), PS[0:64, 0:3, 0:CW], bscale[:, :]).then_inc(scaled, 1)
            token_products(64, lambda t: [(tile(q65[0:64], t), ident[0:64, 0:64])], add_to_h)

        def relative_attention():
            normed()
            feature_products(2, lambda g, c: [(W["qkv"][:, 64 * g:64 * g + 64], chunk(xT, c))],
                             copy_chunk([FA[0:64, 0, :], FB[0:64, 0, :]], 64), on="scalar")
            store_stacked(FA, 64, 1, scr_qb, SPLITS_Q, scale=8 ** -0.5)
            store_stacked(FB, 64, 1, scr_kb, SPLITS_K)
            v = vv[:, :, 0:72].rearrange("p t (h n) -> p t h n", n=9)
            set_ones(v[:, :, :, 8:9])
            token_products(64, lambda t: [(tile(xT, t), W["qkv"][:, 128:192])],
                           lambda t0, t1, tiles: nc.scalar.activation(v[:, t0:t1, :, 0:8], tiles.rearrange("p t (h n) -> p t h n", n=8), ACT.Copy), on="scalar")
            mask_pad_values(vv[:, NT - 1, 0:72])

            def combine(link, i, u, O):
                rec = stat[:, u, 0:NT]
                link(nc.vector.reciprocal(rec, O[:, :, 8]))
                link(nc.vector.tensor_tensor(sq[:, :, :].rearrange("p t (h n) -> p h t n", n=8)[:, i * 2 + u], O[:, :, 0:8], bcast(rec, 8), ALU.mult))
            stacked_attention(8, 8, scr_qb, scr_kb, False, 9, lambda i, u: lambda j: vv[:, j, 0:72].rearrange("p (h n) -> p h n", n=9)[:, i * 2 + u, :],
                              False, True, combine)
            to_features([sq], 64, [xT[0:64, :]], pad=False)
            token_products(64, lambda t: [(tile(xT, t), W["wproj"][:, :])], add_to_h)

        def erf_experts():
            normed()
            route_top2(W["rWg"][:, :], 65, False)
            experts(8, 256, ACT.Gelu, lambda e: A["L2_ffn_W1"][e], lambda e: A["L2_ffn_b1"][e], None,
                    lambda e: A["L2_ffn_W2"].rearrange("e (g p) n -> e p g n", g=2)[e], lambda e: A["L2_ffn_b2"][e])

        def column_attention():
            normed()
            x64 = xT[0:64]
            q, k = FA[0:64, 0, :], FA[0:64, 1, :]
            feature_products(2, lambda g, c: [(W[("gWq", "gWk")[g]][:, :], chunk(x64, c))], copy_chunk([q, k], 64), on="scalar")
            token_products(64, lambda t: [(tile(x64, t), W["gWv"][:, :])],
                           lambda t0, t1, tiles: nc.vector.tensor_copy(vv[:, t0:t1, 0:64], tiles))
            mask_pad_values(vv[:, NT - 1, 0:64])
            with step("scores", "maxed", "raised", "divided", "summed", "linked") as (block, scores, maxed, raised, divided, summed, linked):
                def banks(j):
                    return NC if j == 0 else j // 3 + 1

                def O(t):
                    return PS[0:PT, 6 + t // TPB, D * (t % TPB):D * (t % TPB) + D]

                @block.tensor
                def _(pe):
                    def weigh(j):
                        pe.wait_ge(divided, j + 1)
                        for t in range(NT if j == 0 else j + 1):
                            last = nc.tensor.matmul(O(t), tile(P[0:PT, j % 2], t), vv[:, j, 0:64], start=(j == 0 and t in (0, TPB)), stop=(j == NT - 1),
                                                    skip_group_check=True)
                        last.then_inc(summed, 1)
                    for j in range(NT):
                        b0, nb = 3 * (j % 2), banks(j)
                        if j >= 2:
                            pe.wait_ge(raised, j - 1)
                        for c in range(nb):
                            masked = j == 0 or c == nb - 1
                            last = nc.tensor.matmul(PS[0:PT, b0 + c, 0:CW], tile(k, j), chunk(q, c), start=True, stop=not masked)
                            if masked:
                                r = 0 if j == 0 else PT * (j % 3)
                                m = chunk(mask_cols, c) if j == 0 else mask_diag[:, 0:CW - r]
                                last = nc.tensor.matmul(PS[0:PT, b0 + c, r:CW], ident[0:PT, 0:PT], m, start=False, stop=True)
                        last.then_inc(scores, 1)
                        if j:
                            weigh(j - 1)
                    weigh(NT - 1)

                @block.vector
                def _(dve):
                    link = chain(dve, linked)

                    def divide(j):
                        dve.wait_ge(raised, j + 1)
                        link(nc.vector.reciprocal(stat[:, 1, j:j + 1], stat[:, 0, j:j + 1]))
                        nc.vector.tensor_scalar_mul(vv[:, j, 0:64], vv[:, j, 0:64], stat[:, 1, j:j + 1]).then_inc(divided, 1)
                    for j in range(NT):
                        b0, nb = 3 * (j % 2), banks(j)
                        dve.wait_ge(scores, j + 1)
                        link(nc.vector.tensor_reduce(negmax[:, 0, j:j + 1], PS[0:PT, b0:b0 + nb, 0:CW], AX.XY, ALU.max, negate=True))
                        nc.vector.tensor_scalar_mul(negmax[:, 1, j:j + 1], negmax[:, 0, j:j + 1], 0.125).then_inc(maxed, 1)
                        if j:
                            divide(j - 1)
                    divide(NT - 1)
                    dve.wait_ge(summed, NT)
                    link(nc.vector.tensor_tensor(h[:, 0:TPB, :], h[:, 0:TPB, :], PS[0:PT, 6, :].rearrange("p (t d) -> p t d", d=D), ALU.add))
                    link(nc.vector.tensor_tensor(h[:, TPB:NT, :], h[:, TPB:NT, :], PS[0:PT, 7:8, 0:D], ALU.add))

                @block.scalar
                def _(act):
                    for j in range(NT):
                        b0, nb = 3 * (j % 2), banks(j)
                        act.wait_ge(maxed, j + 1)
                        if j >= 2:
                            act.wait_ge(summed, j - 1)
                        nc.scalar.activation(P[0:PT, j % 2, 0:CW * nb].rearrange("p (c n) -> p c n", n=CW), PS[0:PT, b0:b0 + nb, 0:CW], ACT.Exp,
                                             bias=negmax[:, 1, j:j + 1], scale=0.125, accum_out=stat[:, 0, j:j + 1]).then_inc(raised, 1)

        def grouped_block():
            normalise(h[:, :, :], xn[:, :, :], True, 1e-5)
            normalise(xn[:, :, :], tmp[:, :, 0:64], False, 1e-6)
            to_features([tmp[:, :, 0:64]], 64, [xT[0:64, :]], scale=rms1[:, :])
            x64 = xT[0:64]
            rotate(FA[0:64, 0, :], W["fq"][:, :], W["fqs"][:, :], 64, 2, x64)
            store_stacked(FA, 64, 1, scr_qc, SPLITS_Q, scale=0.25)
            rotate(FA[0:32, 0, :], W["fk"][:, :], W["fks"][:, :], 32, 2, x64)
            store_stacked(FA, 32, 1, scr_kc, SPLITS_K)
            v = vv[:, :, 0:34].rearrange("p t (h n) -> p t h n", n=17)
            set_ones(v[:, :, :, 16:17])
            token_products(32, lambda t: [(tile(x64, t), W["fv"][:, :])],
                           lambda t0, t1, tiles: nc.scalar.activation(v[:, t0:t1, :, 0:16], tiles.rearrange("p t (h n) -> p t h n", n=16), ACT.Copy), on="scalar")
            mask_pad_values(vv[:, NT - 1, 0:34])

            def combine(link, i, u, O):
                rec = stat[:, u, 0:NT]
                link(nc.vector.reciprocal(rec, O[:, :, 16]))
                link(nc.vector.tensor_tensor(sq[:, :, :].rearrange("p t (h n) -> p h t n", n=16)[:, i * 2 + u], O[:, :, 0:16], bcast(rec, 16), ALU.mult))
            stacked_attention(4, 16, scr_qc, scr_kc, True, 17, lambda i, u: lambda j: vv[:, j, 0:34].rearrange("p (h n) -> p h n", n=17)[:, i, :],
                              True, False, combine)
            to_features([sq], 64, [xT[0:64, :]], pad=False)
            token_products(64, lambda t: [(tile(x64, t), W["fo"][:, :])],
                           lambda t0, t1, tiles: nc.vector.tensor_tensor(xn[:, t0:t1, :], xn[:, t0:t1, :], tiles, ALU.add))
            with step("added") as (block, added):
                @block.vector
                def _(dve):
                    nc.vector.tensor_tensor(h[:, :, :], h[:, :, :], xn[:, :, :], ALU.add).then_inc(added, 1)
            normalise(xn[:, :, :], tmp[:, :, 0:64], False, 1e-6)
            to_features([tmp[:, :, 0:64]], 64, [xT[0:64, :]], scale=rms2[:, :])
            route_top2(W["router"][:, :], 64, True)
            experts(8, 170, ACT.Silu, lambda e: A["L3_ffn_w1T"][e], None, lambda e: A["L3_ffn_w3T"][e],
                    lambda e: A["L3_ffn_w2T"].rearrange("e (g p) n -> e p g n", g=2)[e], None)

        layers = [differential_attention, mixture_of_depths, latent_attention, binary_experts, relative_attention, erf_experts,
                  column_attention, grouped_block]
        with nc.Fori(0, B) as b:
            tokeniser(b)
            for layer in layers[0:stop_after - 1]:
                layer()
            with step("stored") as (block, stored):
                @block.sync
                def _(sp):
                    full = NT - 1
                    sp.dma_start(out[:, 0:full * PT, :].rearrange("b (t p) d -> b p t d", p=PT)[b], h[:, 0:full, :]).then_inc(stored, 16)
                    sp.dma_start(out[:, full * PT:T, :][b], h[0:T - full * PT, full, :]).then_inc(stored, 16)
                    sp.wait_ge(stored, 32)


def diagonal(scr, which, head, first, width):
    base = scr[which, head]
    return bass.AP(base.tensor, base.offset + first - (PT - 1), [[1, PT], [1, width]])


def _layout(inputs):
    import numpy as np

    a = {k: np.ascontiguousarray(v) for k, v in inputs.items() if k != "L0_ffn_attention_mask"}
    row = lambda v: np.ascontiguousarray(v.reshape(1, -1))
    col = lambda v: np.ascontiguousarray(v.reshape(-1, 1))
    tr = lambda v: np.ascontiguousarray(np.swapaxes(v, -1, -2))
    out = {k: a[k] for k in ("x", "L0_tok_d_gamma_batched", "L0_tok_Wq", "L0_tok_Wk", "L0_tok_Wv", "L0_tok_Wo", "L0_attn_Wq", "L0_attn_Wkv",
                             "L0_attn_Wout", "L0_attn_Wg", "L0_ffn_wr", "L0_ffn_w1", "L0_ffn_w2", "L1_attn_Wq_comp", "L1_attn_Wkv_comp",
                             "L1_attn_Wqc", "L1_attn_Wqr", "L1_attn_Wkc", "L1_attn_Wkr", "L1_attn_Wv", "L2_attn_qkv_w", "L2_attn_proj_w",
                             "L2_ffn_Wg", "L2_ffn_W1", "L2_ffn_W2")}
    for k in ("L0_tok_bq", "L0_tok_bk", "L0_tok_bv", "L0_tok_bo", "L0_tok_prelu_a", "L0_attn_bout", "L0_attn_bg", "L0_attn_lq1", "L0_attn_lk1",
              "L0_attn_lq2", "L0_attn_lk2", "L0_attn_ln_gamma", "L0_attn_ln_beta", "L0_ffn_br", "L0_ffn_b1", "L0_ffn_b2", "L1_ffn_proj_b",
              "L2_attn_qkv_b", "L2_attn_proj_b", "L2_ffn_bg"):
        out[k] = row(a[k])
    for k in ("cls_tok", "L1_ffn_scale", "L3_ffn_ln1_w", "L3_ffn_ln2_w"):
        out[k] = col(a[k])
    for k in ("L2_ffn_b1", "L2_ffn_b2"):
        out[k] = np.ascontiguousarray(a[k][:, None, :])
    for k in ("L3_attn_Wq", "L3_attn_Wk", "L3_attn_Wv", "L3_ffn_wq", "L3_ffn_wk", "L3_ffn_wv", "L3_ffn_wo", "L1_ffn_proj_w",
              "L3_ffn_w1", "L3_ffn_w2", "L3_ffn_w3"):
        out[k + "T"] = tr(a[k])
    out["L3_ffn_routerT"] = tr(a["L3_ffn_router_w"])
    out["L1_ffn_weightT"] = np.ascontiguousarray(tr(a["L1_ffn_weight"][0]).reshape(8, -1))
    out["rpbT"] = tr(a["L2_attn_rpb_table"])
    out["rpbT_flipped"] = np.ascontiguousarray(out["rpbT"][:, ::-1])
    pair = np.arange(16) ^ 1
    out["L1_attn_Wqr_swapped"] = np.ascontiguousarray(a["L1_attn_Wqr"][:, pair])
    out["L1_attn_Wkr_swapped"] = np.ascontiguousarray(a["L1_attn_Wkr"][:, pair])
    half = lambda n: np.arange(n) ^ 8
    out["L3_ffn_wqT_rotated"] = np.ascontiguousarray(out["L3_ffn_wqT"][:, half(64)])
    out["L3_ffn_wkT_rotated"] = np.ascontiguousarray(out["L3_ffn_wkT"][:, half(32)])
    pos = np.arange(TP, dtype=np.float32)
    f = np.float32
    theta = f(1.0) / f(10000.0) ** (np.arange(8, dtype=f) / f(8))
    rope = np.zeros((64, 4, TP), f)
    rope[:48, 0] = 1.0
    for r in range(16):
        angle = pos * theta[r // 2]
        rope[48 + r, 0] = np.cos(angle)
        rope[48 + r, 1] = np.sin(angle) * (-1.0 if r % 2 == 0 else 1.0)
    for r in range(64):
        angle = pos * theta[r % 8]
        rope[r, 2] = np.cos(angle)
        rope[r, 3] = np.sin(angle) * (-1.0 if r % 16 < 8 else 1.0)
    out["rope"] = rope
    return out


STOP = LAST


def kernel(**inputs):
    import numpy as _np
    import concourse.bacc as _bacc
    from concourse import mybir as _mybir
    from concourse.bass_utils import run_bass_kernel_spmd as _run

    nc = _bacc.Bacc("TRN2", target_bir_lowering=False, num_devices=1)
    arrays, A = {}, {}
    for name, a in _layout(inputs).items():
        arrays["in_" + name] = a
        A[name] = nc.dram_tensor("in_" + name, a.shape, _mybir.dt.from_np(a.dtype), kind="ExternalInput").ap()
    bf = _mybir.dt.bfloat16
    scratch = [nc.dram_tensor(n, s, bf, kind="Internal").ap() for n, s in (
        ("scr_qa", (16, 16, 6, TP)), ("scr_ka", (16, 16, 6, TP)), ("scr_qb", (8, 8, 6, TP)), ("scr_kb", (8, 8, 6, TP)),
        ("scr_qc", (4, 16, 6, TP)), ("scr_kc", (2, 16, 6, TP)), ("scr_m", (16, 3, TP)))]
    scratch.append(nc.dram_tensor("scr_t", (2, 8, 384), _mybir.dt.float32, kind="Internal").ap())
    out = nc.dram_tensor("out", (B, T, D), _mybir.dt.float32, kind="ExternalOutput").ap()
    build(nc, A, scratch, out, STOP)
    r = _run(nc, [arrays], core_ids=[0])
    return r.results[0]["out"]
```

```python
import math
from contextlib import ExitStack, contextmanager

import concourse.bass as bass
from concourse import mybir

B, T0, D = 8, 1024, 64
T = T0 + 1
PT, NT = 114, 9
TP = PT * NT
NC, CW = 3, 342
TPB = 8
LAMBDA_INIT = 0.8 - 0.6 * math.exp(-0.3)
CAPACITY = T // 2 - 1
NEG = -1e30
RPB = 127
RPB0 = T - 1 - (RPB - 1)
SPLITS_Q = (0, 0, 0, 1, 1, 2)
SPLITS_K = (0, 1, 2, 0, 1, 0)
LAST = 9


def build(nc, A, scratch, out, stop_after=LAST):
    fp32, bf16 = mybir.dt.float32, mybir.dt.bfloat16
    ALU, ACT, AX = mybir.AluOpType, mybir.ActivationFunctionType, mybir.AxisListType
    stack = ExitStack()

    pool_sems = [stack.enter_context(nc.semaphore(f"step_{n}")) for n in range(13)]
    assert pool_sems[-1].num - pool_sems[0].num == 12

    def sb(name, shape, dt=fp32):
        return stack.enter_context(nc.sbuf_tensor(name, shape, dt))

    @contextmanager
    def step(*names):
        used = pool_sems[0:len(names)]
        with nc.Block() as block:
            yield (block, *used)
        nc.all_engine_barrier(sems_to_clear=range(used[0].num, used[-1].num + 1))

    def chain(eng, sem):
        count = [0]

        def link(ins):
            count[0] += 1
            ins.then_inc(sem, 1)
            eng.wait_ge(sem, count[0])
        return link

    with stack:
        PS = stack.enter_context(nc.psum_tensor("PS", [128, 8, 512], fp32))

        ident = sb("ident", [128, 128])
        ident_bf = sb("ident_bf", [128, 128], bf16)
        flip = sb("flip", [PT, PT])
        mask_q = sb("mask_q", [PT, CW], bf16)
        mask_k = sb("mask_k", [PT, CW], bf16)
        mask_cols = sb("mask_cols", [PT, TP])
        mask_diag = sb("mask_diag", [PT, CW])
        earlier = sb("earlier", [PT, 2 * TP], bf16)
        select_o = sb("select_o", [128, 128], bf16)
        minus_half = sb("minus_half", [PT, NT])
        ones_row = sb("ones_row", [1, PT])
        real_row = sb("real_row", [PT, 1])
        split1 = sb("split1", [24, 1])
        split2 = sb("split2", [24, 1])
        gammaT = sb("gammaT", [128, 8, T0])
        bias_q = sb("bias_q", [PT, 2, 8, RPB])
        bias_k = sb("bias_k", [PT, 2, 8, 128])
        wsign = sb("wsign", [24, 64 * 64], bf16)
        W = {}
        for name, cols in (("tWq", 64), ("tWk", 64), ("tWv", 64), ("tWo", 64), ("aWg", 256), ("wr", 1), ("rWg", 8),
                           ("qkv", 192), ("wproj", 64)):
            W[name] = sb("w_" + name, [65, cols])
        for name, cols in (("aWq", 256), ("aWk", 256), ("aWv", 256), ("cq", 64), ("ckv", 64), ("lq", 64), ("lqs", 64),
                           ("lk", 64), ("lks", 64), ("lv", 64), ("gWq", 64), ("gWk", 64), ("gWv", 64), ("fq", 64),
                           ("fqs", 64), ("fk", 32), ("fks", 32), ("fv", 32), ("fo", 64), ("router", 8)):
            W[name] = sb("w_" + name, [64, cols])
        gate_w = sb("gate_w", [65, 24])
        aWout = sb("aWout", [128, 2, 64])
        aBout = sb("aBout", [1, 64])
        lam_in = sb("lam_in", [PT, 4, 16])
        lam = sb("lam", [PT, 8])
        ln_g = sb("ln_g", [PT, 32])
        ln_b = sb("ln_b", [PT, 32])
        prelu = sb("prelu", [64, 1])
        bscale = sb("bscale", [64, 1])
        rms1 = sb("rms1", [64, 1])
        rms2 = sb("rms2", [64, 1])
        rope = sb("rope", [64, 4, TP])
        wr_b = sb("wr_b", [65, PT])
        h = sb("h", [PT, NT, D])
        xn = sb("xn", [PT, NT, D])
        sq = sb("sq", [PT, NT, D])
        stat = sb("stat", [PT, 4, 72])
        xT = sb("xT", [65, TP])
        FA = sb("FA", [128, 2, TP])
        FB = sb("FB", [128, 2, TP])
        parts = sb("parts", [128, 3, 2 * TP], bf16)
        qk = [(sb("q_pair0", [128, 2, TP], bf16), sb("k_pair0", [128, 2, TP], bf16)),
              tuple(parts[:, s, :].rearrange("p (u n) -> p u n", u=2) for s in (0, 1))]
        vv = sb("vv", [PT, NT, 8 * 33])
        P = sb("P", [128, 4, TP])
        att = sb("att", [PT, NT, 256])
        att_rows = att[:, :, :].rearrange("p t n -> p (t n)")
        q65, k65 = att_rows[0:65, 0:TP], att_rows[0:65, TP:2 * TP]
        gates = sb("gates", [PT, NT, 256])
        tmp = sb("tmp", [PT, NT, 256])
        negmax = sb("negmax", [PT, 2, NT])
        partmax = sb("partmax", [PT, 2 * NT, NC])
        mparts = sb("mparts", [2 * NT, 3, PT], bf16)
        wd = sb("wd", [PT, 8, NT])
        vpair = sb("vpair", [PT, 2, NT, 33])
        stat_rows = sb("stat_rows", [2 * NT, PT])
        w1 = sb("w1", [65, 2, 256])
        w2 = sb("w2", [128, 2, D])
        b2 = sb("b2", [1, D])
        lg = sb("lg", [PT, 5, NT, 8])
        cmp8 = tmp[:, :, 0:64].rearrange("p t (a b) -> p t a b", b=8)
        x_tok = FB[:, 0, 0:8 * D].rearrange("p (t d) -> p t d", d=D)
        
        scr_qa, scr_ka, scr_qb, scr_kb, scr_qc, scr_kc, scr_t = scratch

        def bcast(ap, n):
            return ap.unsqueeze(2).to_broadcast([ap.shape[0], ap.shape[1], n])

        loads = [(W["tWq"][0:64, :], A["L0_tok_Wq"]), (W["tWq"][64:65, :], A["L0_tok_bq"]),
                 (W["tWk"][0:64, :], A["L0_tok_Wk"]), (W["tWk"][64:65, :], A["L0_tok_bk"]),
                 (W["tWv"][0:64, :], A["L0_tok_Wv"]), (W["tWv"][64:65, :], A["L0_tok_bv"]),
                 (W["tWo"][0:64, :], A["L0_tok_Wo"]), (W["tWo"][64:65, :], A["L0_tok_bo"]),
                 (W["aWq"][:, :], A["L0_attn_Wq"]), (W["aWk"][:, :], A["L0_attn_Wkv"][:, 0:256]),
                 (W["aWv"][:, :], A["L0_attn_Wkv"][:, 256:512]),
                 (W["aWg"][0:64, :], A["L0_attn_Wg"]), (W["aWg"][64:65, :], A["L0_attn_bg"]),
                 (W["wr"][0:64, :], A["L0_ffn_wr"]), (W["wr"][64:65, :], A["L0_ffn_br"]),
                 (W["rWg"][0:64, :], A["L2_ffn_Wg"]), (W["rWg"][64:65, :], A["L2_ffn_bg"]),
                 (W["qkv"][0:64, :], A["L2_attn_qkv_w"]), (W["qkv"][64:65, :], A["L2_attn_qkv_b"]),
                 (W["wproj"][0:64, :], A["L2_attn_proj_w"]), (W["wproj"][64:65, :], A["L2_attn_proj_b"]),
                 (W["cq"][:, :], A["L1_attn_Wq_comp"]), (W["ckv"][:, :], A["L1_attn_Wkv_comp"]),
                 (W["lq"][:, 0:48], A["L1_attn_Wqc"]), (W["lq"][:, 48:64], A["L1_attn_Wqr"]),
                 (W["lqs"][:, 0:48], A["L1_attn_Wqc"]), (W["lqs"][:, 48:64], A["L1_attn_Wqr_swapped"]),
                 (W["lk"][:, 0:48], A["L1_attn_Wkc"]), (W["lk"][:, 48:64], A["L1_attn_Wkr"]),
                 (W["lks"][:, 0:48], A["L1_attn_Wkc"]), (W["lks"][:, 48:64], A["L1_attn_Wkr_swapped"]),
                 (W["lv"][:, :], A["L1_attn_Wv"]),
                 (W["gWq"][:, :], A["L3_attn_WqT"]), (W["gWk"][:, :], A["L3_attn_WkT"]), (W["gWv"][:, :], A["L3_attn_WvT"]),
                 (W["fq"][:, :], A["L3_ffn_wqT"]), (W["fqs"][:, :], A["L3_ffn_wqT_rotated"]),
                 (W["fk"][:, :], A["L3_ffn_wkT"]), (W["fks"][:, :], A["L3_ffn_wkT_rotated"]),
                 (W["fv"][:, :], A["L3_ffn_wvT"]), (W["fo"][:, :], A["L3_ffn_woT"]), (W["router"][:, :], A["L3_ffn_routerT"]),
                 (aWout[:, :, :], A["L0_attn_Wout"].rearrange("(g p) n -> p g n", p=128)), (aBout[:, :], A["L0_attn_bout"]),
                 (ln_g[:, :], A["L0_attn_ln_gamma"].to_broadcast([PT, 32])),
                 (ln_b[:, :], A["L0_attn_ln_beta"].to_broadcast([PT, 32])),
                 (prelu[:, :], A["L0_tok_prelu_a"].to_broadcast([64, 1])),
                 (bscale[:, :], A["L1_ffn_scale"]), (rms1[:, :], A["L3_ffn_ln1_w"]), (rms2[:, :], A["L3_ffn_ln2_w"]),
                 (rope[:, :, :], A["rope"])]
        loads += [(lam_in[:, n, :], A["L0_attn_" + v].to_broadcast([PT, 16])) for n, v in enumerate(("lq1", "lk1", "lq2", "lk2"))]
        for part in range(3):
            loads += [(gate_w[0:64, 8 * part:8 * part + 8], A["L1_ffn_proj_wT"]), (gate_w[64:65, 8 * part:8 * part + 8], A["L1_ffn_proj_b"])]

        with step("weights_loaded", "zeroed", "made") as (block, weights_loaded, zeroed, made):
            @block.sync
            def _(sp):
                for dst, src in loads:
                    sp.dma_start(dst, src).then_inc(weights_loaded, 16)
                sp.wait_ge(weights_loaded, 16 * len(loads))

            @block.gpsimd
            def _(pool):
                cleared = [(t, 0.0) for t in (ident, ident_bf, flip, mask_q, mask_k, mask_diag, mask_cols, select_o)]
                cleared += [(t, 1.0) for t in (earlier, real_row, split1, split2, ones_row)] + [(minus_half, -0.5)]
                clear = chain(pool, zeroed)
                for t, value in cleared:
                    clear(nc.gpsimd.memset(t[tuple(slice(None) for _ in t.shape)], value))
                clear(nc.gpsimd.memset(xT[64:65, :], 1.0))
                link = chain(pool, made)

                def where(ap, compare, fill, base, pattern, channel):
                    link(nc.gpsimd.affine_select(out=ap, in_=ap, compare_op=compare, fill=fill, base=base,
                                                 pattern=pattern, channel_multiplier=channel))
                for m in (ident, ident_bf):
                    where(m[:, :], ALU.not_equal, 1.0, 0, [[-1, 128]], 1)
                where(flip[:, :], ALU.not_equal, 1.0, 1 - PT, [[1, PT]], 1)
                where(mask_q[:, :], ALU.is_ge, NEG, 0, [[-1, CW]], 1)
                where(mask_k[:, :], ALU.is_ge, NEG, PT - CW, [[1, CW]], -1)
                where(mask_cols[:, :], ALU.is_gt, -1e10, 0, [[-1, TP]], 1)
                where(mask_cols[:, T:TP], ALU.is_gt, NEG, -1, [[-1, 1]], 0)
                where(mask_diag[:, :], ALU.is_gt, -1e10, 0, [[-1, CW]], 1)
                where(mask_diag[:, :], ALU.is_gt, NEG, PT, [[-1, CW]], 0)
                where(earlier[:, :], ALU.is_gt, 0.0, TP, [[-1, 2 * TP]], 1)
                where(real_row[:, :], ALU.is_gt, 0.0, PT - 1, [[0, 1]], -1)
                where(split1[:, :], ALU.is_ge, 0.0, -8, [[0, 1]], 1)
                where(split2[:, :], ALU.is_ge, 0.0, -16, [[0, 1]], 1)
                link(nc.gpsimd.memset(select_o[0:64, 62:63], 1.0))
                link(nc.gpsimd.memset(select_o[64:128, 63:64], 1.0))

        with step("made", "raised", "loaded", "stored") as (block, made, raised, loaded, stored):
            table = FA[0:8, 0, 0:384]
            flipped = FA[0:8, 1, 0:384]
            raw = FB[0:8, 0, 0:2 * RPB + 1]

            @block.sync
            def _(sp):
                sp.dma_start(raw[:, 0:RPB], A["rpbT"]).then_inc(loaded, 16)
                sp.dma_start(raw[:, RPB:2 * RPB], A["rpbT_flipped"]).then_inc(loaded, 16)
                sp.wait_ge(made, 11)
                sp.dma_start(scr_t[0], table).then_inc(stored, 16)
                sp.dma_start(scr_t[1], flipped).then_inc(stored, 16)
                sp.wait_ge(stored, 32)

            @block.vector
            def _(dve):
                link = chain(dve, made)
                link(nc.vector.tensor_tensor(lam_in[:, 0, :], lam_in[:, 0, :], lam_in[:, 1, :], ALU.mult))
                link(nc.vector.tensor_tensor(lam_in[:, 2, :], lam_in[:, 2, :], lam_in[:, 3, :], ALU.mult))
                link(nc.vector.reduce_sum(lam[:, 0:1], lam_in[:, 0, :], AX.X))
                link(nc.vector.reduce_sum(lam[:, 1:2], lam_in[:, 2, :], AX.X))
                link(nc.vector.memset(FA[0:8, :, 0:384], 0.0))
                dve.wait_ge(loaded, 32)
                link(nc.vector.tensor_scalar(table[:, 1:1 + RPB], raw[:, 0:RPB], raw[:, RPB - 1:RPB], None, ALU.subtract))
                link(nc.vector.tensor_scalar(flipped[:, 227:227 + RPB], raw[:, RPB:2 * RPB], raw[:, RPB - 1:RPB], None, ALU.subtract))
                link(nc.vector.tensor_scalar_mul(ln_g[:, :], ln_g[:, :], 1.0 - LAMBDA_INIT))
                link(nc.vector.tensor_scalar_mul(ln_b[:, :], ln_b[:, :], 1.0 - LAMBDA_INIT))
                link(nc.vector.memset(wr_b[:, :], 1.0))
                link(nc.vector.tensor_scalar_mul(wr_b[:, :], wr_b[:, :], W["wr"][:, :]))
                dve.wait_ge(raised, 1)
                link(nc.vector.tensor_tensor(lam[:, 4:5], lam[:, 3:4], lam[:, 2:3], ALU.subtract))
                link(nc.vector.tensor_scalar_add(lam[:, 5:6], lam[:, 4:5], -LAMBDA_INIT))

            @block.scalar
            def _(act):
                act.wait_ge(made, 4)
                nc.scalar.activation(lam[:, 2:4], lam[:, 0:2], ACT.Exp).then_inc(raised, 1)

        with step("loaded", "split") as (block, loaded, split):
            whole = FB[0:24, :, :].rearrange("p a n -> p (a n)")

            @block.sync
            def _(sp):
                for half in range(2):
                    for part in range(3):
                        sp.dma_start(P[8 * part:8 * part + 8, half, 0:1024], A["L1_ffn_weightT"][:, 2048 * half:2048 * half + 1024]).then_inc(loaded, 16)
                        sp.dma_start(FA[8 * part:8 * part + 8, half, 0:1024], A["L1_ffn_weightT"][:, 2048 * half + 1024:2048 * half + 2048]).then_inc(loaded, 16)
                for tile in range(2):
                    for head in range(8):
                        q0 = 227 - PT * tile
                        sp.dma_start(bias_q[:, tile, head, :], diagonal(scr_t, 1, head, q0, RPB)).then_inc(loaded, 16)
                        k0 = 1 + T - 1 - PT * (7 + tile)
                        sp.dma_start(bias_k[:, tile, head, :], diagonal(scr_t, 0, head, k0, 128)).then_inc(loaded, 16)
                sp.wait_ge(loaded, 16 * (12 + 32))

            @block.vector
            def _(dve):
                dve.wait_ge(loaded, 16 * (12 + 32))
                link = chain(dve, split)
                for q, buf in enumerate((P[0:24, 0, 0:1024], FA[0:24, 0, 0:1024], P[0:24, 1, 0:1024], FA[0:24, 1, 0:1024])):
                    dst = wsign[:, 1024 * q:1024 * q + 1024]
                    work = FB[0:24, 0, 0:1024]
                    for mask in (split1, split2):
                        link(nc.vector.tensor_copy(dst, buf))
                        link(nc.vector.tensor_scalar_mul(work, dst, mask[:, :]))
                        link(nc.vector.tensor_tensor(buf, buf, work, ALU.subtract))
                    link(nc.vector.tensor_copy(dst, buf))
                link(nc.vector.memset(bias_k[0:1, 1, :, :], 0.0))

        with step("loaded_even", "loaded_odd", "transposed", "copied") as (block, loaded_even, loaded_odd, transposed, copied):
            loaded = (loaded_even, loaded_odd)

            @block.sync
            def _(sp):
                for t in range(8):
                    if t >= 2:
                        sp.wait_ge(transposed, t - 1)
                    sp.dma_start(P[:, t % 2, 0:T0], A["L0_tok_d_gamma_batched"][128 * t:128 * t + 128, :]).then_inc(loaded[t % 2], 16)

            @block.tensor
            def _(pe):
                for t in range(8):
                    pe.wait_ge(loaded[t % 2], 16 * (t // 2 + 1))
                    if t >= 2:
                        pe.wait_ge(copied, t - 1)
                    for s in range(8):
                        last = nc.tensor.transpose(PS[:, 2 * (t % 2) + s // 4, 128 * (s % 4):128 * (s % 4) + 128],
                                                   P[:, t % 2, 128 * s:128 * s + 128], ident[:, :])
                    last.then_inc(transposed, 1)

            @block.scalar
            def _(act):
                for t in range(8):
                    act.wait_ge(transposed, t + 1)
                    nc.scalar.activation(gammaT[:, :, 128 * t:128 * t + 128].rearrange("p (a s) n -> p a s n", a=2),
                                         PS[:, 2 * (t % 2):2 * (t % 2) + 2, :].rearrange("p a (s n) -> p a s n", n=128),
                                         ACT.Copy).then_inc(copied, 1)

        def feature_products(groups, terms, consume, on="vector"):
            with step("product", "consumed") as (block, product, consumed):
                @block.tensor
                def _(pe):
                    for g in range(groups):
                        for c in range(NC):
                            pairs = terms(g, c)
                            for n, (lhsT, rhs) in enumerate(pairs):
                                last = nc.tensor.matmul(PS[0:lhsT.shape[-1], 3 * g + c, 0:CW], lhsT, rhs,
                                                        start=(n == 0), stop=(n == len(pairs) - 1))
                            last.then_inc(product, 1)

                def program(eng):
                    for g in range(groups):
                        for c in range(NC):
                            eng.wait_ge(product, 3 * g + c + 1)
                            consume(g, c, PS[:, 3 * g + c, 0:CW]).then_inc(consumed, 1)
                (block.vector if on == "vector" else block.scalar)(program)

        def token_products(width, terms, consume, on="vector"):
            per = min(512 // width, NT)
            banks = -(-NT // per)
            with step("product", "consumed") as (block, product, consumed):
                @block.tensor
                def _(pe):
                    for t in range(NT):
                        pairs = terms(t)
                        for n, (lhsT, rhs) in enumerate(pairs):
                            last = nc.tensor.matmul(PS[0:PT, t // per, width * (t % per):width * (t % per) + width], lhsT, rhs,
                                                    start=(n == 0), stop=(n == len(pairs) - 1))
                        if t % per == per - 1 or t == NT - 1:
                            last.then_inc(product, 1)

                def program(eng):
                    for b in range(banks):
                        t0, t1 = b * per, min(NT, b * per + per)
                        eng.wait_ge(product, b + 1)
                        consume(t0, t1, PS[0:PT, b, 0:width * (t1 - t0)].rearrange("p (t n) -> p t n", n=width)).then_inc(consumed, 1)
                (block.vector if on == "vector" else block.scalar)(program)

        def tile(ap, t):
            return ap[:, PT * t:PT * t + PT]

        def chunk(ap, c):
            return ap[:, CW * c:CW * c + CW]

        def normalise(src, dst, layer, eps):
            with step("linked", "variance", "rstd") as (block, linked, variance, rstd):
                @block.vector
                def _(dve):
                    link = chain(dve, linked)
                    base = src
                    if layer:
                        link(nc.vector.reduce_sum(stat[:, 0, 0:NT], src, AX.X))
                        link(nc.vector.tensor_scalar_mul(stat[:, 1, 0:NT], stat[:, 0, 0:NT], -1.0 / D))
                        link(nc.vector.tensor_tensor(dst, src, bcast(stat[:, 1, 0:NT], D), ALU.add))
                        base = dst
                    link(nc.vector.tensor_tensor(sq[:, :, :], base, base, ALU.mult))
                    link(nc.vector.reduce_sum(stat[:, 2, 0:NT], sq[:, :, :], AX.X))
                    nc.vector.tensor_scalar(stat[:, 3, 0:NT], stat[:, 2, 0:NT], 1.0 / D, eps, ALU.mult, ALU.add).then_inc(variance, 1)
                    dve.wait_ge(rstd, 1)
                    link(nc.vector.tensor_tensor(dst, base, bcast(stat[:, 0, 0:NT], D), ALU.mult))

                @block.gpsimd
                def _(pool):
                    pool.wait_ge(variance, 1)
                    nc.gpsimd.tensor_tensor(stat[:, 0, 0:NT], stat[:, 3, 0:NT], minus_half[:, :], ALU.pow).then_inc(rstd, 1)

        def to_features(src, rows, dst, pad=True, scale=None):
            with step("transposed", "copied") as (block, transposed, copied):
                @block.tensor
                def _(pe):
                    for g, s in enumerate(src):
                        for t in range(NT):
                            last = nc.tensor.transpose(PS[0:rows, 3 * g + t // 3, PT * (t % 3):PT * (t % 3) + PT], s[:, t, :],
                                                       ident[0:PT, 0:PT])
                            if t % 3 == 2:
                                last.then_inc(transposed, 1)

                @block.vector
                def _(dve):
                    for g, d in enumerate(dst):
                        for c in range(NC):
                            dve.wait_ge(transposed, 3 * g + c + 1)
                            if scale is None:
                                nc.vector.tensor_copy(chunk(d, c), PS[0:rows, 3 * g + c, 0:CW]).then_inc(copied, 1)
                            else:
                                nc.vector.tensor_scalar_mul(chunk(d, c), PS[0:rows, 3 * g + c, 0:CW], scale).then_inc(copied, 1)
                    if pad:
                        dve.wait_ge(copied, 3 * len(dst))
                        for d in dst:
                            nc.vector.tensor_copy(d[:, T:TP], d[:, 0:1]).then_inc(copied, 1)

        def add_to_h(t0, t1, tiles):
            return nc.vector.tensor_tensor(h[:, t0:t1, :], h[:, t0:t1, :], tiles, ALU.add)

        def copy_chunk(dst, rows):
            return lambda g, c, bank: nc.scalar.activation(chunk(dst[g], c), bank[0:rows, :], ACT.Copy)

        def store_stacked(x, rows, groups, scr, splits, scale=1.0):
            flat = x[0:rows, 0:groups, :].rearrange("p g n -> p (g n)")
            P1, P2, P3 = (parts[0:rows, s, 0:groups * TP] for s in range(3))
            with step("linked", "stored") as (block, linked, stored):
                @block.vector
                def _(dve):
                    link = chain(dve, linked)
                    if scale != 1.0:
                        link(nc.vector.tensor_scalar_mul(flat, flat, scale))
                    link(nc.vector.tensor_copy(P1, flat))
                    link(nc.vector.tensor_tensor(flat, flat, P1, ALU.subtract))
                    link(nc.vector.tensor_copy(P2, flat))
                    link(nc.vector.tensor_tensor(P3, flat, P2, ALU.subtract))

                @block.sync
                def _(sp):
                    count = 0
                    for slot, part in sorted(enumerate(splits), key=lambda sp_: sp_[1]):
                        sp.wait_ge(linked, (0, 1, 3, 4)[part + 1] + (scale != 1.0))
                        for g in range(groups):
                            sp.dma_start(scr.rearrange("h r s n -> (h r) s n")[rows * g:rows * g + rows, slot, :],
                                         parts[0:rows, part, TP * g:TP * g + TP]).then_inc(stored, 16)
                            count += 1
                    sp.wait_ge(stored, 16 * count)

        def attention_step(K, causal, bias, width, shared, maxima_of, values_of, load, combine):
            units_a = [(u, t, c) for u in range(2) for t in range(NT) for c in range(t // 3 + 1 if causal else NC)] if maxima_of else []
            units_b = [(j, u, c) for j in range(NT) for u in range(2) for c in range(j // 3 if causal else 0, NC)] if values_of else []
            groups = [(j, c) for j in range(NT) for c in range(j // 3 if causal else 0, NC)] if values_of else []
            raised_by = [units_b.index((j, 1, c)) + 1 for j, c in groups]
            LAG = 3

            def summed_before(j):
                return sum(g[0] <= j for g in groups)

            def ring(j, u, c):
                first = (j % 2 * 2 + u) * TP + CW * c
                return P[0:PT, :, :].rearrange("p a n -> p (a n)")[:, first:first + CW]

            with step("loaded_even", "loaded_odd", "scores_a", "taken", "scores_b", "raised", "summed", "copied", "max_transposed",
                      "out_transposed", "linked", "maxima_stored", "values_ready") as (
                    block, loaded_even, loaded_odd, scores_a, taken, scores_b, raised, summed, copied, max_transposed,
                    out_transposed, linked, maxima_stored, values_ready):
                loaded = (loaded_even, loaded_odd)

                @block.gpsimd
                def _(pool):
                    if values_of:
                        v, i = values_of[3:5]
                        for u in range(1 if shared else 2):
                            nc.gpsimd.tensor_copy(vpair[:, u, :, 0:width], v(i, u)).then_inc(values_ready, 1)

                @block.sync
                def _(sp):
                    if maxima_of:
                        load(sp, maxima_of, loaded)
                        q = maxima_of[0]
                        sp.wait_ge(linked, 5)
                        for u in range(2):
                            for part in range(3):
                                sp.dma_start(q[K + part:K + part + 1, u, :].rearrange("o (t n) -> o t n", n=PT),
                                             mparts[NT * u:NT * u + NT, part, :]).then_inc(maxima_stored, 16)
                        sp.wait_ge(maxima_stored, 16 * 6)

                @block.tensor
                def _(pe):
                    def query_major(n):
                        u, t, c = units_a[n]
                        q, k, heads = maxima_of
                        if t == 0 and c == 0:
                            pe.wait_ge(loaded[u], 32)
                        if n >= 2:
                            pe.wait_ge(taken, n - 1)
                        o = PS[0:PT, 3 + n % 2, :]
                        masked = causal and c == t // 3
                        biased = bias and t < 2 and c == 2
                        last = nc.tensor.matmul(o[:, 0:CW], tile(q[0:K, u], t), chunk(k[0:K, u], c), start=True, stop=not (masked or biased))
                        if masked:
                            r = PT * (t % 3)
                            last = nc.tensor.matmul(o[:, r:CW], ident_bf[0:PT, 0:PT], mask_q[:, 0:CW - r], start=False, stop=True)
                        if biased:
                            k0 = RPB0 - 2 * CW
                            last = nc.tensor.matmul(o[:, k0:k0 + RPB], flip[:, :], bias_q[:, t, heads[u], :], start=False, stop=True)
                        last.then_inc(scores_a, 1)

                    def key_major(n):
                        j, u, c = units_b[n]
                        q, k, heads, v, i = values_of
                        if n >= 3:
                            pe.wait_ge(raised, n - 2)
                        o = PS[0:PT, n % 3, :]
                        masked = causal and c == j // 3
                        biased = bias and j >= 7 and c == 0
                        last = nc.tensor.matmul(o[:, 0:CW], tile(k[0:K + 3, u], j), chunk(q[0:K + 3, u], c), start=True, stop=not (masked or biased))
                        if masked:
                            r = PT * (j % 3)
                            last = nc.tensor.matmul(o[:, 0:r + PT], ident_bf[0:PT, 0:PT], mask_k[:, CW - PT - r:CW], start=False, stop=True)
                        if biased:
                            last = nc.tensor.matmul(o[:, 0:128], flip[:, :], bias_k[:, j - 7, heads[u], :], start=False, stop=True)
                        last.then_inc(scores_b, 1)

                    def weigh(g):
                        j, c = groups[g]
                        if g == 0:
                            pe.wait_ge(values_ready, 1 if shared else 2)
                        pe.wait_ge(raised, raised_by[g])
                        for u in range(2):
                            last = nc.tensor.matmul(PS[64 * u:64 * u + width, 5 + c, 0:CW], vpair[:, 0 if shared else u, j, 0:width], ring(j, u, c),
                                                    start=(j == 0), stop=(j == (3 * c + 2 if causal else NT - 1)))
                        last.then_inc(summed, 1)
                    g = 0
                    for n in range(max(len(units_a), len(units_b))):
                        if n < len(units_b):
                            key_major(n)
                        if n < len(units_a):
                            query_major(n)
                        while g < len(groups) and raised_by[g] + LAG <= n:
                            weigh(g)
                            g += 1
                    while g < len(groups):
                        weigh(g)
                        g += 1
                    if maxima_of:
                        pe.wait_ge(linked, 1)
                        nc.tensor.transpose(PS[0:2 * NT, 3, 0:PT], negmax[:, :, :].rearrange("p u t -> p (u t)"), ident[0:PT, 0:PT]).then_inc(max_transposed, 1)
                    if values_of:
                        pe.wait_ge(copied, 2)
                        for t in range(NT):
                            last = nc.tensor.transpose(PS[0:PT, t // 3, 97 * (t % 3):97 * (t % 3) + 97], tile(FA[0:97, 0], t), ident[0:97, 0:97])
                        last.then_inc(out_transposed, 1)

                def copy_sums(eng, u):
                    eng.wait_ge(summed, len(groups))
                    dst = FA[64 * u:64 * u + width, 0, :].rearrange("p (c n) -> p c n", n=CW)
                    src = PS[64 * u:64 * u + width, 5:8, 0:CW]
                    return nc.scalar.activation(dst, src, ACT.Copy) if u == 0 else nc.vector.tensor_copy(dst, src)

                @block.scalar
                def _(act):
                    for n, (j, u, c) in enumerate(units_b):
                        act.wait_ge(scores_b, n + 1)
                        if j >= 2:
                            act.wait_ge(summed, summed_before(j - 2))
                        nc.scalar.activation(ring(j, u, c), PS[0:PT, n % 3, 0:CW], ACT.Exp).then_inc(raised, 1)
                    if values_of:
                        copy_sums(act, 0).then_inc(copied, 1)

                @block.vector
                def _(dve):
                    link = chain(dve, linked)
                    for n, (u, t, c) in enumerate(units_a):
                        dve.wait_ge(scores_a, n + 1)
                        nc.vector.tensor_reduce(partmax[:, NT * u + t, c:c + 1], PS[0:PT, 3 + n % 2, 0:CW], AX.X, ALU.max).then_inc(taken, 1)
                    if maxima_of:
                        dve.wait_ge(taken, len(units_a))
                        link(nc.vector.tensor_reduce(negmax[:, :, :].rearrange("p u t -> p (u t)"), partmax[:, :, :], AX.X, ALU.max, negate=True))
                    if maxima_of:
                        dve.wait_ge(max_transposed, 1)
                        rows = PS[0:2 * NT, 3, 0:PT]
                        p1, p2, p3 = (mparts[:, s, :] for s in range(3))
                        rest = stat_rows[:, :]
                        link(nc.vector.tensor_copy(p1, rows))
                        link(nc.vector.tensor_tensor(rest, rows, p1, ALU.subtract))
                        link(nc.vector.tensor_copy(p2, rest))
                        link(nc.vector.tensor_tensor(p3, rest, p2, ALU.subtract))
                    if values_of:
                        copy_sums(dve, 1).then_inc(copied, 1)
                        dve.wait_ge(out_transposed, 1)
                        for u in range(2):
                            combine(link, values_of[4], u, PS[0:PT, 0:3, 0:3 * 97].rearrange("p a (b n) -> p a b n", n=97)[:, :, :, 64 * u:64 * u + width])

        def stacked_attention(nh, d, scr_q, scr_k, shared_keys, width, shared_values, causal, bias, combine):
            def v_of(i, u):
                n = nh // 2 if shared_values else nh
                heads = vv[:, :, 0:n * width].rearrange("p t (h n) -> p h t n", n=width)
                return heads[:, i if shared_values else i * 2 + u]
            K = 6 * d
            pairs = nh // 2
            with step("ones_written", "cleared") as (block, ones_written, cleared):
                @block.gpsimd
                def _(pool):
                    link = chain(pool, ones_written)
                    base = K // 32 * 32
                    for q, k in qk:
                        link(nc.gpsimd.memset(k[base:base + 32, :, :], 1.0))

                @block.vector
                def _(dve):
                    nc.vector.memset(FA[0:97, 0, :], 0.0).then_inc(cleared, 1)
                    nc.vector.memset(partmax[:, :, :], NEG).then_inc(cleared, 1)

            def load(sp, maxima_of, sems):
                q, k, heads = maxima_of
                for u in range(2):
                    sp.dma_start(q[0:K, u, :], scr_q.rearrange("h r s n -> h (r s) n")[heads[u]]).then_inc(sems[u], 16)
                    sp.dma_start(k[0:K, u, :], scr_k.rearrange("h r s n -> h (r s) n")[heads[2] if shared_keys else heads[u]]).then_inc(sems[u], 16)

            def side_a(i, parity):
                return (*qk[parity], [i * 2, i * 2 + 1, i])

            def side_b(i, parity):
                return (*qk[parity], [i * 2, i * 2 + 1, i], v_of, i)

            def run(a, b):
                attention_step(K, causal, bias, width, shared_values, a, b, load, combine)

            run(side_a(0, 0), None)
            if pairs > 2:
                with nc.Fori(0, pairs // 2 - 1) as two:
                    run(side_a(two * 2 + 1, 1), side_b(two * 2, 0))
                    run(side_a(two * 2 + 2, 0), side_b(two * 2 + 1, 1))
            run(side_a(pairs - 1, 1), side_b(pairs - 2, 0))
            run(None, side_b(pairs - 1, 1))

        def nine(ap):
            return ap.rearrange("p (a b) n -> p a b n", b=3) if len(ap.shape) == 3 else ap.rearrange("p (a b) -> p a b", b=3)

        def over(ap, n):
            return ap.unsqueeze(3).to_broadcast([*ap.shape, n])

        def mask_pad_values(ap):
            with step("masked") as (block, masked):
                @block.vector
                def _(dve):
                    nc.vector.tensor_scalar_mul(ap, ap, real_row[:, :]).then_inc(masked, 1)

        def set_ones(ap):
            with step("set") as (block, done):
                @block.gpsimd
                def _(pool):
                    nc.gpsimd.memset(ap, 1.0).then_inc(done, 1)

        def experts(count, hidden, func, w1_of, b1_of, w3_of, w2_of, b2_of):
            F = hidden // 2
            K = 65 if b1_of else 64
            n_loads = 2 + bool(b1_of) + bool(w3_of) + bool(b2_of)
            with nc.Fori(0, count) as e:
                with step("loaded", "hidden_ready", "activated", "gated", "output") as (block, loaded, hidden_ready, activated, gated, output):
                    @block.sync
                    def _(sp):
                        sp.dma_start(w1[0:64, 0, 0:hidden], w1_of(e)).then_inc(loaded, 16)
                        sp.dma_start(w2[0:F, :, :], w2_of(e)).then_inc(loaded, 16)
                        if b1_of:
                            sp.dma_start(w1[64:65, 0, 0:hidden], b1_of(e)).then_inc(loaded, 16)
                        if w3_of:
                            sp.dma_start(w1[0:64, 1, 0:hidden], w3_of(e)).then_inc(loaded, 16)
                        if b2_of:
                            sp.dma_start(b2[:, :], b2_of(e)).then_inc(loaded, 16)

                    @block.tensor
                    def _(pe):
                        pe.wait_ge(loaded, 16 * n_loads)
                        for j in range(2):
                            if w3_of and j:
                                pe.wait_ge(gated, 1)
                            b0 = 0 if w3_of else 3 * j
                            for c in range(NC):
                                last = nc.tensor.matmul(PS[0:F, b0 + c, 0:CW], w1[0:K, 0, F * j:F * j + F], chunk(xT[0:K], c), start=True, stop=True)
                                if w3_of:
                                    last = nc.tensor.matmul(PS[0:F, 3 + c, 0:CW], w1[0:64, 1, F * j:F * j + F], chunk(xT[0:64], c), start=True, stop=True)
                            last.then_inc(hidden_ready, 1)
                        pe.wait_ge(gated if w3_of else activated, 2)
                        for t in range(NT):
                            o = PS[0:PT, 6 + t // TPB, D * (t % TPB):D * (t % TPB) + D]
                            nc.tensor.matmul(o, tile(FA[0:F, 0], t), w2[0:F, 0, :], start=True, stop=False)
                            last = nc.tensor.matmul(o, tile(FA[0:F, 1], t), w2[0:F, 1, :], start=False, stop=not b2_of)
                            if b2_of:
                                last = nc.tensor.matmul(o, ones_row[:, :], b2[:, :], start=False, stop=True)
                        last.then_inc(output, 1)

                    @block.scalar
                    def _(act):
                        for j in range(2):
                            b0 = 0 if w3_of else 3 * j
                            act.wait_ge(hidden_ready, j + 1)
                            nc.scalar.activation(FA[0:F, j, :].rearrange("p (c n) -> p c n", n=CW), PS[0:F, b0:b0 + 3, 0:CW], func).then_inc(activated, 1)

                    @block.vector
                    def _(dve):
                        if w3_of:
                            for j in range(2):
                                dve.wait_ge(activated, j + 1)
                                row = FA[0:F, j, :].rearrange("p (c n) -> p c n", n=CW)
                                nc.vector.tensor_tensor(row, row, PS[0:F, 3:6, 0:CW], ALU.mult).then_inc(gated, 1)
                        dve.wait_ge(output, 1)
                        for t in range(NT):
                            nc.vector.scalar_tensor_tensor(h[:, t, :], PS[0:PT, 6 + t // TPB, D * (t % TPB):D * (t % TPB) + D],
                                                           wd[:, e, t:t + 1], h[:, t, :], ALU.mult, ALU.add).then_inc(gated, 1)

        def route_top2(weights, K, probabilities):
            logit, shifted, raised_, key, chosen = (lg[:, n, :, :] for n in range(5))
            token_products(8, lambda t: [(tile(xT[0:K], t), weights)],
                           lambda t0, t1, tiles: nc.vector.tensor_copy(logit[:, t0:t1, :], tiles))
            with step("linked", "shift_ready", "raised") as (block, linked, shift_ready, raised):
                @block.vector
                def _(dve):
                    link = chain(dve, linked)
                    link(nc.vector.reduce_max(stat[:, 0, 0:NT], logit, AX.X))
                    nc.vector.tensor_tensor(shifted, logit, bcast(stat[:, 0, 0:NT], 8), ALU.subtract).then_inc(shift_ready, 1)
                    dve.wait_ge(raised, 1)
                    score = logit
                    if probabilities:
                        link(nc.vector.reduce_sum(stat[:, 1, 0:NT], raised_, AX.X))
                        link(nc.vector.reciprocal(stat[:, 2, 0:NT], stat[:, 1, 0:NT]))
                        link(nc.vector.tensor_tensor(key, raised_, bcast(stat[:, 2, 0:NT], 8), ALU.mult))
                        score = key
                    value = score if probabilities else raised_
                    for e in range(8):
                        own = score[:, :, e:e + 1]
                        link(nc.vector.tensor_tensor(cmp8[:, :, 0:e + 1, e], own.to_broadcast([PT, NT, e + 1]), score[:, :, 0:e + 1], ALU.is_gt))
                        if e < 7:
                            link(nc.vector.tensor_tensor(cmp8[:, :, e + 1:8, e], own.to_broadcast([PT, NT, 7 - e]), score[:, :, e + 1:8], ALU.is_ge))
                    link(nc.vector.reduce_sum(chosen, cmp8[:, :, :, :], AX.X))
                    link(nc.vector.tensor_scalar(chosen, chosen, 2.0, None, ALU.is_lt))
                    link(nc.vector.tensor_tensor(chosen, chosen, value, ALU.mult))
                    link(nc.vector.reduce_sum(stat[:, 1, 0:NT], chosen, AX.X))
                    if probabilities:
                        link(nc.vector.tensor_scalar_add(stat[:, 1, 0:NT], stat[:, 1, 0:NT], 1e-9))
                    link(nc.vector.reciprocal(stat[:, 2, 0:NT], stat[:, 1, 0:NT]))
                    link(nc.vector.tensor_tensor(wd[:, :, :].rearrange("p e t -> p t e"), chosen, bcast(stat[:, 2, 0:NT], 8), ALU.mult))

                @block.scalar
                def _(act):
                    act.wait_ge(shift_ready, 1)
                    nc.scalar.activation(raised_, shifted, ACT.Exp).then_inc(raised, 1)

        def tokeniser(b):
            hT = FB[0:64, 1, :]
            q, k, ret = FA[0:64, 0, 0:T0], FA[0:64, 1, 0:T0], q65
            v = vv[:, :, 0:64]
            vt = x_tok
            with step("loaded", "transposed", "copied", "padded") as (block, loaded, transposed, copied, padded):
                @block.sync
                def _(sp):
                    sp.dma_start(x_tok[:, :, :], A["x"].rearrange("b o (t p) d -> b (o p) t d", p=128)[b]).then_inc(loaded, 16)
                    sp.dma_start(hT[:, 0:1], A["cls_tok"]).then_inc(loaded, 16)

                @block.tensor
                def _(pe):
                    pe.wait_ge(loaded, 32)
                    for t in range(8):
                        last = nc.tensor.transpose(PS[0:64, t // 4, 128 * (t % 4):128 * (t % 4) + 128], x_tok[:, t, :], ident[:, :])
                    last.then_inc(transposed, 1)

                @block.scalar
                def _(act):
                    act.wait_ge(transposed, 1)
                    nc.scalar.activation(xT[0:64, 0:T0].rearrange("p (a n) -> p a n", a=2), PS[0:64, 0:2, :], ACT.Copy).then_inc(copied, 1)

                @block.gpsimd
                def _(pool):
                    nc.gpsimd.memset(hT[:, T:TP], 0.0).then_inc(padded, 1)
                    pool.wait_ge(padded, 1)
                    nc.gpsimd.memset(q65[64:65, :], 1.0).then_inc(padded, 1)

            with step("product", "copied") as (block, product, copied):
                @block.tensor
                def _(pe):
                    for n, w in enumerate((W["tWq"], W["tWk"])):
                        for c in range(2):
                            nc.tensor.matmul(PS[0:64, 2 * n + c, :], w[:, :], xT[:, 512 * c:512 * c + 512], start=True, stop=True).then_inc(product, 1)
                    for t in range(8):
                        last = nc.tensor.matmul(PS[:, 4, D * t:D * t + D], xT[:, 128 * t:128 * t + 128], W["tWv"][:, :], start=True, stop=True)
                    last.then_inc(product, 1)

                @block.scalar
                def _(act):
                    for n, dst in enumerate((q, k)):
                        act.wait_ge(product, 2 * n + 2)
                        nc.scalar.activation(dst.rearrange("p (a n) -> p a n", a=2), PS[0:64, 2 * n:2 * n + 2, :], ACT.Copy).then_inc(copied, 1)

                @block.vector
                def _(dve):
                    dve.wait_ge(product, 5)
                    nc.vector.tensor_copy(vt[:, :, :], PS[:, 4, :].rearrange("p (t d) -> p t d", d=D)).then_inc(copied, 1)

            with step("scores", "decayed", "summed", "copied") as (block, scores, decayed, summed, copied):
                @block.tensor
                def _(pe):
                    def weigh(s):
                        pe.wait_ge(decayed, s + 1)
                        for c in range(2):
                            last = nc.tensor.matmul(PS[0:64, 6 + c, :], vt[:, s, :], P[:, s % 2, 512 * c:512 * c + 512], start=(s == 0), stop=(s == 7))
                        last.then_inc(summed, 1)
                    for s in range(8):
                        if s >= 2:
                            pe.wait_ge(decayed, s - 1)
                        for c in range(2):
                            last = nc.tensor.matmul(PS[:, 2 * (s % 2) + c, :], k[:, 128 * s:128 * s + 128], q[:, 512 * c:512 * c + 512], start=True, stop=True)
                        last.then_inc(scores, 1)
                        if s:
                            weigh(s - 1)
                    weigh(7)

                @block.vector
                def _(dve):
                    for s in range(8):
                        dve.wait_ge(scores, s + 1)
                        if s >= 2:
                            dve.wait_ge(summed, s - 1)
                        nc.vector.tensor_tensor(P[:, s % 2, 0:T0].rearrange("p (a n) -> p a n", a=2), gammaT[:, s, :].rearrange("p (a n) -> p a n", a=2),
                                                PS[:, 2 * (s % 2):2 * (s % 2) + 2, :], ALU.mult).then_inc(decayed, 1)

                @block.scalar
                def _(act):
                    act.wait_ge(summed, 8)
                    nc.scalar.activation(ret[0:64, 0:T0].rearrange("p (a n) -> p a n", a=2), PS[0:64, 6:8, :], ACT.Copy).then_inc(copied, 1)

            with step("product", "linked") as (block, product, linked):
                @block.tensor
                def _(pe):
                    for c in range(2):
                        last = nc.tensor.matmul(PS[0:64, c, :], W["tWo"][:, :], ret[:, 512 * c:512 * c + 512], start=True, stop=True)
                    last.then_inc(product, 1)

                @block.vector
                def _(dve):
                    link = chain(dve, linked)
                    y = PS[0:64, 0:2, :]
                    below = FA[0:64, 0, 0:T0].rearrange("p (a n) -> p a n", a=2)
                    dve.wait_ge(product, 1)
                    link(nc.vector.tensor_scalar(below, y, 0.0, prelu[:, :], ALU.min, ALU.mult))
                    link(nc.vector.scalar_tensor_tensor(hT[:, 1:T].rearrange("p (a n) -> p a n", a=2), y, 0.0, below, ALU.max, ALU.add))

            with step("transposed", "copied") as (block, transposed, copied):
                @block.tensor
                def _(pe):
                    for t in range(NT):
                        last = nc.tensor.transpose(PS[0:PT, t // TPB, D * (t % TPB):D * (t % TPB) + D], tile(hT, t), ident[0:64, 0:64])
                    last.then_inc(transposed, 1)

                @block.vector
                def _(dve):
                    dve.wait_ge(transposed, 1)
                    nc.vector.tensor_copy(h[:, 0:TPB, :], PS[0:PT, 0, :].rearrange("p (t d) -> p t d", d=D)).then_inc(copied, 1)
                    nc.vector.tensor_copy(h[:, TPB:NT, :], PS[0:PT, 1:2, 0:D]).then_inc(copied, 1)

        def normed(eps=1e-5):
            normalise(h[:, :, :], xn[:, :, :], True, eps)
            to_features([xn], 64, [xT[0:64, :]])

        def differential_attention():
            normed()
            x64 = xT[0:64]
            for w, dst in (("aWq", FA), ("aWk", FB)):
                feature_products(2, lambda g, c: [(W[w][:, 128 * g:128 * g + 128], chunk(x64, c))],
                                 copy_chunk([dst[:, 0, :], dst[:, 1, :]], 128), on="scalar")
            store_stacked(FA, 128, 2, scr_qa, SPLITS_Q, scale=0.25)
            store_stacked(FB, 128, 2, scr_ka, SPLITS_K)
            v = vv[:, :, :].rearrange("p t (h n) -> p t h n", n=33)
            set_ones(v[:, :, :, 32:33])
            token_products(256, lambda t: [(tile(x64, t), W["aWv"][:, :])],
                           lambda t0, t1, tiles: nc.scalar.activation(v[:, t0:t1, :, 0:32], tiles.rearrange("p t (h n) -> p t h n", n=32), ACT.Copy), on="scalar")
            mask_pad_values(vv[:, NT - 1, :])
            token_products(256, lambda t: [(tile(xT, t), W["aWg"][:, :])],
                           lambda t0, t1, tiles: nc.scalar.activation(gates[:, t0:t1, :], tiles, ACT.Sigmoid), on="scalar")

            def combine(link, i, u, O):
                rec, half = nine(stat[:, u, 0:NT]), nine(tmp[:, :, 32 * u:32 * u + 32])
                link(nc.vector.reciprocal(rec, O[:, :, :, 32]))
                if u:
                    link(nc.vector.tensor_scalar_mul(rec, rec, lam[:, 5:6]))
                link(nc.vector.tensor_tensor(half, O[:, :, :, 0:32], over(rec, 32), ALU.mult))
                if u:
                    link(nc.vector.tensor_tensor(att[:, :, :].rearrange("p t (i n) -> p i t n", n=32)[:, i], tmp[:, :, 0:32], tmp[:, :, 32:64], ALU.add))
            stacked_attention(16, 16, scr_qa, scr_ka, False, 33, True, False, False, combine)

            with step("linked", "variance", "rstd") as (block, linked, variance, rstd):
                a3 = att[:, :, :].rearrange("p t (h n) -> p (t h) n", n=32)
                t3 = tmp[:, :, :].rearrange("p t (h n) -> p (t h) n", n=32)

                @block.vector
                def _(dve):
                    link = chain(dve, linked)
                    link(nc.vector.reduce_sum(stat[:, 0, :], a3, AX.X))
                    link(nc.vector.tensor_scalar_mul(stat[:, 1, :], stat[:, 0, :], -1.0 / 32))
                    link(nc.vector.tensor_tensor(a3, a3, bcast(stat[:, 1, :], 32), ALU.add))
                    link(nc.vector.tensor_tensor(t3, a3, a3, ALU.mult))
                    link(nc.vector.reduce_sum(stat[:, 2, :], t3, AX.X))
                    nc.vector.tensor_scalar(stat[:, 3, :], stat[:, 2, :], 1.0 / 32, 1e-5, ALU.mult, ALU.add).then_inc(variance, 1)
                    dve.wait_ge(rstd, 1)
                    link(nc.vector.tensor_tensor(a3, a3, bcast(stat[:, 0, :], 32), ALU.mult))
                    link(nc.vector.tensor_tensor(a3, a3, ln_g[:, :].unsqueeze(1).to_broadcast([PT, 72, 32]), ALU.mult))
                    link(nc.vector.tensor_tensor(a3, a3, ln_b[:, :].unsqueeze(1).to_broadcast([PT, 72, 32]), ALU.add))
                    link(nc.vector.tensor_tensor(att[:, :, :], att[:, :, :], gates[:, :, :], ALU.mult))

                @block.gpsimd
                def _(pool):
                    pool.wait_ge(variance, 1)
                    nc.gpsimd.tensor_tensor(stat[:, 0, :], stat[:, 3, :], minus_half[:, 0:1].to_broadcast([PT, 72]), ALU.pow).then_inc(rstd, 1)
            to_features([att[:, :, 0:128], att[:, :, 128:256]], 128, [FA[:, 0, :], FA[:, 1, :]], pad=False)
            token_products(64, lambda t: [(tile(FA[:, 0], t), aWout[:, 0, :]), (tile(FA[:, 1], t), aWout[:, 1, :]), (ones_row[:, :], aBout[:, :])], add_to_h)

        def mixture_of_depths():
            normed()
            with step("product", "copied", "linked") as (block, product, copied, linked):
                wb = P[0:PT, 0, :]

                @block.tensor
                def _(pe):
                    for c in range(NC):
                        last = nc.tensor.matmul(PS[0:PT, c, 0:CW], wr_b[:, :], chunk(xT, c), start=True, stop=True)
                    last.then_inc(product, 1)

                @block.scalar
                def _(act):
                    act.wait_ge(product, 1)
                    nc.scalar.activation(wb.rearrange("p (c n) -> p c n", n=CW), PS[0:PT, 0:3, 0:CW], ACT.Copy).then_inc(copied, 1)

                @block.vector
                def _(dve):
                    link = chain(dve, linked)
                    own, more, ties = stat[:, 0, 0:NT], stat[:, 1, 0:NT], stat[:, 2, 0:NT]
                    work = P[0:PT, 1, :]
                    dve.wait_ge(copied, 1)
                    link(nc.vector.tensor_tensor(work.rearrange("p (t n) -> p t n", n=PT), wb.rearrange("p (t n) -> p t n", n=PT),
                                                 ident[0:PT, 0:PT].unsqueeze(1).to_broadcast([PT, NT, PT]), ALU.mult))
                    link(nc.vector.reduce_sum(own, work.rearrange("p (t n) -> p t n", n=PT), AX.X))
                    for t in range(NT):
                        link(nc.vector.tensor_scalar(work[:, 0:T], wb[:, 0:T], own[:, t:t + 1], None, ALU.is_gt, ALU.add, accum_out=more[:, t:t + 1]))
                        link(nc.vector.scalar_tensor_tensor(work[:, 0:T], wb[:, 0:T], own[:, t:t + 1], earlier[:, TP - PT * t:TP - PT * t + T],
                                                            ALU.is_equal, ALU.mult, accum_out=ties[:, t:t + 1]))
                    link(nc.vector.tensor_tensor(more, more, ties, ALU.add))
                    link(nc.vector.tensor_scalar(more, more, float(CAPACITY), None, ALU.is_lt))
                    link(nc.vector.tensor_tensor(wd[:, 0, :], more, own, ALU.mult))
                    link(nc.vector.tensor_tensor(h[:, :, :], h[:, :, :], xn[:, :, :], ALU.add))
            experts(1, 256, ACT.Gelu_apprx_tanh, lambda e: A["L0_ffn_w1"], lambda e: A["L0_ffn_b1"], None,
                    lambda e: A["L0_ffn_w2"].rearrange("(g p) n -> p g n", g=2), lambda e: A["L0_ffn_b2"])

        def rotate(dst, main, swapped, rows, table, x, scale=1.0):
            def consume(g, c, bank):
                return nc.vector.tensor_tensor(chunk((dst, FB[0:rows, 1])[g], c), bank[0:rows, :],
                                               rope[0:rows, table + g, CW * c:CW * c + CW], ALU.mult)
            feature_products(2, lambda g, c: [((main, swapped)[g], chunk(x, c))], consume)
            with step("linked") as (block, linked):
                @block.vector
                def _(dve):
                    link = chain(dve, linked)
                    link(nc.vector.tensor_tensor(dst, dst, FB[0:rows, 1, :], ALU.add))
                    if scale != 1.0:
                        link(nc.vector.tensor_scalar_mul(dst, dst, scale))

        def latent_attention():
            normed()
            cq, ckv = FA[0:64, 0, :], FA[0:64, 1, :]
            feature_products(2, lambda g, c: [(W[("cq", "ckv")[g]][:, :], chunk(xT[0:64], c))], copy_chunk([cq, ckv], 64), on="scalar")
            rotate(q65[0:64], W["lq"][:, :], W["lqs"][:, :], 64, 0, cq, scale=0.125)
            rotate(k65[0:64], W["lk"][:, :], W["lks"][:, :], 64, 0, ckv)
            set_ones(vv[:, :, 64:65])
            set_ones(k65[64:65, :])
            token_products(64, lambda t: [(tile(ckv, t), W["lv"][:, :])],
                           lambda t0, t1, tiles: nc.vector.tensor_copy(vv[:, t0:t1, 0:64], tiles))
            mask_pad_values(vv[:, NT - 1, 0:65])
            wide_maxima_pass()
            with step("transposed", "copied") as (block, transposed, copied):
                @block.tensor
                def _(pe):
                    for t in range(NT):
                        last = nc.tensor.transpose(PS[0:1, t // 3, PT * (t % 3):PT * (t % 3) + PT], negmax[:, 0, t:t + 1], ident[0:PT, 0:PT])
                    last.then_inc(transposed, 1)

                @block.vector
                def _(dve):
                    dve.wait_ge(transposed, 1)
                    nc.vector.tensor_copy(q65[64:65, :].rearrange("p (c n) -> p c n", n=CW), PS[0:1, 0:3, 0:CW]).then_inc(copied, 1)
            wide_values_pass()

        def wide_maxima_pass():
            with step("scores", "taken") as (block, scores, taken):
                @block.tensor
                def _(pe):
                    for t in range(NT):
                        if t >= 2:
                            pe.wait_ge(taken, t - 1)
                        b0, nb, r = 3 * (t % 2), t // 3 + 1, PT * (t % 3)
                        for c in range(nb):
                            last = nc.tensor.matmul(PS[0:PT, b0 + c, 0:CW], tile(q65[0:64], t), chunk(k65[0:64], c), start=True, stop=(c != nb - 1))
                        last = nc.tensor.matmul(PS[0:PT, b0 + nb - 1, r:CW], ident_bf[0:PT, 0:PT], mask_q[:, 0:CW - r], start=False, stop=True)
                        last.then_inc(scores, 1)

                @block.vector
                def _(dve):
                    for t in range(NT):
                        b0, nb = 3 * (t % 2), t // 3 + 1
                        dve.wait_ge(scores, t + 1)
                        nc.vector.tensor_reduce(negmax[:, 0, t:t + 1], PS[0:PT, b0:b0 + nb, 0:CW], AX.XY, ALU.max, negate=True).then_inc(taken, 1)

        def wide_values_pass():
            with step("scores", "raised", "summed", "linked") as (block, scores, raised, summed, linked):
                def O(t):
                    return PS[0:PT, 6 + t // 5, 65 * (t % 5):65 * (t % 5) + 65]

                @block.tensor
                def _(pe):
                    def weigh(j):
                        pe.wait_ge(raised, j + 1)
                        for t in range(j, NT):
                            last = nc.tensor.matmul(O(t), tile(P[0:PT, j % 2], t), vv[:, j, 0:65], start=(j == 0 and t in (0, 5)),
                                                    stop=(j == t), skip_group_check=True)
                        last.then_inc(summed, 1)
                    for j in range(NT):
                        if j >= 2:
                            pe.wait_ge(raised, j - 1)
                        b0, c0, r = 3 * (j % 2), j // 3, PT * (j % 3)
                        for c in range(c0, NC):
                            first = r if c == c0 else 0
                            last = nc.tensor.matmul(PS[0:PT, b0 + c, first:CW], tile(k65[0:65], j), q65[0:65, CW * c + first:CW * c + CW],
                                                    start=True, stop=(c != c0))
                            if c == c0:
                                last = nc.tensor.matmul(PS[0:PT, b0 + c, first:first + PT], ident_bf[0:PT, 0:PT], mask_k[:, CW - PT:CW], start=False, stop=True)
                        last.then_inc(scores, 1)
                        if j:
                            weigh(j - 1)
                    weigh(NT - 1)

                @block.scalar
                def _(act):
                    for j in range(NT):
                        b0, c0, r = 3 * (j % 2), j // 3, PT * (j % 3)
                        act.wait_ge(scores, j + 1)
                        if j >= 2:
                            act.wait_ge(summed, j - 1)
                        if r:
                            last = nc.scalar.activation(P[0:PT, j % 2, CW * c0 + r:CW * c0 + CW], PS[0:PT, b0 + c0, r:CW], ACT.Exp)
                            c0 += 1
                        if c0 < NC:
                            last = nc.scalar.activation(P[0:PT, j % 2, CW * c0:TP].rearrange("p (c n) -> p c n", n=CW), PS[0:PT, b0 + c0:b0 + NC, 0:CW], ACT.Exp)
                        last.then_inc(raised, 1)

                @block.vector
                def _(dve):
                    link = chain(dve, linked)
                    dve.wait_ge(summed, NT)
                    for bank, t0, t1 in ((6, 0, 5), (7, 5, NT)):
                        o = PS[0:PT, bank, 0:65 * (t1 - t0)].rearrange("p (t n) -> p t n", n=65)
                        link(nc.vector.reciprocal(stat[:, 0, t0:t1], o[:, :, 64]))
                        link(nc.vector.tensor_tensor(sq[:, t0:t1, :], o[:, :, 0:64], bcast(stat[:, 0, t0:t1], 64), ALU.mult))
                    link(nc.vector.tensor_tensor(h[:, :, :], h[:, :, :], sq[:, :, :], ALU.add))

        def binary_experts():
            normed()
            gate = parts[0:24, 0, 0:TP]
            signs = parts[:, 1, 0:TP]
            feature_products(1, lambda g, c: [(gate_w[:, :], chunk(xT, c))],
                             lambda g, c, bank: nc.vector.tensor_scalar(chunk(gate, c), bank[0:24, :], 2.0 ** -23, None, ALU.is_gt))
            with step("signed") as (block, signed):
                @block.scalar
                def _(act):
                    for half in range(2):
                        nc.scalar.activation(signs[64 * half:64 * half + 64, :], xT[0:64, :], ACT.Sign).then_inc(signed, 1)
            pairs = D // 2
            with step("mixed", "signed", "multiplied", "summed", "scaled") as (block, mixed, signed, multiplied, summed, scaled):
                SLOTS = 4
                sg, pr = FA, FB
                sgb = FA[:, :, :].bitcast(bf16).rearrange("p a n -> p (a n)")
                prb = FB[:, :, :].bitcast(bf16).rearrange("p a n -> p (a n)")
                units = [(o, c) for o in range(pairs) for c in range(NC)]

                @block.tensor
                def _(pe):
                    def add_up(n):
                        o, c = units[n]
                        pe.wait_ge(multiplied, n + 1)
                        nc.tensor.matmul(PS[0:64, c, 0:CW], select_o[:, 62 - 2 * o:126 - 2 * o], prb[:, CW * (n % SLOTS):CW * (n % SLOTS) + CW],
                                         start=(o == 0), stop=(o == pairs - 1)).then_inc(summed, 1)
                    for n, (o, c) in enumerate(units):
                        if n >= SLOTS:
                            pe.wait_ge(signed, n - SLOTS + 1)
                        nc.tensor.matmul(PS[:, 3 + n % SLOTS, 0:CW], wsign[:, 128 * o:128 * o + 128], chunk(gate, c), start=True, stop=True).then_inc(mixed, 1)
                        if n >= 2:
                            add_up(n - 2)
                    add_up(len(units) - 2)
                    add_up(len(units) - 1)

                @block.scalar
                def _(act):
                    for n in range(len(units)):
                        act.wait_ge(mixed, n + 1)
                        if n >= SLOTS:
                            act.wait_ge(multiplied, n - SLOTS + 1)
                        nc.scalar.activation(sgb[:, CW * (n % SLOTS):CW * (n % SLOTS) + CW], PS[:, 3 + n % SLOTS, 0:CW], ACT.Sign).then_inc(signed, 1)

                @block.vector
                def _(dve):
                    for n, (o, c) in enumerate(units):
                        dve.wait_ge(signed, n + 1)
                        if n >= SLOTS:
                            dve.wait_ge(summed, n - SLOTS + 1)
                        nc.vector.tensor_tensor(prb[:, CW * (n % SLOTS):CW * (n % SLOTS) + CW], sgb[:, CW * (n % SLOTS):CW * (n % SLOTS) + CW],
                                                chunk(signs, c), ALU.mult).then_inc(multiplied, 1)
                    dve.wait_ge(summed, len(units))
                    nc.vector.tensor_scalar_mul(q65[0:64, :].rearrange("p (c n) -> p c n", n=CW), PS[0:64, 0:3, 0:CW], bscale[:, :]).then_inc(scaled, 1)
            token_products(64, lambda t: [(tile(q65[0:64], t), ident[0:64, 0:64])], add_to_h)

        def relative_attention():
            normed()
            feature_products(2, lambda g, c: [(W["qkv"][:, 64 * g:64 * g + 64], chunk(xT, c))],
                             copy_chunk([FA[0:64, 0, :], FB[0:64, 0, :]], 64), on="scalar")
            store_stacked(FA, 64, 1, scr_qb, SPLITS_Q, scale=8 ** -0.5)
            store_stacked(FB, 64, 1, scr_kb, SPLITS_K)
            v = vv[:, :, 0:72].rearrange("p t (h n) -> p t h n", n=9)
            set_ones(v[:, :, :, 8:9])
            token_products(64, lambda t: [(tile(xT, t), W["qkv"][:, 128:192])],
                           lambda t0, t1, tiles: nc.scalar.activation(v[:, t0:t1, :, 0:8], tiles.rearrange("p t (h n) -> p t h n", n=8), ACT.Copy), on="scalar")
            mask_pad_values(vv[:, NT - 1, 0:72])

            def combine(link, i, u, O):
                rec = nine(stat[:, u, 0:NT])
                link(nc.vector.reciprocal(rec, O[:, :, :, 8]))
                link(nc.vector.tensor_tensor(nine(sq[:, :, :].rearrange("p t (h n) -> p h t n", n=8)[:, i * 2 + u]), O[:, :, :, 0:8], over(rec, 8), ALU.mult))
            stacked_attention(8, 8, scr_qb, scr_kb, False, 9, False, False, True, combine)
            to_features([sq], 64, [xT[0:64, :]], pad=False)
            token_products(64, lambda t: [(tile(xT, t), W["wproj"][:, :])], add_to_h)

        def erf_experts():
            normed()
            route_top2(W["rWg"][:, :], 65, False)
            experts(8, 256, ACT.Gelu, lambda e: A["L2_ffn_W1"][e], lambda e: A["L2_ffn_b1"][e], None,
                    lambda e: A["L2_ffn_W2"].rearrange("e (g p) n -> e p g n", g=2)[e], lambda e: A["L2_ffn_b2"][e])

        def column_attention():
            normed()
            x64 = xT[0:64]
            q, k = FA[0:64, 0, :], FA[0:64, 1, :]
            feature_products(2, lambda g, c: [(W[("gWq", "gWk")[g]][:, :], chunk(x64, c))], copy_chunk([q, k], 64), on="scalar")
            token_products(64, lambda t: [(tile(x64, t), W["gWv"][:, :])],
                           lambda t0, t1, tiles: nc.vector.tensor_copy(vv[:, t0:t1, 0:64], tiles))
            mask_pad_values(vv[:, NT - 1, 0:64])
            with step("scores", "maxed", "raised", "divided", "summed", "linked") as (block, scores, maxed, raised, divided, summed, linked):
                def banks(j):
                    return NC if j == 0 else j // 3 + 1

                def O(t):
                    return PS[0:PT, 6 + t // TPB, D * (t % TPB):D * (t % TPB) + D]

                @block.tensor
                def _(pe):
                    def weigh(j):
                        pe.wait_ge(divided, j + 1)
                        for t in range(NT if j == 0 else j + 1):
                            last = nc.tensor.matmul(O(t), tile(P[0:PT, j % 2], t), vv[:, j, 0:64], start=(j == 0 and t in (0, TPB)), stop=(j == NT - 1),
                                                    skip_group_check=True)
                        last.then_inc(summed, 1)
                    for j in range(NT):
                        b0, nb = 3 * (j % 2), banks(j)
                        if j >= 2:
                            pe.wait_ge(raised, j - 1)
                        for c in range(nb):
                            masked = j == 0 or c == nb - 1
                            last = nc.tensor.matmul(PS[0:PT, b0 + c, 0:CW], tile(k, j), chunk(q, c), start=True, stop=not masked)
                            if masked:
                                r = 0 if j == 0 else PT * (j % 3)
                                m = chunk(mask_cols, c) if j == 0 else mask_diag[:, 0:CW - r]
                                last = nc.tensor.matmul(PS[0:PT, b0 + c, r:CW], ident[0:PT, 0:PT], m, start=False, stop=True)
                        last.then_inc(scores, 1)
                        if j:
                            weigh(j - 1)
                    weigh(NT - 1)

                @block.vector
                def _(dve):
                    link = chain(dve, linked)

                    def divide(j):
                        dve.wait_ge(raised, j + 1)
                        link(nc.vector.reciprocal(stat[:, 1, j:j + 1], stat[:, 0, j:j + 1]))
                        nc.vector.tensor_scalar_mul(vv[:, j, 0:64], vv[:, j, 0:64], stat[:, 1, j:j + 1]).then_inc(divided, 1)
                    for j in range(NT):
                        b0, nb = 3 * (j % 2), banks(j)
                        dve.wait_ge(scores, j + 1)
                        link(nc.vector.tensor_reduce(negmax[:, 0, j:j + 1], PS[0:PT, b0:b0 + nb, 0:CW], AX.XY, ALU.max, negate=True))
                        nc.vector.tensor_scalar_mul(negmax[:, 1, j:j + 1], negmax[:, 0, j:j + 1], 0.125).then_inc(maxed, 1)
                        if j:
                            divide(j - 1)
                    divide(NT - 1)
                    dve.wait_ge(summed, NT)
                    link(nc.vector.tensor_tensor(h[:, 0:TPB, :], h[:, 0:TPB, :], PS[0:PT, 6, :].rearrange("p (t d) -> p t d", d=D), ALU.add))
                    link(nc.vector.tensor_tensor(h[:, TPB:NT, :], h[:, TPB:NT, :], PS[0:PT, 7:8, 0:D], ALU.add))

                @block.scalar
                def _(act):
                    for j in range(NT):
                        b0, nb = 3 * (j % 2), banks(j)
                        act.wait_ge(maxed, j + 1)
                        if j >= 2:
                            act.wait_ge(summed, j - 1)
                        nc.scalar.activation(P[0:PT, j % 2, 0:CW * nb].rearrange("p (c n) -> p c n", n=CW), PS[0:PT, b0:b0 + nb, 0:CW], ACT.Exp,
                                             bias=negmax[:, 1, j:j + 1], scale=0.125, accum_out=stat[:, 0, j:j + 1]).then_inc(raised, 1)

        def grouped_block():
            normalise(h[:, :, :], xn[:, :, :], True, 1e-5)
            normalise(xn[:, :, :], tmp[:, :, 0:64], False, 1e-6)
            to_features([tmp[:, :, 0:64]], 64, [xT[0:64, :]], scale=rms1[:, :])
            x64 = xT[0:64]
            rotate(FA[0:64, 0, :], W["fq"][:, :], W["fqs"][:, :], 64, 2, x64)
            store_stacked(FA, 64, 1, scr_qc, SPLITS_Q, scale=0.25)
            rotate(FA[0:32, 0, :], W["fk"][:, :], W["fks"][:, :], 32, 2, x64)
            store_stacked(FA, 32, 1, scr_kc, SPLITS_K)
            v = vv[:, :, 0:34].rearrange("p t (h n) -> p t h n", n=17)
            set_ones(v[:, :, :, 16:17])
            token_products(32, lambda t: [(tile(x64, t), W["fv"][:, :])],
                           lambda t0, t1, tiles: nc.scalar.activation(v[:, t0:t1, :, 0:16], tiles.rearrange("p t (h n) -> p t h n", n=16), ACT.Copy), on="scalar")
            mask_pad_values(vv[:, NT - 1, 0:34])

            def combine(link, i, u, O):
                rec = nine(stat[:, u, 0:NT])
                link(nc.vector.reciprocal(rec, O[:, :, :, 16]))
                link(nc.vector.tensor_tensor(nine(sq[:, :, :].rearrange("p t (h n) -> p h t n", n=16)[:, i * 2 + u]), O[:, :, :, 0:16], over(rec, 16), ALU.mult))
            stacked_attention(4, 16, scr_qc, scr_kc, True, 17, True, True, False, combine)
            to_features([sq], 64, [xT[0:64, :]], pad=False)
            token_products(64, lambda t: [(tile(x64, t), W["fo"][:, :])],
                           lambda t0, t1, tiles: nc.vector.tensor_tensor(xn[:, t0:t1, :], xn[:, t0:t1, :], tiles, ALU.add))
            with step("added") as (block, added):
                @block.vector
                def _(dve):
                    nc.vector.tensor_tensor(h[:, :, :], h[:, :, :], xn[:, :, :], ALU.add).then_inc(added, 1)
            normalise(xn[:, :, :], tmp[:, :, 0:64], False, 1e-6)
            to_features([tmp[:, :, 0:64]], 64, [xT[0:64, :]], scale=rms2[:, :])
            route_top2(W["router"][:, :], 64, True)
            experts(8, 170, ACT.Silu, lambda e: A["L3_ffn_w1T"][e], None, lambda e: A["L3_ffn_w3T"][e],
                    lambda e: A["L3_ffn_w2T"].rearrange("e (g p) n -> e p g n", g=2)[e], None)

        layers = [differential_attention, mixture_of_depths, latent_attention, binary_experts, relative_attention, erf_experts,
                  column_attention, grouped_block]
        with nc.Fori(0, B) as b:
            tokeniser(b)
            for layer in layers[0:stop_after - 1]:
                layer()
            with step("stored") as (block, stored):
                @block.sync
                def _(sp):
                    full = NT - 1
                    sp.dma_start(out[:, 0:full * PT, :].rearrange("b (t p) d -> b p t d", p=PT)[b], h[:, 0:full, :]).then_inc(stored, 16)
                    sp.dma_start(out[:, full * PT:T, :][b], h[0:T - full * PT, full, :]).then_inc(stored, 16)
                    sp.wait_ge(stored, 32)


def diagonal(scr, which, head, first, width):
    base = scr[which, head]
    return bass.AP(base.tensor, base.offset + first - (PT - 1), [[1, PT], [1, width]])


def _layout(inputs):
    import numpy as np

    a = {k: np.ascontiguousarray(v) for k, v in inputs.items() if k != "L0_ffn_attention_mask"}
    row = lambda v: np.ascontiguousarray(v.reshape(1, -1))
    col = lambda v: np.ascontiguousarray(v.reshape(-1, 1))
    tr = lambda v: np.ascontiguousarray(np.swapaxes(v, -1, -2))
    out = {k: a[k] for k in ("x", "L0_tok_d_gamma_batched", "L0_tok_Wq", "L0_tok_Wk", "L0_tok_Wv", "L0_tok_Wo", "L0_attn_Wq", "L0_attn_Wkv",
                             "L0_attn_Wout", "L0_attn_Wg", "L0_ffn_wr", "L0_ffn_w1", "L0_ffn_w2", "L1_attn_Wq_comp", "L1_attn_Wkv_comp",
                             "L1_attn_Wqc", "L1_attn_Wqr", "L1_attn_Wkc", "L1_attn_Wkr", "L1_attn_Wv", "L2_attn_qkv_w", "L2_attn_proj_w",
                             "L2_ffn_Wg", "L2_ffn_W1", "L2_ffn_W2")}
    for k in ("L0_tok_bq", "L0_tok_bk", "L0_tok_bv", "L0_tok_bo", "L0_tok_prelu_a", "L0_attn_bout", "L0_attn_bg", "L0_attn_lq1", "L0_attn_lk1",
              "L0_attn_lq2", "L0_attn_lk2", "L0_attn_ln_gamma", "L0_attn_ln_beta", "L0_ffn_br", "L0_ffn_b1", "L0_ffn_b2", "L1_ffn_proj_b",
              "L2_attn_qkv_b", "L2_attn_proj_b", "L2_ffn_bg"):
        out[k] = row(a[k])
    for k in ("cls_tok", "L1_ffn_scale", "L3_ffn_ln1_w", "L3_ffn_ln2_w"):
        out[k] = col(a[k])
    for k in ("L2_ffn_b1", "L2_ffn_b2"):
        out[k] = np.ascontiguousarray(a[k][:, None, :])
    for k in ("L3_attn_Wq", "L3_attn_Wk", "L3_attn_Wv", "L3_ffn_wq", "L3_ffn_wk", "L3_ffn_wv", "L3_ffn_wo", "L1_ffn_proj_w",
              "L3_ffn_w1", "L3_ffn_w2", "L3_ffn_w3"):
        out[k + "T"] = tr(a[k])
    out["L3_ffn_routerT"] = tr(a["L3_ffn_router_w"])
    out["L1_ffn_weightT"] = np.ascontiguousarray(tr(a["L1_ffn_weight"][0]).reshape(8, -1))
    out["rpbT"] = tr(a["L2_attn_rpb_table"])
    out["rpbT_flipped"] = np.ascontiguousarray(out["rpbT"][:, ::-1])
    pair = np.arange(16) ^ 1
    out["L1_attn_Wqr_swapped"] = np.ascontiguousarray(a["L1_attn_Wqr"][:, pair])
    out["L1_attn_Wkr_swapped"] = np.ascontiguousarray(a["L1_attn_Wkr"][:, pair])
    half = lambda n: np.arange(n) ^ 8
    out["L3_ffn_wqT_rotated"] = np.ascontiguousarray(out["L3_ffn_wqT"][:, half(64)])
    out["L3_ffn_wkT_rotated"] = np.ascontiguousarray(out["L3_ffn_wkT"][:, half(32)])
    pos = np.arange(TP, dtype=np.float32)
    f = np.float32
    theta = f(1.0) / f(10000.0) ** (np.arange(8, dtype=f) / f(8))
    rope = np.zeros((64, 4, TP), f)
    rope[:48, 0] = 1.0
    for r in range(16):
        angle = pos * theta[r // 2]
        rope[48 + r, 0] = np.cos(angle)
        rope[48 + r, 1] = np.sin(angle) * (-1.0 if r % 2 == 0 else 1.0)
    for r in range(64):
        angle = pos * theta[r % 8]
        rope[r, 2] = np.cos(angle)
        rope[r, 3] = np.sin(angle) * (-1.0 if r % 16 < 8 else 1.0)
    out["rope"] = rope
    return out


STOP = LAST


def kernel(**inputs):
    import numpy as _np
    import concourse.bacc as _bacc
    from concourse import mybir as _mybir
    from concourse.bass_utils import run_bass_kernel_spmd as _run

    nc = _bacc.Bacc("TRN2", target_bir_lowering=False, num_devices=1)
    arrays, A = {}, {}
    for name, a in _layout(inputs).items():
        arrays["in_" + name] = a
        A[name] = nc.dram_tensor("in_" + name, a.shape, _mybir.dt.from_np(a.dtype), kind="ExternalInput").ap()
    bf = _mybir.dt.bfloat16
    scratch = [nc.dram_tensor(n, s, bf, kind="Internal").ap() for n, s in (
        ("scr_qa", (16, 16, 6, TP)), ("scr_ka", (16, 16, 6, TP)), ("scr_qb", (8, 8, 6, TP)), ("scr_kb", (8, 8, 6, TP)),
        ("scr_qc", (4, 16, 6, TP)), ("scr_kc", (2, 16, 6, TP)))]
    scratch.append(nc.dram_tensor("scr_t", (2, 8, 384), _mybir.dt.float32, kind="Internal").ap())
    out = nc.dram_tensor("out", (B, T, D), _mybir.dt.float32, kind="ExternalOutput").ap()
    build(nc, A, scratch, out, STOP)
    r = _run(nc, [arrays], core_ids=[0])
    return r.results[0]["out"]
```

```python
import math
from contextlib import ExitStack, contextmanager

import concourse.bass as bass
from concourse import mybir

B, T0, D = 8, 1024, 64
T = T0 + 1
PT, NT = 114, 9
TP = PT * NT
NC, CW = 3, 342
TPB = 8
LAMBDA_INIT = 0.8 - 0.6 * math.exp(-0.3)
CAPACITY = T // 2 - 1
NEG = -1e30
RPB = 127
RPB0 = T - 1 - (RPB - 1)
SPLITS_Q = (0, 0, 0, 1, 1, 2)
SPLITS_K = (0, 1, 2, 0, 1, 0)
LAST = 9


def build(nc, A, scratch, out, stop_after=LAST):
    fp32, bf16 = mybir.dt.float32, mybir.dt.bfloat16
    ALU, ACT, AX = mybir.AluOpType, mybir.ActivationFunctionType, mybir.AxisListType
    stack = ExitStack()

    pool_sems = [stack.enter_context(nc.semaphore(f"step_{n}")) for n in range(15)]
    assert pool_sems[-1].num - pool_sems[0].num == 14

    def sb(name, shape, dt=fp32):
        return stack.enter_context(nc.sbuf_tensor(name, shape, dt))

    @contextmanager
    def step(*names):
        used = pool_sems[0:len(names)]
        with nc.Block() as block:
            yield (block, *used)
        nc.all_engine_barrier(sems_to_clear=range(used[0].num, used[-1].num + 1))

    def chain(eng, sem):
        count = [0]

        def link(ins):
            count[0] += 1
            ins.then_inc(sem, 1)
            eng.wait_ge(sem, count[0])
        return link

    with stack:
        PS = stack.enter_context(nc.psum_tensor("PS", [128, 8, 512], fp32))

        ident = sb("ident", [128, 128])
        ident_bf = sb("ident_bf", [128, 128], bf16)
        flip = sb("flip", [PT, PT])
        mask_q = sb("mask_q", [PT, CW], bf16)
        mask_k = sb("mask_k", [PT, CW], bf16)
        mask_cols = sb("mask_cols", [PT, TP])
        mask_diag = sb("mask_diag", [PT, CW])
        earlier = sb("earlier", [PT, 2 * TP], bf16)
        select_o = sb("select_o", [128, 128], bf16)
        fold = sb("fold", [128, D])
        minus_half = sb("minus_half", [PT, NT])
        ones_row = sb("ones_row", [1, PT])
        real_row = sb("real_row", [PT, 1])
        split1 = sb("split1", [24, 1])
        split2 = sb("split2", [24, 1])
        gammaT = sb("gammaT", [128, 8, T0])
        bias_q = sb("bias_q", [PT, 2, 8, RPB])
        bias_k = sb("bias_k", [PT, 2, 8, 128])
        wsign = sb("wsign", [24, 64 * 64], bf16)
        W = {}
        for name, cols in (("tWq", 64), ("tWk", 64), ("tWv", 64), ("tWo", 64), ("aWg", 256), ("wr", 1), ("rWg", 8),
                           ("qkv", 192), ("wproj", 64)):
            W[name] = sb("w_" + name, [65, cols])
        for name, cols in (("aWq", 256), ("aWk", 256), ("aWv", 256), ("cq", 64), ("ckv", 64), ("lq", 64), ("lqs", 64),
                           ("lk", 64), ("lks", 64), ("lv", 64), ("gWq", 64), ("gWk", 64), ("gWv", 64), ("fq", 64),
                           ("fqs", 64), ("fk", 32), ("fks", 32), ("fv", 32), ("fo", 64), ("router", 8)):
            W[name] = sb("w_" + name, [64, cols])
        gate_w = sb("gate_w", [65, 24])
        aWout = sb("aWout", [128, 2, 64])
        aBout = sb("aBout", [1, 64])
        lam_in = sb("lam_in", [PT, 4, 16])
        lam = sb("lam", [PT, 8])
        ln_g = sb("ln_g", [PT, 32])
        ln_b = sb("ln_b", [PT, 32])
        prelu = sb("prelu", [64, 1])
        bscale = sb("bscale", [64, 1])
        rms1 = sb("rms1", [64, 1])
        rms2 = sb("rms2", [64, 1])
        rope = sb("rope", [64, 4, TP])
        wr_b = sb("wr_b", [65, PT])
        h = sb("h", [PT, NT, D])
        xn = sb("xn", [PT, NT, D])
        sq = sb("sq", [PT, NT, D])
        stat = sb("stat", [PT, 4, 72])
        xT = sb("xT", [65, TP])
        FA = sb("FA", [128, 2, TP])
        FB = sb("FB", [128, 2, TP])
        parts = sb("parts", [128, 3, 2 * TP], bf16)
        qk = [(sb("q_pair0", [128, 2, TP], bf16), sb("k_pair0", [128, 2, TP], bf16)),
              tuple(parts[:, s, :].rearrange("p (u n) -> p u n", u=2) for s in (0, 1)),
              tuple(FB[:, s, :].bitcast(bf16).rearrange("p (u n) -> p u n", u=2) for s in (0, 1))]
        vv = sb("vv", [PT, NT, 8 * 33])
        P = sb("P", [128, 4, TP])
        att = sb("att", [PT, NT, 256])
        att_rows = att[:, :, :].rearrange("p t n -> p (t n)")
        q65, k65 = att_rows[0:65, 0:TP], att_rows[0:65, TP:2 * TP]
        gates = sb("gates", [PT, NT, 256])
        tmp = sb("tmp", [PT, NT, 256])
        negmax = sb("negmax", [PT, 2, NT])
        partmax = sb("partmax", [PT, 2 * NT, NC])
        mparts = sb("mparts", [2 * NT, 3, PT], bf16)
        wd = sb("wd", [PT, 8, NT])
        vpair = sb("vpair", [PT, 2, NT, 33])
        stat_rows = sb("stat_rows", [2 * NT, PT])
        w1 = sb("w1", [65, 2, 256])
        w2 = sb("w2", [128, 2, D])
        b2 = sb("b2", [8, D])
        routing_rows = tmp[0:8 * NT, 0, 0:PT]
        lg = sb("lg", [PT, 5, NT, 8])
        cmp8 = tmp[:, :, 0:64].rearrange("p t (a b) -> p t a b", b=8)
        x_tok = FB[:, 0, 0:8 * D].rearrange("p (t d) -> p t d", d=D)

        scr_qa, scr_ka, scr_qb, scr_kb, scr_qc, scr_kc, scr_t, scr_w = scratch

        def bcast(ap, n):
            return ap.unsqueeze(2).to_broadcast([ap.shape[0], ap.shape[1], n])

        loads = [(W["tWq"][0:64, :], A["L0_tok_Wq"]), (W["tWq"][64:65, :], A["L0_tok_bq"]),
                 (W["tWk"][0:64, :], A["L0_tok_Wk"]), (W["tWk"][64:65, :], A["L0_tok_bk"]),
                 (W["tWv"][0:64, :], A["L0_tok_Wv"]), (W["tWv"][64:65, :], A["L0_tok_bv"]),
                 (W["tWo"][0:64, :], A["L0_tok_Wo"]), (W["tWo"][64:65, :], A["L0_tok_bo"]),
                 (W["aWq"][:, :], A["L0_attn_Wq"]), (W["aWk"][:, :], A["L0_attn_Wkv"][:, 0:256]),
                 (W["aWv"][:, :], A["L0_attn_Wkv"][:, 256:512]),
                 (W["aWg"][0:64, :], A["L0_attn_Wg"]), (W["aWg"][64:65, :], A["L0_attn_bg"]),
                 (W["wr"][0:64, :], A["L0_ffn_wr"]), (W["wr"][64:65, :], A["L0_ffn_br"]),
                 (W["rWg"][0:64, :], A["L2_ffn_Wg"]), (W["rWg"][64:65, :], A["L2_ffn_bg"]),
                 (W["qkv"][0:64, :], A["L2_attn_qkv_w"]), (W["qkv"][64:65, :], A["L2_attn_qkv_b"]),
                 (W["wproj"][0:64, :], A["L2_attn_proj_w"]), (W["wproj"][64:65, :], A["L2_attn_proj_b"]),
                 (W["cq"][:, :], A["L1_attn_Wq_comp"]), (W["ckv"][:, :], A["L1_attn_Wkv_comp"]),
                 (W["lq"][:, 0:48], A["L1_attn_Wqc"]), (W["lq"][:, 48:64], A["L1_attn_Wqr"]),
                 (W["lqs"][:, 0:48], A["L1_attn_Wqc"]), (W["lqs"][:, 48:64], A["L1_attn_Wqr_swapped"]),
                 (W["lk"][:, 0:48], A["L1_attn_Wkc"]), (W["lk"][:, 48:64], A["L1_attn_Wkr"]),
                 (W["lks"][:, 0:48], A["L1_attn_Wkc"]), (W["lks"][:, 48:64], A["L1_attn_Wkr_swapped"]),
                 (W["lv"][:, :], A["L1_attn_Wv"]),
                 (W["gWq"][:, :], A["L3_attn_WqT"]), (W["gWk"][:, :], A["L3_attn_WkT"]), (W["gWv"][:, :], A["L3_attn_WvT"]),
                 (W["fq"][:, :], A["L3_ffn_wqT"]), (W["fqs"][:, :], A["L3_ffn_wqT_rotated"]),
                 (W["fk"][:, :], A["L3_ffn_wkT"]), (W["fks"][:, :], A["L3_ffn_wkT_rotated"]),
                 (W["fv"][:, :], A["L3_ffn_wvT"]), (W["fo"][:, :], A["L3_ffn_woT"]), (W["router"][:, :], A["L3_ffn_routerT"]),
                 (aWout[:, :, :], A["L0_attn_Wout"].rearrange("(g p) n -> p g n", p=128)), (aBout[:, :], A["L0_attn_bout"]),
                 (ln_g[:, :], A["L0_attn_ln_gamma"].to_broadcast([PT, 32])),
                 (ln_b[:, :], A["L0_attn_ln_beta"].to_broadcast([PT, 32])),
                 (prelu[:, :], A["L0_tok_prelu_a"].to_broadcast([64, 1])),
                 (bscale[:, :], A["L1_ffn_scale"]), (rms1[:, :], A["L3_ffn_ln1_w"]), (rms2[:, :], A["L3_ffn_ln2_w"]),
                 (rope[:, :, :], A["rope"])]
        loads += [(lam_in[:, n, :], A["L0_attn_" + v].to_broadcast([PT, 16])) for n, v in enumerate(("lq1", "lk1", "lq2", "lk2"))]
        for part in range(3):
            loads += [(gate_w[0:64, 8 * part:8 * part + 8], A["L1_ffn_proj_wT"]), (gate_w[64:65, 8 * part:8 * part + 8], A["L1_ffn_proj_b"])]

        with step("weights_loaded", "zeroed", "made") as (block, weights_loaded, zeroed, made):
            @block.sync
            def _(sp):
                for dst, src in loads:
                    sp.dma_start(dst, src).then_inc(weights_loaded, 16)
                sp.wait_ge(weights_loaded, 16 * len(loads))

            @block.gpsimd
            def _(pool):
                cleared = [(t, 0.0) for t in (ident, ident_bf, flip, mask_q, mask_k, mask_diag, mask_cols, select_o)]
                cleared += [(t, 1.0) for t in (earlier, real_row, split1, split2, ones_row)] + [(minus_half, -0.5)]
                clear = chain(pool, zeroed)
                for t, value in cleared:
                    clear(nc.gpsimd.memset(t[tuple(slice(None) for _ in t.shape)], value))
                clear(nc.gpsimd.memset(xT[64:65, :], 1.0))
                link = chain(pool, made)

                def where(ap, compare, fill, base, pattern, channel):
                    link(nc.gpsimd.affine_select(out=ap, in_=ap, compare_op=compare, fill=fill, base=base,
                                                 pattern=pattern, channel_multiplier=channel))
                for m in (ident, ident_bf):
                    where(m[:, :], ALU.not_equal, 1.0, 0, [[-1, 128]], 1)
                where(flip[:, :], ALU.not_equal, 1.0, 1 - PT, [[1, PT]], 1)
                where(mask_q[:, :], ALU.is_ge, NEG, 0, [[-1, CW]], 1)
                where(mask_k[:, :], ALU.is_ge, NEG, PT - CW, [[1, CW]], -1)
                where(mask_cols[:, :], ALU.is_gt, -1e10, 0, [[-1, TP]], 1)
                where(mask_cols[:, T:TP], ALU.is_gt, NEG, -1, [[-1, 1]], 0)
                where(mask_diag[:, :], ALU.is_gt, -1e10, 0, [[-1, CW]], 1)
                where(mask_diag[:, :], ALU.is_gt, NEG, PT, [[-1, CW]], 0)
                where(earlier[:, :], ALU.is_gt, 0.0, TP, [[-1, 2 * TP]], 1)
                where(real_row[:, :], ALU.is_gt, 0.0, PT - 1, [[0, 1]], -1)
                where(split1[:, :], ALU.is_ge, 0.0, -8, [[0, 1]], 1)
                where(split2[:, :], ALU.is_ge, 0.0, -16, [[0, 1]], 1)
                link(nc.gpsimd.memset(select_o[0:64, 62:63], 1.0))
                link(nc.gpsimd.memset(select_o[64:128, 63:64], 1.0))

        with step("made", "raised", "loaded", "stored") as (block, made, raised, loaded, stored):
            table = FA[0:8, 0, 0:384]
            flipped = FA[0:8, 1, 0:384]
            raw = FB[0:8, 0, 0:2 * RPB + 1]

            @block.sync
            def _(sp):
                sp.dma_start(raw[:, 0:RPB], A["rpbT"]).then_inc(loaded, 16)
                sp.dma_start(raw[:, RPB:2 * RPB], A["rpbT_flipped"]).then_inc(loaded, 16)
                sp.wait_ge(made, 11)
                sp.dma_start(scr_t[0], table).then_inc(stored, 16)
                sp.dma_start(scr_t[1], flipped).then_inc(stored, 16)
                sp.wait_ge(stored, 32)

            @block.vector
            def _(dve):
                link = chain(dve, made)
                link(nc.vector.tensor_tensor(lam_in[:, 0, :], lam_in[:, 0, :], lam_in[:, 1, :], ALU.mult))
                link(nc.vector.tensor_tensor(lam_in[:, 2, :], lam_in[:, 2, :], lam_in[:, 3, :], ALU.mult))
                link(nc.vector.reduce_sum(lam[:, 0:1], lam_in[:, 0, :], AX.X))
                link(nc.vector.reduce_sum(lam[:, 1:2], lam_in[:, 2, :], AX.X))
                link(nc.vector.memset(FA[0:8, :, 0:384], 0.0))
                dve.wait_ge(loaded, 32)
                link(nc.vector.tensor_scalar(table[:, 1:1 + RPB], raw[:, 0:RPB], raw[:, RPB - 1:RPB], None, ALU.subtract))
                link(nc.vector.tensor_scalar(flipped[:, 227:227 + RPB], raw[:, RPB:2 * RPB], raw[:, RPB - 1:RPB], None, ALU.subtract))
                link(nc.vector.tensor_scalar_mul(ln_g[:, :], ln_g[:, :], 1.0 - LAMBDA_INIT))
                link(nc.vector.tensor_scalar_mul(ln_b[:, :], ln_b[:, :], 1.0 - LAMBDA_INIT))
                link(nc.vector.memset(wr_b[:, :], 1.0))
                link(nc.vector.tensor_tensor(fold[:, :], ident[:, 0:D], ident[:, D:2 * D], ALU.add))
                link(nc.vector.tensor_scalar_mul(wr_b[:, :], wr_b[:, :], W["wr"][:, :]))
                dve.wait_ge(raised, 1)
                link(nc.vector.tensor_tensor(lam[:, 4:5], lam[:, 3:4], lam[:, 2:3], ALU.subtract))
                link(nc.vector.tensor_scalar_add(lam[:, 5:6], lam[:, 4:5], -LAMBDA_INIT))

            @block.scalar
            def _(act):
                act.wait_ge(made, 4)
                nc.scalar.activation(lam[:, 2:4], lam[:, 0:2], ACT.Exp).then_inc(raised, 1)

        with step("loaded", "split") as (block, loaded, split):
            whole = FB[0:24, :, :].rearrange("p a n -> p (a n)")

            @block.sync
            def _(sp):
                for half in range(2):
                    for part in range(3):
                        sp.dma_start(P[8 * part:8 * part + 8, half, 0:1024], A["L1_ffn_weightT"][:, 2048 * half:2048 * half + 1024]).then_inc(loaded, 16)
                        sp.dma_start(FA[8 * part:8 * part + 8, half, 0:1024], A["L1_ffn_weightT"][:, 2048 * half + 1024:2048 * half + 2048]).then_inc(loaded, 16)
                for tile in range(2):
                    for head in range(8):
                        q0 = 227 - PT * tile
                        sp.dma_start(bias_q[:, tile, head, :], diagonal(scr_t, 1, head, q0, RPB)).then_inc(loaded, 16)
                        k0 = 1 + T - 1 - PT * (7 + tile)
                        sp.dma_start(bias_k[:, tile, head, :], diagonal(scr_t, 0, head, k0, 128)).then_inc(loaded, 16)
                sp.wait_ge(loaded, 16 * (12 + 32))

            @block.vector
            def _(dve):
                dve.wait_ge(loaded, 16 * (12 + 32))
                link = chain(dve, split)
                for q, buf in enumerate((P[0:24, 0, 0:1024], FA[0:24, 0, 0:1024], P[0:24, 1, 0:1024], FA[0:24, 1, 0:1024])):
                    dst = wsign[:, 1024 * q:1024 * q + 1024]
                    work = FB[0:24, 0, 0:1024]
                    for mask in (split1, split2):
                        link(nc.vector.tensor_copy(dst, buf))
                        link(nc.vector.tensor_scalar_mul(work, dst, mask[:, :]))
                        link(nc.vector.tensor_tensor(buf, buf, work, ALU.subtract))
                    link(nc.vector.tensor_copy(dst, buf))
                link(nc.vector.memset(bias_k[0:1, 1, :, :], 0.0))

        with step("loaded_even", "loaded_odd", "transposed", "copied") as (block, loaded_even, loaded_odd, transposed, copied):
            loaded = (loaded_even, loaded_odd)

            @block.sync
            def _(sp):
                for t in range(8):
                    if t >= 2:
                        sp.wait_ge(transposed, t - 1)
                    sp.dma_start(P[:, t % 2, 0:T0], A["L0_tok_d_gamma_batched"][128 * t:128 * t + 128, :]).then_inc(loaded[t % 2], 16)

            @block.tensor
            def _(pe):
                for t in range(8):
                    pe.wait_ge(loaded[t % 2], 16 * (t // 2 + 1))
                    if t >= 2:
                        pe.wait_ge(copied, t - 1)
                    for s in range(8):
                        last = nc.tensor.transpose(PS[:, 2 * (t % 2) + s // 4, 128 * (s % 4):128 * (s % 4) + 128],
                                                   P[:, t % 2, 128 * s:128 * s + 128], ident[:, :])
                    last.then_inc(transposed, 1)

            @block.scalar
            def _(act):
                for t in range(8):
                    act.wait_ge(transposed, t + 1)
                    nc.scalar.activation(gammaT[:, :, 128 * t:128 * t + 128].rearrange("p (a s) n -> p a s n", a=2),
                                         PS[:, 2 * (t % 2):2 * (t % 2) + 2, :].rearrange("p a (s n) -> p a s n", n=128),
                                         ACT.Copy).then_inc(copied, 1)

        def feature_banks(groups, terms, consume):
            def unit(g, c):
                def fill(bank):
                    pairs = terms(g, c)
                    for n, (lhsT, rhs) in enumerate(pairs):
                        last = nc.tensor.matmul(bank[0:lhsT.shape[-1], 0:CW], lhsT, rhs, start=(n == 0), stop=(n == len(pairs) - 1))
                    return last
                return fill, lambda bank: consume(g, c, bank[:, 0:CW])
            return [unit(g, c) for g in range(groups) for c in range(NC)]

        def token_banks(width, terms, consume):
            per = min(512 // width, NT)

            def unit(t0, t1):
                def fill(bank):
                    for t in range(t0, t1):
                        pairs = terms(t)
                        for n, (lhsT, rhs) in enumerate(pairs):
                            last = nc.tensor.matmul(bank[0:PT, width * (t - t0):width * (t - t0 + 1)], lhsT, rhs, start=(n == 0), stop=(n == len(pairs) - 1))
                    return last
                return fill, lambda bank: consume(t0, t1, bank[0:PT, 0:width * (t1 - t0)].rearrange("p (t n) -> p t n", n=width))
            return [unit(t0, min(NT, t0 + per)) for t0 in range(0, NT, per)]

        def through_banks(block, product, consumed, units, on):
            @block.tensor
            def _(pe):
                for n, (fill, _) in enumerate(units):
                    if n >= 8:
                        pe.wait_ge(consumed, n - 7)
                    fill(PS[:, n % 8, :]).then_inc(product, 1)

            def program(eng):
                for n, (_, take) in enumerate(units):
                    eng.wait_ge(product, n + 1)
                    take(PS[:, n % 8, :]).then_inc(consumed, 1)
            (block.vector if on == "vector" else block.scalar)(program)

        def feature_products(groups, terms, consume, on="vector"):
            with step("product", "consumed") as (block, product, consumed):
                through_banks(block, product, consumed, feature_banks(groups, terms, consume), on)

        def token_products(width, terms, consume, on="vector"):
            with step("product", "consumed") as (block, product, consumed):
                through_banks(block, product, consumed, token_banks(width, terms, consume), on)

        def tile(ap, t):
            return ap[:, PT * t:PT * t + PT]

        def chunk(ap, c):
            return ap[:, CW * c:CW * c + CW]

        def normalise(src, dst, layer, eps):
            with step("linked", "variance", "rstd") as (block, linked, variance, rstd):
                @block.vector
                def _(dve):
                    link = chain(dve, linked)
                    base = src
                    if layer:
                        link(nc.vector.reduce_sum(stat[:, 0, 0:NT], src, AX.X))
                        link(nc.vector.tensor_scalar_mul(stat[:, 1, 0:NT], stat[:, 0, 0:NT], -1.0 / D))
                        link(nc.vector.tensor_tensor(dst, src, bcast(stat[:, 1, 0:NT], D), ALU.add))
                        base = dst
                    link(nc.vector.tensor_tensor(sq[:, :, :], base, base, ALU.mult))
                    link(nc.vector.reduce_sum(stat[:, 2, 0:NT], sq[:, :, :], AX.X))
                    nc.vector.tensor_scalar(stat[:, 3, 0:NT], stat[:, 2, 0:NT], 1.0 / D, eps, ALU.mult, ALU.add).then_inc(variance, 1)
                    dve.wait_ge(rstd, 1)
                    link(nc.vector.tensor_tensor(dst, base, bcast(stat[:, 0, 0:NT], D), ALU.mult))

                @block.gpsimd
                def _(pool):
                    pool.wait_ge(variance, 1)
                    nc.gpsimd.tensor_tensor(stat[:, 0, 0:NT], stat[:, 3, 0:NT], minus_half[:, :], ALU.pow).then_inc(rstd, 1)

        def to_features(src, rows, dst, pad=True, scale=None):
            with step("transposed", "copied") as (block, transposed, copied):
                @block.tensor
                def _(pe):
                    for g, s in enumerate(src):
                        for t in range(NT):
                            last = nc.tensor.transpose(PS[0:rows, 3 * g + t // 3, PT * (t % 3):PT * (t % 3) + PT], s[:, t, :],
                                                       ident[0:PT, 0:PT])
                            if t % 3 == 2:
                                last.then_inc(transposed, 1)

                @block.vector
                def _(dve):
                    for g, d in enumerate(dst):
                        for c in range(NC):
                            dve.wait_ge(transposed, 3 * g + c + 1)
                            if scale is None:
                                nc.vector.tensor_copy(chunk(d, c), PS[0:rows, 3 * g + c, 0:CW]).then_inc(copied, 1)
                            else:
                                nc.vector.tensor_scalar_mul(chunk(d, c), PS[0:rows, 3 * g + c, 0:CW], scale).then_inc(copied, 1)
                    if pad:
                        dve.wait_ge(copied, 3 * len(dst))
                        for d in dst:
                            nc.vector.tensor_copy(d[:, T:TP], d[:, 0:1]).then_inc(copied, 1)

        def add_to_h(t0, t1, tiles):
            return nc.vector.tensor_tensor(h[:, t0:t1, :], h[:, t0:t1, :], tiles, ALU.add)

        def copy_chunk(dst, rows):
            return lambda g, c, bank: nc.scalar.activation(chunk(dst[g], c), bank[0:rows, :], ACT.Copy)

        def store_stacked(x, rows, groups, scr, splits, scale=1.0, beside=()):
            flat = x[0:rows, 0:groups, :].rearrange("p g n -> p (g n)")
            P1, P2, P3 = (parts[0:rows, s, 0:groups * TP] for s in range(3))
            with step("linked", "stored", "product", "consumed") as (block, linked, stored, product, consumed):
                if beside:
                    through_banks(block, product, consumed, beside, "scalar")

                @block.vector
                def _(dve):
                    link = chain(dve, linked)
                    if scale != 1.0:
                        link(nc.vector.tensor_scalar_mul(flat, flat, scale))
                    link(nc.vector.tensor_copy(P1, flat))
                    link(nc.vector.tensor_tensor(flat, flat, P1, ALU.subtract))
                    link(nc.vector.tensor_copy(P2, flat))
                    link(nc.vector.tensor_tensor(P3, flat, P2, ALU.subtract))

                @block.sync
                def _(sp):
                    count = 0
                    for slot, part in sorted(enumerate(splits), key=lambda sp_: sp_[1]):
                        sp.wait_ge(linked, (0, 1, 3, 4)[part + 1] + (scale != 1.0))
                        for g in range(groups):
                            sp.dma_start(scr.rearrange("h r s n -> (h r) s n")[rows * g:rows * g + rows, slot, :],
                                         parts[0:rows, part, TP * g:TP * g + TP]).then_inc(stored, 16)
                            count += 1
                    sp.wait_ge(stored, 16 * count)

        def attention_step(K, causal, bias, width, shared, maxima_of, values_of, before, load_next, combine):
            units_a = [(u, t, c) for u in range(2) for t in range(NT) for c in range(t // 3 + 1 if causal else NC)] if maxima_of else []
            units_b = [(j, c, u) for j in range(NT) for c in range(j // 3 if causal else 0, NC) for u in range(2)] if values_of else []
            groups = units_b[::2]
            BANKS_B, BANKS_A = 2, 3
            BATCH = 2 if causal or width > 32 else 4
            AHEAD = 6
            LAG = 3

            def summed_before(j):
                return sum(g[0] <= j for g in groups)

            def ring(j, u, c):
                first = (j % 2 * 2 + u) * TP + CW * c
                return P[0:PT, :, :].rearrange("p a n -> p (a n)")[:, first:first + CW]

            def place(u):
                return 64 * u

            with step("scores_a", "taken", "scores_b", "raised", "summed", "copied", "max_ready", "max_transposed", "max_split",
                      "max_stored", "out_transposed", "linked", "combined", "values_ready", "next_loaded") as (
                    block, scores_a, taken, scores_b, raised, summed, copied, max_ready, max_transposed, max_split,
                    max_stored, out_transposed, linked, combined, values_ready, next_loaded):
                @block.sync
                def _(sp):
                    if load_next:
                        load_next(sp, next_loaded)
                        sp.wait_ge(next_loaded, 16 * 4)
                    if maxima_of:
                        q = maxima_of[0]
                        sp.wait_ge(max_split, 1)
                        for u in range(2):
                            for part in range(3):
                                sp.dma_start(q[K + part:K + part + 1, u, :].rearrange("o (t n) -> o t n", n=PT),
                                             mparts[NT * u:NT * u + NT, part, :]).then_inc(max_stored, 16)
                        sp.wait_ge(max_stored, 16 * 6)

                @block.gpsimd
                def _(pool):
                    if values_of:
                        v, i = values_of[3:5]
                        for u in range(1 if shared else 2):
                            nc.gpsimd.tensor_copy(vpair[:, u, :, 0:width], v(i, u)).then_inc(values_ready, 1)

                @block.tensor
                def _(pe):
                    def query_major(n):
                        u, t, c = units_a[n]
                        q, k, heads = maxima_of[0:3]
                        if n >= BANKS_A:
                            pe.wait_ge(taken, n - BANKS_A + 1)
                        o = PS[0:PT, BANKS_B + n % BANKS_A, :]
                        masked = causal and c == t // 3
                        biased = bias and t < 2 and c == 2
                        last = nc.tensor.matmul(o[:, 0:CW], tile(q[0:K, u], t), chunk(k[0:K, u], c), start=True, stop=not (masked or biased))
                        if masked:
                            r = PT * (t % 3)
                            last = nc.tensor.matmul(o[:, r:CW], ident_bf[0:PT, 0:PT], mask_q[:, 0:CW - r], start=False, stop=True)
                        if biased:
                            k0 = RPB0 - 2 * CW
                            last = nc.tensor.matmul(o[:, k0:k0 + RPB], flip[:, :], bias_q[:, t, heads[u], :], start=False, stop=True)
                        last.then_inc(scores_a, 1)

                    def key_major(n):
                        j, c, u = units_b[n]
                        q, k, heads, v, i = values_of
                        if n >= BANKS_B:
                            pe.wait_ge(raised, n - BANKS_B + 1)
                        o = PS[0:PT, n % BANKS_B, :]
                        masked = causal and c == j // 3
                        biased = bias and j >= 7 and c == 0
                        last = nc.tensor.matmul(o[:, 0:CW], tile(k[0:K + 3, u], j), chunk(q[0:K + 3, u], c), start=True, stop=not (masked or biased))
                        if masked:
                            r = PT * (j % 3)
                            last = nc.tensor.matmul(o[:, 0:r + PT], ident_bf[0:PT, 0:PT], mask_k[:, CW - PT - r:CW], start=False, stop=True)
                        if biased:
                            last = nc.tensor.matmul(o[:, 0:128], flip[:, :], bias_k[:, j - 7, heads[u], :], start=False, stop=True)
                        last.then_inc(scores_b, 1)

                    def weigh(g):
                        if g == 0:
                            pe.wait_ge(values_ready, 1 if shared else 2)
                            if before is not None:
                                pe.wait_ge(combined, 2)
                        j, c, _ = groups[g]
                        pe.wait_ge(raised, 2 * g + 2)
                        for u in range(2):
                            p0 = place(u)
                            last = nc.tensor.matmul(PS[p0:p0 + width, 5 + c, 0:CW], vpair[:, 0 if shared else u, j, 0:width], ring(j, u, c),
                                                    start=(j == 0), stop=(j == (3 * c + 2 if causal else NT - 1)))
                        last.then_inc(summed, 1)

                    def transpose_sums():
                        for t in range(NT):
                            last = nc.tensor.transpose(PS[0:PT, 5 + t // 3, 97 * (t % 3):97 * (t % 3) + 97], tile(sums, t), ident[0:97, 0:97])
                        last.then_inc(out_transposed, 1)
                    def transpose_maxima():
                        pe.wait_ge(max_ready, 1)
                        nc.tensor.transpose(PS[0:2 * NT, 3, 0:PT], negmax[:, :, :].rearrange("p u t -> p (u t)"), ident[0:PT, 0:PT]).then_inc(max_transposed, 1)

                    a = g = 0
                    if not maxima_of and not values_of:
                        transpose_sums()
                    for n in range(len(units_b)):
                        key_major(n)
                        while a < min(len(units_a), (n + 1) * AHEAD // 4):
                            query_major(a)
                            a += 1
                        if n == 1 and before is not None:
                            transpose_sums()
                        if maxima_of and n == min(4 * len(units_a) // AHEAD + 3, len(units_b) - 1):
                            transpose_maxima()
                        while n % BATCH == BATCH - 1 and 2 * g + 2 + LAG <= n:
                            weigh(g)
                            g += 1
                    for g in range(g, len(groups)):
                        weigh(g)
                    if not values_of:
                        for a in range(a, len(units_a)):
                            query_major(a)
                        if maxima_of:
                            transpose_maxima()

                def copy_sums(eng, u):
                    whole = sums[64 * u:64 * u + width]
                    for c in range(NC):
                        eng.wait_ge(summed, max(n for n, g in enumerate(groups) if g[1] == c) + 1)
                        dst, src = chunk(whole, c), PS[place(u):place(u) + width, 5 + c, 0:CW]
                        (nc.scalar.activation(dst, src, ACT.Copy) if u == 0 else nc.vector.tensor_copy(dst, src)).then_inc(copied, 1)

                @block.scalar
                def _(act):
                    for n, (j, c, u) in enumerate(units_b):
                        act.wait_ge(scores_b, n + 1)
                        if j >= 2:
                            act.wait_ge(summed, summed_before(j - 2))
                        nc.scalar.activation(ring(j, u, c), PS[0:PT, n % BANKS_B, 0:CW], ACT.Exp).then_inc(raised, 1)
                    if values_of:
                        copy_sums(act, 0)

                @block.vector
                def _(dve):
                    link, read = chain(dve, linked), chain(dve, combined)

                    def combine_before(u):
                        if u == 0:
                            dve.wait_ge(out_transposed, 1)
                        combine(link, read, before[-1], u, PS[0:PT, 5:8, 0:3 * 97].rearrange("p a (b n) -> p a b n", n=97)[:, :, :, 64 * u:64 * u + width])
                    after = {2: 0, 5: 1} if units_a else {}
                    if before is not None and not units_a:
                        combine_before(0)
                        combine_before(1)
                    for n, (u, t, c) in enumerate(units_a):
                        dve.wait_ge(scores_a, n + 1)
                        nc.vector.tensor_reduce(partmax[:, NT * u + t, c:c + 1], PS[0:PT, BANKS_B + n % BANKS_A, 0:CW], AX.X, ALU.max).then_inc(taken, 1)
                        if before is not None and n in after:
                            combine_before(after[n])
                    if maxima_of:
                        dve.wait_ge(taken, len(units_a))
                        nc.vector.tensor_reduce(negmax[:, :, :].rearrange("p u t -> p (u t)"), partmax[:, :, :], AX.X, ALU.max, negate=True).then_inc(max_ready, 1)
                        dve.wait_ge(max_transposed, 1)
                        rows = PS[0:2 * NT, 3, 0:PT]
                        p1, p2, p3 = (mparts[:, s, :] for s in range(3))
                        rest = stat_rows[:, :]
                        link(nc.vector.tensor_copy(p1, rows))
                        link(nc.vector.tensor_tensor(rest, rows, p1, ALU.subtract))
                        link(nc.vector.tensor_copy(p2, rest))
                        nc.vector.tensor_tensor(p3, rest, p2, ALU.subtract).then_inc(max_split, 1)
                    if values_of:
                        copy_sums(dve, 1)

        sums = FA[0:97, 0, :]

        def stacked_attention(nh, d, scr_q, scr_k, shared_keys, width, shared_values, causal, bias, combine):
            K = 6 * d
            pairs = nh // 2

            def v_of(i, u):
                n = nh // 2 if shared_values else nh
                heads = vv[:, :, 0:n * width].rearrange("p t (h n) -> p h t n", n=width)
                return heads[:, i if shared_values else i * 2 + u]

            def load(sp, i, turn, sem):
                q, k = qk[turn % 3]
                for u in range(2):
                    sp.dma_start(q[0:K, u, :], scr_q.rearrange("h r s n -> h (r s) n")[i * 2 + u]).then_inc(sem, 16)
                    sp.dma_start(k[0:K, u, :], scr_k.rearrange("h r s n -> h (r s) n")[i if shared_keys else i * 2 + u]).then_inc(sem, 16)

            with step("ones_written", "cleared", "loaded") as (block, ones_written, cleared, loaded):
                base = K // 32 * 32

                @block.gpsimd
                def _(pool):
                    nc.gpsimd.memset(qk[1][1][base:base + 32, :, :], 1.0).then_inc(cleared, 1)

                @block.vector
                def _(dve):
                    nc.vector.memset(qk[0][1][base:base + 32, :, :], 1.0).then_inc(ones_written, 1)
                    nc.vector.memset(qk[2][1][base:base + 32, :, :], 1.0).then_inc(cleared, 1)
                    nc.vector.memset(FA[0:97, 0, :], 0.0).then_inc(cleared, 1)
                    nc.vector.memset(partmax[:, :, :], NEG).then_inc(cleared, 1)

                @block.sync
                def _(sp):
                    sp.wait_ge(ones_written, 1)
                    load(sp, 0, 0, loaded)
                    sp.wait_ge(loaded, 16 * 4)

            def run(place, i=None, following=None):
                looped = i is not None
                if not looped:
                    i, following = place, place + 2

                def side(n):
                    if looped or 0 <= i + n < pairs:
                        return (*qk[(place + n) % 3], [(i + n) * 2, (i + n) * 2 + 1], v_of, i + n)
                loads = looped or following < pairs
                attention_step(K, causal, bias, width, shared_values, side(1), side(0), side(-1),
                               (lambda sp, sem: load(sp, following, place + 2, sem)) if loads else None, combine)

            run(-1)
            run(0)
            turns = 2 if pairs == 8 else 0
            if turns:
                with nc.Fori(0, turns) as turn:
                    run(1, turn * 3 + 1, turn * 3 + 3)
                    run(2, turn * 3 + 2, turn * 3 + 4)
                    run(3, turn * 3 + 3, turn * 2 + 5)
            for i in range(1 + 3 * turns, pairs + 1):
                run(i)

        def nine(ap):
            return ap.rearrange("p (a b) n -> p a b n", b=3) if len(ap.shape) == 3 else ap.rearrange("p (a b) -> p a b", b=3)

        def over(ap, n):
            return ap.unsqueeze(3).to_broadcast([*ap.shape, n])

        def mask_pad_values(ap):
            with step("masked") as (block, masked):
                @block.vector
                def _(dve):
                    nc.vector.tensor_scalar_mul(ap, ap, real_row[:, :]).then_inc(masked, 1)

        def set_ones(ap):
            with step("set") as (block, done):
                @block.gpsimd
                def _(pool):
                    nc.gpsimd.memset(ap, 1.0).then_inc(done, 1)

        def experts(count, hidden, func, w1_of, b1_of, w3_of, w2_of, b2_all):
            F = hidden // 2
            K = 65 if b1_of else 64
            n_loads = 3 + bool(b1_of) + bool(w3_of)
            gate_rows = gates[:, :, :].rearrange("p t n -> p (t n)")
            first = (w1, gate_rows[0:65, 0:512].rearrange("p (a n) -> p a n", a=2))
            second = (w2, P[:, 2, 0:2 * D].rearrange("p (g n) -> p g n", g=2))
            routing = (P[:, 0, :], P[:, 1, :])
            wd_rows, wdT = routing_rows, FB[0:count, 0, :]
            shares = scr_w[0:count, :]

            def load(sp, e, turn, sem):
                wa, wb = first[turn % 2], second[turn % 2]
                row = scr_w[e:e + 1, :] if isinstance(e, int) else scr_w.rearrange("e (o n) -> e o n", o=1)[e]
                sp.dma_start(wa[0:64, 0, 0:hidden], w1_of(e)).then_inc(sem, 16)
                sp.dma_start(wb[0:F, :, :], w2_of(e)).then_inc(sem, 16)
                sp.dma_start(routing[turn % 2][0:F, :], row.to_broadcast([F, TP])).then_inc(sem, 16)
                if b1_of:
                    sp.dma_start(wa[64:65, 0, 0:hidden], b1_of(e)).then_inc(sem, 16)
                if w3_of:
                    sp.dma_start(wa[0:64, 1, 0:hidden], w3_of(e)).then_inc(sem, 16)

            with step("transposed", "copied", "stored", "loaded") as (block, transposed, copied, stored, loaded):
                @block.tensor
                def _(pe):
                    nc.tensor.transpose(PS[0:count * NT, 0, 0:PT], wd[:, 0:count, :].rearrange("p e t -> p (e t)"), ident[0:PT, 0:PT]).then_inc(transposed, 1)

                @block.vector
                def _(dve):
                    dve.wait_ge(transposed, 1)
                    nc.vector.tensor_copy(wd_rows[0:count * NT, :], PS[0:count * NT, 0, 0:PT]).then_inc(copied, 1)

                @block.sync
                def _(sp):
                    sp.wait_ge(copied, 1)
                    sp.dma_start(shares.rearrange("e (t n) -> (e t) n", n=PT), wd_rows[0:count * NT, :]).then_inc(stored, 16)
                    sp.wait_ge(stored, 16)
                    load(sp, 0, 0, loaded)
                    if b2_all is not None:
                        sp.dma_start(wdT, shares).then_inc(loaded, 16)
                        sp.dma_start(b2[0:count, :], b2_all).then_inc(loaded, 16)
                    sp.wait_ge(loaded, 16 * (n_loads + 2 * (b2_all is not None)))

            def expert(turn, is_first, is_last, following):
                wa, wb, shares_row = first[turn % 2], second[turn % 2], routing[turn % 2]
                units = [(c, j) for c in range(NC) for j in range(2)]
                per = 2 if w3_of else 1
                SLOTS = 4 // per
                with step("loaded", "hidden_ready", "activated", "shared", "weighted", "output") as (
                        block, loaded, hidden_ready, activated, shared, weighted, output):
                    @block.sync
                    def _(sp):
                        if following is not None:
                            load(sp, following, turn + 1, loaded)
                            sp.wait_ge(loaded, 16 * n_loads)

                    @block.tensor
                    def _(pe):
                        def add_up(c):
                            pe.wait_ge(weighted, 2 * c + 2)
                            for j in range(2):
                                last = nc.tensor.matmul(PS[64 * j:64 * j + D, 5 + c, 0:CW], wb[0:F, j, :], chunk(FA[0:F, j], c), start=is_first,
                                                        stop=is_last, skip_group_check=True)
                            if is_first and b2_all is not None:
                                last = nc.tensor.matmul(PS[0:D, 5 + c, 0:CW], b2[0:count, :], chunk(wdT, c), start=False, stop=is_last,
                                                        skip_group_check=True)
                            last.then_inc(output, 1)
                        for n, (c, j) in enumerate(units):
                            if n >= SLOTS:
                                pe.wait_ge(activated, n - SLOTS + 1)
                                if w3_of:
                                    pe.wait_ge(shared, n - SLOTS + 1)
                            bank = n % SLOTS * per
                            last = nc.tensor.matmul(PS[0:F, bank, 0:CW], wa[0:K, 0, F * j:F * j + F], chunk(xT[0:K], c), start=True, stop=True)
                            if w3_of:
                                last = nc.tensor.matmul(PS[0:F, bank + 1, 0:CW], wa[0:64, 1, F * j:F * j + F], chunk(xT[0:64], c), start=True, stop=True)
                            last.then_inc(hidden_ready, 1)
                            if n in (3, 5):
                                add_up(n // 2 - 1)
                        add_up(NC - 1)

                    @block.scalar
                    def _(act):
                        for n, (c, j) in enumerate(units):
                            act.wait_ge(hidden_ready, n + 1)
                            nc.scalar.activation(chunk(FA[0:F, j], c), PS[0:F, n % SLOTS * per, 0:CW], func).then_inc(activated, 1)

                    @block.vector
                    def _(dve):
                        for n, (c, j) in enumerate(units):
                            share = chunk(shares_row[0:F], c)
                            if w3_of:
                                dve.wait_ge(hidden_ready, n + 1)
                                share = chunk(FB[0:F, 1], n % NC)
                                nc.vector.tensor_tensor(share, PS[0:F, n % SLOTS * per + 1, 0:CW], chunk(shares_row[0:F], c), ALU.mult).then_inc(shared, 1)
                                dve.wait_ge(shared, n + 1)
                            dve.wait_ge(activated, n + 1)
                            nc.vector.tensor_tensor(chunk(FA[0:F, j], c), chunk(FA[0:F, j], c), share, ALU.mult).then_inc(weighted, 1)

            expert(0, True, count == 1, 1 if count > 1 else None)
            if count > 1:
                with nc.Fori(0, count // 2 - 1) as two:
                    expert(1, False, False, two * 2 + 2)
                    expert(2, False, False, two * 2 + 3)
                expert(1, False, True, None)
            with step("copied") as (block, copied):
                @block.scalar
                def _(act):
                    for c in (0, 2):
                        nc.scalar.activation(chunk(FA[:, 0], c), PS[:, 5 + c, 0:CW], ACT.Copy).then_inc(copied, 1)

                @block.vector
                def _(dve):
                    nc.vector.tensor_copy(chunk(FA[:, 0], 1), PS[:, 6, 0:CW]).then_inc(copied, 1)
            token_products(64, lambda t: [(tile(FA[:, 0], t), fold[:, :])], add_to_h)

        def route_top2(weights, K, probabilities):
            logit, shifted, raised_, key, chosen = (lg[:, n, :, :] for n in range(5))
            token_products(8, lambda t: [(tile(xT[0:K], t), weights)],
                           lambda t0, t1, tiles: nc.vector.tensor_copy(logit[:, t0:t1, :], tiles))
            with step("linked", "shift_ready", "raised") as (block, linked, shift_ready, raised):
                @block.vector
                def _(dve):
                    link = chain(dve, linked)
                    link(nc.vector.reduce_max(stat[:, 0, 0:NT], logit, AX.X))
                    nc.vector.tensor_tensor(shifted, logit, bcast(stat[:, 0, 0:NT], 8), ALU.subtract).then_inc(shift_ready, 1)
                    dve.wait_ge(raised, 1)
                    score = logit
                    if probabilities:
                        link(nc.vector.reduce_sum(stat[:, 1, 0:NT], raised_, AX.X))
                        link(nc.vector.reciprocal(stat[:, 2, 0:NT], stat[:, 1, 0:NT]))
                        link(nc.vector.tensor_tensor(key, raised_, bcast(stat[:, 2, 0:NT], 8), ALU.mult))
                        score = key
                    value = score if probabilities else raised_
                    for e in range(8):
                        own = score[:, :, e:e + 1]
                        link(nc.vector.tensor_tensor(cmp8[:, :, 0:e + 1, e], own.to_broadcast([PT, NT, e + 1]), score[:, :, 0:e + 1], ALU.is_gt))
                        if e < 7:
                            link(nc.vector.tensor_tensor(cmp8[:, :, e + 1:8, e], own.to_broadcast([PT, NT, 7 - e]), score[:, :, e + 1:8], ALU.is_ge))
                    link(nc.vector.reduce_sum(chosen, cmp8[:, :, :, :], AX.X))
                    link(nc.vector.tensor_scalar(chosen, chosen, 2.0, None, ALU.is_lt))
                    link(nc.vector.tensor_tensor(chosen, chosen, value, ALU.mult))
                    link(nc.vector.reduce_sum(stat[:, 1, 0:NT], chosen, AX.X))
                    if probabilities:
                        link(nc.vector.tensor_scalar_add(stat[:, 1, 0:NT], stat[:, 1, 0:NT], 1e-9))
                    link(nc.vector.reciprocal(stat[:, 2, 0:NT], stat[:, 1, 0:NT]))
                    link(nc.vector.tensor_tensor(wd[:, :, :].rearrange("p e t -> p t e"), chosen, bcast(stat[:, 2, 0:NT], 8), ALU.mult))

                @block.scalar
                def _(act):
                    act.wait_ge(shift_ready, 1)
                    nc.scalar.activation(raised_, shifted, ACT.Exp).then_inc(raised, 1)

        def tokeniser(b):
            hT = FB[0:64, 1, :]
            q, k, ret = FA[0:64, 0, 0:T0], FA[0:64, 1, 0:T0], q65
            v = vv[:, :, 0:64]
            vt = x_tok
            with step("loaded", "transposed", "copied", "padded") as (block, loaded, transposed, copied, padded):
                @block.sync
                def _(sp):
                    sp.dma_start(x_tok[:, :, :], A["x"].rearrange("b o (t p) d -> b (o p) t d", p=128)[b]).then_inc(loaded, 16)
                    sp.dma_start(hT[:, 0:1], A["cls_tok"]).then_inc(loaded, 16)

                @block.tensor
                def _(pe):
                    pe.wait_ge(loaded, 32)
                    for t in range(8):
                        last = nc.tensor.transpose(PS[0:64, t // 4, 128 * (t % 4):128 * (t % 4) + 128], x_tok[:, t, :], ident[:, :])
                    last.then_inc(transposed, 1)

                @block.scalar
                def _(act):
                    act.wait_ge(transposed, 1)
                    nc.scalar.activation(xT[0:64, 0:T0].rearrange("p (a n) -> p a n", a=2), PS[0:64, 0:2, :], ACT.Copy).then_inc(copied, 1)

                @block.gpsimd
                def _(pool):
                    nc.gpsimd.memset(hT[:, T:TP], 0.0).then_inc(padded, 1)
                    pool.wait_ge(padded, 1)
                    nc.gpsimd.memset(q65[64:65, :], 1.0).then_inc(padded, 1)

            with step("product", "copied") as (block, product, copied):
                @block.tensor
                def _(pe):
                    for n, w in enumerate((W["tWq"], W["tWk"])):
                        for c in range(2):
                            nc.tensor.matmul(PS[0:64, 2 * n + c, :], w[:, :], xT[:, 512 * c:512 * c + 512], start=True, stop=True).then_inc(product, 1)
                    for t in range(8):
                        last = nc.tensor.matmul(PS[:, 4, D * t:D * t + D], xT[:, 128 * t:128 * t + 128], W["tWv"][:, :], start=True, stop=True)
                    last.then_inc(product, 1)

                @block.scalar
                def _(act):
                    for n, dst in enumerate((q, k)):
                        act.wait_ge(product, 2 * n + 2)
                        nc.scalar.activation(dst.rearrange("p (a n) -> p a n", a=2), PS[0:64, 2 * n:2 * n + 2, :], ACT.Copy).then_inc(copied, 1)

                @block.vector
                def _(dve):
                    dve.wait_ge(product, 5)
                    nc.vector.tensor_copy(vt[:, :, :], PS[:, 4, :].rearrange("p (t d) -> p t d", d=D)).then_inc(copied, 1)

            with step("scores", "decayed", "summed", "copied") as (block, scores, decayed, summed, copied):
                @block.tensor
                def _(pe):
                    def weigh(s):
                        pe.wait_ge(decayed, s + 1)
                        for c in range(2):
                            last = nc.tensor.matmul(PS[64 * c:64 * c + 64, 6 + c, :], vt[:, s, :], P[:, s % 2, 512 * c:512 * c + 512], start=(s == 0), stop=(s == 7))
                        last.then_inc(summed, 1)
                    for s in range(8):
                        if s >= 2:
                            pe.wait_ge(decayed, s - 1)
                        for c in range(2):
                            last = nc.tensor.matmul(PS[:, 2 * (s % 2) + c, :], k[:, 128 * s:128 * s + 128], q[:, 512 * c:512 * c + 512], start=True, stop=True)
                        last.then_inc(scores, 1)
                        if s:
                            weigh(s - 1)
                    weigh(7)

                @block.vector
                def _(dve):
                    for s in range(8):
                        dve.wait_ge(scores, s + 1)
                        if s >= 2:
                            dve.wait_ge(summed, s - 1)
                        nc.vector.tensor_tensor(P[:, s % 2, 0:T0].rearrange("p (a n) -> p a n", a=2), gammaT[:, s, :].rearrange("p (a n) -> p a n", a=2),
                                                PS[:, 2 * (s % 2):2 * (s % 2) + 2, :], ALU.mult).then_inc(decayed, 1)

                @block.scalar
                def _(act):
                    act.wait_ge(summed, 8)
                    for c in range(2):
                        nc.scalar.activation(ret[0:64, 512 * c:512 * c + 512], PS[64 * c:64 * c + 64, 6 + c, :], ACT.Copy).then_inc(copied, 1)

            with step("product", "linked") as (block, product, linked):
                @block.tensor
                def _(pe):
                    for c in range(2):
                        last = nc.tensor.matmul(PS[0:64, c, :], W["tWo"][:, :], ret[:, 512 * c:512 * c + 512], start=True, stop=True)
                    last.then_inc(product, 1)

                @block.vector
                def _(dve):
                    link = chain(dve, linked)
                    y = PS[0:64, 0:2, :]
                    below = FA[0:64, 0, 0:T0].rearrange("p (a n) -> p a n", a=2)
                    dve.wait_ge(product, 1)
                    link(nc.vector.tensor_scalar(below, y, 0.0, prelu[:, :], ALU.min, ALU.mult))
                    link(nc.vector.scalar_tensor_tensor(hT[:, 1:T].rearrange("p (a n) -> p a n", a=2), y, 0.0, below, ALU.max, ALU.add))

            with step("transposed", "copied") as (block, transposed, copied):
                @block.tensor
                def _(pe):
                    for t in range(NT):
                        last = nc.tensor.transpose(PS[0:PT, t // TPB, D * (t % TPB):D * (t % TPB) + D], tile(hT, t), ident[0:64, 0:64])
                    last.then_inc(transposed, 1)

                @block.vector
                def _(dve):
                    dve.wait_ge(transposed, 1)
                    nc.vector.tensor_copy(h[:, 0:TPB, :], PS[0:PT, 0, :].rearrange("p (t d) -> p t d", d=D)).then_inc(copied, 1)
                    nc.vector.tensor_copy(h[:, TPB:NT, :], PS[0:PT, 1:2, 0:D]).then_inc(copied, 1)

        def normed(eps=1e-5):
            normalise(h[:, :, :], xn[:, :, :], True, eps)
            to_features([xn], 64, [xT[0:64, :]])

        def differential_attention():
            normed()
            x64 = xT[0:64]
            v = vv[:, :, :].rearrange("p t (h n) -> p t h n", n=33)
            set_ones(v[:, :, :, 32:33])

            def project(w, dst):
                return feature_banks(2, lambda g, c: [(W[w][:, 128 * g:128 * g + 128], chunk(x64, c))], copy_chunk([dst[:, 0, :], dst[:, 1, :]], 128))
            with step("product", "consumed") as (block, product, consumed):
                through_banks(block, product, consumed, project("aWq", FA), "scalar")
            to_values = token_banks(256, lambda t: [(tile(x64, t), W["aWv"][:, :])], lambda t0, t1, tiles: nc.scalar.activation(
                v[:, t0:t1, :, 0:32], tiles.rearrange("p t (h n) -> p t h n", n=32), ACT.Copy))
            to_gates = token_banks(256, lambda t: [(tile(xT, t), W["aWg"][:, :])],
                                   lambda t0, t1, tiles: nc.scalar.activation(gates[:, t0:t1, :], tiles, ACT.Sigmoid))
            store_stacked(FA, 128, 2, scr_qa, SPLITS_Q, scale=0.25, beside=project("aWk", FB) + to_values)
            store_stacked(FB, 128, 2, scr_ka, SPLITS_K, beside=to_gates)
            mask_pad_values(vv[:, NT - 1, :])

            def combine(link, read, i, u, O):
                rec, half = nine(stat[:, u, 0:NT]), nine(tmp[:, :, 32 * u:32 * u + 32])
                link(nc.vector.reciprocal(rec, O[:, :, :, 32]))
                if u:
                    link(nc.vector.tensor_scalar_mul(rec, rec, lam[:, 5:6]))
                read(nc.vector.tensor_tensor(half, O[:, :, :, 0:32], over(rec, 32), ALU.mult))
                if u:
                    link(nc.vector.tensor_tensor(att[:, :, :].rearrange("p t (i n) -> p i t n", n=32)[:, i], tmp[:, :, 0:32], tmp[:, :, 32:64], ALU.add))
            stacked_attention(16, 16, scr_qa, scr_ka, False, 33, True, False, False, combine)

            with step("linked", "variance", "deviation") as (block, linked, variance, deviation):
                a3 = att[:, :, :].rearrange("p t (h n) -> p (t h) n", n=32)
                t3 = tmp[:, :, :].rearrange("p t (h n) -> p (t h) n", n=32)

                @block.vector
                def _(dve):
                    link = chain(dve, linked)
                    link(nc.vector.reduce_sum(stat[:, 0, :], a3, AX.X))
                    link(nc.vector.tensor_scalar_mul(stat[:, 1, :], stat[:, 0, :], -1.0 / 32))
                    link(nc.vector.tensor_tensor(a3, a3, bcast(stat[:, 1, :], 32), ALU.add))
                    link(nc.vector.tensor_tensor(t3, a3, a3, ALU.mult))
                    link(nc.vector.reduce_sum(stat[:, 2, :], t3, AX.X))
                    nc.vector.tensor_scalar(stat[:, 3, :], stat[:, 2, :], 1.0 / 32, 1e-5, ALU.mult, ALU.add).then_inc(variance, 1)
                    dve.wait_ge(deviation, 1)
                    link(nc.vector.reciprocal(stat[:, 0, :], stat[:, 2, :]))
                    link(nc.vector.tensor_tensor(a3, a3, bcast(stat[:, 0, :], 32), ALU.mult))
                    link(nc.vector.tensor_tensor(a3, a3, ln_g[:, :].unsqueeze(1).to_broadcast([PT, 72, 32]), ALU.mult))
                    link(nc.vector.tensor_tensor(a3, a3, ln_b[:, :].unsqueeze(1).to_broadcast([PT, 72, 32]), ALU.add))
                    link(nc.vector.tensor_tensor(att[:, :, :], att[:, :, :], gates[:, :, :], ALU.mult))

                @block.scalar
                def _(act):
                    act.wait_ge(variance, 1)
                    nc.scalar.activation(stat[:, 2, :], stat[:, 3, :], ACT.Sqrt).then_inc(deviation, 1)
            to_features([att[:, :, 0:128], att[:, :, 128:256]], 128, [FA[:, 0, :], FA[:, 1, :]], pad=False)
            token_products(64, lambda t: [(tile(FA[:, 0], t), aWout[:, 0, :]), (tile(FA[:, 1], t), aWout[:, 1, :]), (ones_row[:, :], aBout[:, :])], add_to_h)

        def mixture_of_depths():
            normed()
            with step("product", "copied", "linked") as (block, product, copied, linked):
                wb = P[0:PT, 0, :]

                @block.tensor
                def _(pe):
                    for c in range(NC):
                        last = nc.tensor.matmul(PS[0:PT, c, 0:CW], wr_b[:, :], chunk(xT, c), start=True, stop=True)
                    last.then_inc(product, 1)

                @block.scalar
                def _(act):
                    act.wait_ge(product, 1)
                    nc.scalar.activation(wb.rearrange("p (c n) -> p c n", n=CW), PS[0:PT, 0:3, 0:CW], ACT.Copy).then_inc(copied, 1)

                @block.vector
                def _(dve):
                    link = chain(dve, linked)
                    own, more, ties = stat[:, 0, 0:NT], stat[:, 1, 0:NT], stat[:, 2, 0:NT]
                    work = P[0:PT, 1, :]
                    dve.wait_ge(copied, 1)
                    link(nc.vector.tensor_tensor(work.rearrange("p (t n) -> p t n", n=PT), wb.rearrange("p (t n) -> p t n", n=PT),
                                                 ident[0:PT, 0:PT].unsqueeze(1).to_broadcast([PT, NT, PT]), ALU.mult))
                    link(nc.vector.reduce_sum(own, work.rearrange("p (t n) -> p t n", n=PT), AX.X))
                    for t in range(NT):
                        link(nc.vector.tensor_scalar(work[:, 0:T], wb[:, 0:T], own[:, t:t + 1], None, ALU.is_gt, ALU.add, accum_out=more[:, t:t + 1]))
                        link(nc.vector.scalar_tensor_tensor(work[:, 0:T], wb[:, 0:T], own[:, t:t + 1], earlier[:, TP - PT * t:TP - PT * t + T],
                                                            ALU.is_equal, ALU.mult, accum_out=ties[:, t:t + 1]))
                    link(nc.vector.tensor_tensor(more, more, ties, ALU.add))
                    link(nc.vector.tensor_scalar(more, more, float(CAPACITY), None, ALU.is_lt))
                    link(nc.vector.tensor_tensor(wd[:, 0, :], more, own, ALU.mult))
                    link(nc.vector.tensor_tensor(h[:, :, :], h[:, :, :], xn[:, :, :], ALU.add))
            experts(1, 256, ACT.Gelu_apprx_tanh, lambda e: A["L0_ffn_w1"], lambda e: A["L0_ffn_b1"], None,
                    lambda e: A["L0_ffn_w2"].rearrange("(g p) n -> p g n", g=2), A["L0_ffn_b2"])

        def rotate(dst, main, swapped, rows, table, x, scale=1.0):
            def consume(g, c, bank):
                return nc.vector.tensor_tensor(chunk((dst, FB[0:rows, 1])[g], c), bank[0:rows, :],
                                               rope[0:rows, table + g, CW * c:CW * c + CW], ALU.mult)
            feature_products(2, lambda g, c: [((main, swapped)[g], chunk(x, c))], consume)
            with step("linked") as (block, linked):
                @block.vector
                def _(dve):
                    link = chain(dve, linked)
                    link(nc.vector.tensor_tensor(dst, dst, FB[0:rows, 1, :], ALU.add))
                    if scale != 1.0:
                        link(nc.vector.tensor_scalar_mul(dst, dst, scale))

        def latent_attention():
            normed()
            cq, ckv = FA[0:64, 0, :], FA[0:64, 1, :]
            feature_products(2, lambda g, c: [(W[("cq", "ckv")[g]][:, :], chunk(xT[0:64], c))], copy_chunk([cq, ckv], 64), on="scalar")
            rotate(q65[0:64], W["lq"][:, :], W["lqs"][:, :], 64, 0, cq, scale=0.125)
            rotate(k65[0:64], W["lk"][:, :], W["lks"][:, :], 64, 0, ckv)
            set_ones(vv[:, :, 64:65])
            set_ones(k65[64:65, :])
            token_products(64, lambda t: [(tile(ckv, t), W["lv"][:, :])],
                           lambda t0, t1, tiles: nc.vector.tensor_copy(vv[:, t0:t1, 0:64], tiles))
            mask_pad_values(vv[:, NT - 1, 0:65])
            wide_maxima_pass()
            with step("transposed", "copied") as (block, transposed, copied):
                @block.tensor
                def _(pe):
                    for t in range(NT):
                        last = nc.tensor.transpose(PS[0:1, t // 3, PT * (t % 3):PT * (t % 3) + PT], negmax[:, 0, t:t + 1], ident[0:PT, 0:PT])
                    last.then_inc(transposed, 1)

                @block.vector
                def _(dve):
                    dve.wait_ge(transposed, 1)
                    nc.vector.tensor_copy(q65[64:65, :].rearrange("p (c n) -> p c n", n=CW), PS[0:1, 0:3, 0:CW]).then_inc(copied, 1)
            wide_values_pass()

        def wide_maxima_pass():
            with step("scores", "taken") as (block, scores, taken):
                @block.tensor
                def _(pe):
                    for t in range(NT):
                        if t >= 2:
                            pe.wait_ge(taken, t - 1)
                        b0, nb, r = 3 * (t % 2), t // 3 + 1, PT * (t % 3)
                        for c in range(nb):
                            last = nc.tensor.matmul(PS[0:PT, b0 + c, 0:CW], tile(q65[0:64], t), chunk(k65[0:64], c), start=True, stop=(c != nb - 1))
                        last = nc.tensor.matmul(PS[0:PT, b0 + nb - 1, r:CW], ident_bf[0:PT, 0:PT], mask_q[:, 0:CW - r], start=False, stop=True)
                        last.then_inc(scores, 1)

                @block.vector
                def _(dve):
                    for t in range(NT):
                        b0, nb = 3 * (t % 2), t // 3 + 1
                        dve.wait_ge(scores, t + 1)
                        nc.vector.tensor_reduce(negmax[:, 0, t:t + 1], PS[0:PT, b0:b0 + nb, 0:CW], AX.XY, ALU.max, negate=True).then_inc(taken, 1)

        def wide_values_pass():
            with step("scores", "raised", "summed", "linked") as (block, scores, raised, summed, linked):
                def O(t):
                    return PS[0:PT, 6 + t // 5, 65 * (t % 5):65 * (t % 5) + 65]

                @block.tensor
                def _(pe):
                    def weigh(j):
                        pe.wait_ge(raised, j + 1)
                        for t in range(j, NT):
                            last = nc.tensor.matmul(O(t), tile(P[0:PT, j % 2], t), vv[:, j, 0:65], start=(j == 0 and t in (0, 5)),
                                                    stop=(j == t), skip_group_check=True)
                        last.then_inc(summed, 1)
                    for j in range(NT):
                        if j >= 2:
                            pe.wait_ge(raised, j - 1)
                        b0, c0, r = 3 * (j % 2), j // 3, PT * (j % 3)
                        for c in range(c0, NC):
                            first = r if c == c0 else 0
                            last = nc.tensor.matmul(PS[0:PT, b0 + c, first:CW], tile(k65[0:65], j), q65[0:65, CW * c + first:CW * c + CW],
                                                    start=True, stop=(c != c0))
                            if c == c0:
                                last = nc.tensor.matmul(PS[0:PT, b0 + c, first:first + PT], ident_bf[0:PT, 0:PT], mask_k[:, CW - PT:CW], start=False, stop=True)
                        last.then_inc(scores, 1)
                        if j:
                            weigh(j - 1)
                    weigh(NT - 1)

                @block.scalar
                def _(act):
                    for j in range(NT):
                        b0, c0, r = 3 * (j % 2), j // 3, PT * (j % 3)
                        act.wait_ge(scores, j + 1)
                        if j >= 2:
                            act.wait_ge(summed, j - 1)
                        if r:
                            last = nc.scalar.activation(P[0:PT, j % 2, CW * c0 + r:CW * c0 + CW], PS[0:PT, b0 + c0, r:CW], ACT.Exp)
                            c0 += 1
                        if c0 < NC:
                            last = nc.scalar.activation(P[0:PT, j % 2, CW * c0:TP].rearrange("p (c n) -> p c n", n=CW), PS[0:PT, b0 + c0:b0 + NC, 0:CW], ACT.Exp)
                        last.then_inc(raised, 1)

                @block.vector
                def _(dve):
                    link = chain(dve, linked)
                    dve.wait_ge(summed, NT)
                    for bank, t0, t1 in ((6, 0, 5), (7, 5, NT)):
                        o = PS[0:PT, bank, 0:65 * (t1 - t0)].rearrange("p (t n) -> p t n", n=65)
                        link(nc.vector.reciprocal(stat[:, 0, t0:t1], o[:, :, 64]))
                        link(nc.vector.tensor_tensor(sq[:, t0:t1, :], o[:, :, 0:64], bcast(stat[:, 0, t0:t1], 64), ALU.mult))
                    link(nc.vector.tensor_tensor(h[:, :, :], h[:, :, :], sq[:, :, :], ALU.add))

        def binary_experts():
            normed()
            gate = parts[0:24, 0, 0:TP]
            signs = parts[:, 1, 0:TP]
            feature_products(1, lambda g, c: [(gate_w[:, :], chunk(xT, c))],
                             lambda g, c, bank: nc.vector.tensor_scalar(chunk(gate, c), bank[0:24, :], 2.0 ** -23, None, ALU.is_gt))
            with step("signed") as (block, signed):
                @block.scalar
                def _(act):
                    for half in range(2):
                        nc.scalar.activation(signs[64 * half:64 * half + 64, :], xT[0:64, :], ACT.Sign).then_inc(signed, 1)
            pairs = D // 2
            with step("mixed", "signed", "multiplied", "summed", "scaled") as (block, mixed, signed, multiplied, summed, scaled):
                SLOTS = 4
                sg, pr = FA, FB
                sgb = FA[:, :, :].bitcast(bf16).rearrange("p a n -> p (a n)")
                prb = FB[:, :, :].bitcast(bf16).rearrange("p a n -> p (a n)")
                units = [(o, c) for o in range(pairs) for c in range(NC)]

                @block.tensor
                def _(pe):
                    def add_up(n):
                        o, c = units[n]
                        pe.wait_ge(multiplied, n + 1)
                        nc.tensor.matmul(PS[0:64, c, 0:CW], select_o[:, 62 - 2 * o:126 - 2 * o], prb[:, CW * (n % SLOTS):CW * (n % SLOTS) + CW],
                                         start=(o == 0), stop=(o == pairs - 1)).then_inc(summed, 1)
                    for n, (o, c) in enumerate(units):
                        if n >= SLOTS:
                            pe.wait_ge(signed, n - SLOTS + 1)
                        nc.tensor.matmul(PS[:, 3 + n % SLOTS, 0:CW], wsign[:, 128 * o:128 * o + 128], chunk(gate, c), start=True, stop=True).then_inc(mixed, 1)
                        if n >= 2:
                            add_up(n - 2)
                    add_up(len(units) - 2)
                    add_up(len(units) - 1)

                @block.scalar
                def _(act):
                    for n in range(len(units)):
                        act.wait_ge(mixed, n + 1)
                        if n >= SLOTS:
                            act.wait_ge(multiplied, n - SLOTS + 1)
                        nc.scalar.activation(sgb[:, CW * (n % SLOTS):CW * (n % SLOTS) + CW], PS[:, 3 + n % SLOTS, 0:CW], ACT.Sign).then_inc(signed, 1)

                @block.vector
                def _(dve):
                    for n, (o, c) in enumerate(units):
                        dve.wait_ge(signed, n + 1)
                        if n >= SLOTS:
                            dve.wait_ge(summed, n - SLOTS + 1)
                        nc.vector.tensor_tensor(prb[:, CW * (n % SLOTS):CW * (n % SLOTS) + CW], sgb[:, CW * (n % SLOTS):CW * (n % SLOTS) + CW],
                                                chunk(signs, c), ALU.mult).then_inc(multiplied, 1)
                    dve.wait_ge(summed, len(units))
                    nc.vector.tensor_scalar_mul(q65[0:64, :].rearrange("p (c n) -> p c n", n=CW), PS[0:64, 0:3, 0:CW], bscale[:, :]).then_inc(scaled, 1)
            token_products(64, lambda t: [(tile(q65[0:64], t), ident[0:64, 0:64])], add_to_h)

        def relative_attention():
            normed()
            feature_products(2, lambda g, c: [(W["qkv"][:, 64 * g:64 * g + 64], chunk(xT, c))],
                             copy_chunk([FA[0:64, 0, :], FB[0:64, 0, :]], 64), on="scalar")
            store_stacked(FA, 64, 1, scr_qb, SPLITS_Q, scale=8 ** -0.5)
            v = vv[:, :, 0:72].rearrange("p t (h n) -> p t h n", n=9)
            set_ones(v[:, :, :, 8:9])
            store_stacked(FB, 64, 1, scr_kb, SPLITS_K, beside=token_banks(64, lambda t: [(tile(xT, t), W["qkv"][:, 128:192])],
                lambda t0, t1, tiles: nc.scalar.activation(v[:, t0:t1, :, 0:8], tiles.rearrange("p t (h n) -> p t h n", n=8), ACT.Copy)))
            mask_pad_values(vv[:, NT - 1, 0:72])

            def combine(link, read, i, u, O):
                rec = nine(stat[:, u, 0:NT])
                link(nc.vector.reciprocal(rec, O[:, :, :, 8]))
                read(nc.vector.tensor_tensor(nine(sq[:, :, :].rearrange("p t (h n) -> p h t n", n=8)[:, i * 2 + u]), O[:, :, :, 0:8], over(rec, 8), ALU.mult))
            stacked_attention(8, 8, scr_qb, scr_kb, False, 9, False, False, True, combine)
            to_features([sq], 64, [xT[0:64, :]], pad=False)
            token_products(64, lambda t: [(tile(xT, t), W["wproj"][:, :])], add_to_h)

        def erf_experts():
            normed()
            route_top2(W["rWg"][:, :], 65, False)
            experts(8, 256, ACT.Gelu, lambda e: A["L2_ffn_W1"][e], lambda e: A["L2_ffn_b1"][e], None,
                    lambda e: A["L2_ffn_W2"].rearrange("e (g p) n -> e p g n", g=2)[e], A["L2_ffn_b2"])

        def column_attention():
            normed()
            x64 = xT[0:64]
            q, k = FA[0:64, 0, :], FA[0:64, 1, :]
            feature_products(2, lambda g, c: [(W[("gWq", "gWk")[g]][:, :], chunk(x64, c))], copy_chunk([q, k], 64), on="scalar")
            token_products(64, lambda t: [(tile(x64, t), W["gWv"][:, :])],
                           lambda t0, t1, tiles: nc.vector.tensor_copy(vv[:, t0:t1, 0:64], tiles))
            mask_pad_values(vv[:, NT - 1, 0:64])
            with step("scores", "maxed", "raised", "divided", "summed", "linked") as (block, scores, maxed, raised, divided, summed, linked):
                def banks(j):
                    return NC if j == 0 else j // 3 + 1

                def O(t):
                    return PS[0:PT, 6 + t // TPB, D * (t % TPB):D * (t % TPB) + D]

                @block.tensor
                def _(pe):
                    def weigh(j):
                        pe.wait_ge(divided, j + 1)
                        for t in range(NT if j == 0 else j + 1):
                            last = nc.tensor.matmul(O(t), tile(P[0:PT, j % 2], t), vv[:, j, 0:64], start=(j == 0 and t in (0, TPB)), stop=(j == NT - 1),
                                                    skip_group_check=True)
                        last.then_inc(summed, 1)
                    for j in range(NT):
                        b0, nb = 3 * (j % 2), banks(j)
                        if j >= 2:
                            pe.wait_ge(raised, j - 1)
                        for c in range(nb):
                            masked = j == 0 or c == nb - 1
                            last = nc.tensor.matmul(PS[0:PT, b0 + c, 0:CW], tile(k, j), chunk(q, c), start=True, stop=not masked)
                            if masked:
                                r = 0 if j == 0 else PT * (j % 3)
                                m = chunk(mask_cols, c) if j == 0 else mask_diag[:, 0:CW - r]
                                last = nc.tensor.matmul(PS[0:PT, b0 + c, r:CW], ident[0:PT, 0:PT], m, start=False, stop=True)
                        last.then_inc(scores, 1)
                        if j:
                            weigh(j - 1)
                    weigh(NT - 1)

                @block.vector
                def _(dve):
                    link = chain(dve, linked)

                    def divide(j):
                        dve.wait_ge(raised, j + 1)
                        link(nc.vector.reciprocal(stat[:, 1, j:j + 1], stat[:, 0, j:j + 1]))
                        nc.vector.tensor_scalar_mul(vv[:, j, 0:64], vv[:, j, 0:64], stat[:, 1, j:j + 1]).then_inc(divided, 1)
                    for j in range(NT):
                        b0, nb = 3 * (j % 2), banks(j)
                        dve.wait_ge(scores, j + 1)
                        link(nc.vector.tensor_reduce(negmax[:, 0, j:j + 1], PS[0:PT, b0:b0 + nb, 0:CW], AX.XY, ALU.max, negate=True))
                        nc.vector.tensor_scalar_mul(negmax[:, 1, j:j + 1], negmax[:, 0, j:j + 1], 0.125).then_inc(maxed, 1)
                        if j:
                            divide(j - 1)
                    divide(NT - 1)
                    dve.wait_ge(summed, NT)
                    link(nc.vector.tensor_tensor(h[:, 0:TPB, :], h[:, 0:TPB, :], PS[0:PT, 6, :].rearrange("p (t d) -> p t d", d=D), ALU.add))
                    link(nc.vector.tensor_tensor(h[:, TPB:NT, :], h[:, TPB:NT, :], PS[0:PT, 7:8, 0:D], ALU.add))

                @block.scalar
                def _(act):
                    for j in range(NT):
                        b0, nb = 3 * (j % 2), banks(j)
                        act.wait_ge(maxed, j + 1)
                        if j >= 2:
                            act.wait_ge(summed, j - 1)
                        nc.scalar.activation(P[0:PT, j % 2, 0:CW * nb].rearrange("p (c n) -> p c n", n=CW), PS[0:PT, b0:b0 + nb, 0:CW], ACT.Exp,
                                             bias=negmax[:, 1, j:j + 1], scale=0.125, accum_out=stat[:, 0, j:j + 1]).then_inc(raised, 1)

        def grouped_block():
            normalise(h[:, :, :], xn[:, :, :], True, 1e-5)
            normalise(xn[:, :, :], tmp[:, :, 0:64], False, 1e-6)
            to_features([tmp[:, :, 0:64]], 64, [xT[0:64, :]], scale=rms1[:, :])
            x64 = xT[0:64]
            rotate(FA[0:64, 0, :], W["fq"][:, :], W["fqs"][:, :], 64, 2, x64)
            store_stacked(FA, 64, 1, scr_qc, SPLITS_Q, scale=0.25)
            rotate(FA[0:32, 0, :], W["fk"][:, :], W["fks"][:, :], 32, 2, x64)
            v = vv[:, :, 0:34].rearrange("p t (h n) -> p t h n", n=17)
            set_ones(v[:, :, :, 16:17])
            store_stacked(FA, 32, 1, scr_kc, SPLITS_K, beside=token_banks(32, lambda t: [(tile(x64, t), W["fv"][:, :])],
                lambda t0, t1, tiles: nc.scalar.activation(v[:, t0:t1, :, 0:16], tiles.rearrange("p t (h n) -> p t h n", n=16), ACT.Copy)))
            mask_pad_values(vv[:, NT - 1, 0:34])

            def combine(link, read, i, u, O):
                rec = nine(stat[:, u, 0:NT])
                link(nc.vector.reciprocal(rec, O[:, :, :, 16]))
                read(nc.vector.tensor_tensor(nine(sq[:, :, :].rearrange("p t (h n) -> p h t n", n=16)[:, i * 2 + u]), O[:, :, :, 0:16], over(rec, 16), ALU.mult))
            stacked_attention(4, 16, scr_qc, scr_kc, True, 17, True, True, False, combine)
            to_features([sq], 64, [xT[0:64, :]], pad=False)
            token_products(64, lambda t: [(tile(x64, t), W["fo"][:, :])],
                           lambda t0, t1, tiles: nc.vector.tensor_tensor(xn[:, t0:t1, :], xn[:, t0:t1, :], tiles, ALU.add))
            with step("added") as (block, added):
                @block.vector
                def _(dve):
                    nc.vector.tensor_tensor(h[:, :, :], h[:, :, :], xn[:, :, :], ALU.add).then_inc(added, 1)
            normalise(xn[:, :, :], tmp[:, :, 0:64], False, 1e-6)
            to_features([tmp[:, :, 0:64]], 64, [xT[0:64, :]], scale=rms2[:, :])
            route_top2(W["router"][:, :], 64, True)
            experts(8, 170, ACT.Silu, lambda e: A["L3_ffn_w1T"][e], None, lambda e: A["L3_ffn_w3T"][e],
                    lambda e: A["L3_ffn_w2T"].rearrange("e (g p) n -> e p g n", g=2)[e], None)

        layers = [differential_attention, mixture_of_depths, latent_attention, binary_experts, relative_attention, erf_experts,
                  column_attention, grouped_block]
        with nc.Fori(0, B) as b:
            tokeniser(b)
            for layer in layers[0:stop_after - 1]:
                layer()
            with step("stored") as (block, stored):
                @block.sync
                def _(sp):
                    full = NT - 1
                    sp.dma_start(out[:, 0:full * PT, :].rearrange("b (t p) d -> b p t d", p=PT)[b], h[:, 0:full, :]).then_inc(stored, 16)
                    sp.dma_start(out[:, full * PT:T, :][b], h[0:T - full * PT, full, :]).then_inc(stored, 16)
                    sp.wait_ge(stored, 32)


def diagonal(scr, which, head, first, width):
    base = scr[which, head]
    return bass.AP(base.tensor, base.offset + first - (PT - 1), [[1, PT], [1, width]])


def _layout(inputs):
    import numpy as np

    a = {k: np.ascontiguousarray(v) for k, v in inputs.items() if k != "L0_ffn_attention_mask"}
    row = lambda v: np.ascontiguousarray(v.reshape(1, -1))
    col = lambda v: np.ascontiguousarray(v.reshape(-1, 1))
    tr = lambda v: np.ascontiguousarray(np.swapaxes(v, -1, -2))
    out = {k: a[k] for k in ("x", "L0_tok_d_gamma_batched", "L0_tok_Wq", "L0_tok_Wk", "L0_tok_Wv", "L0_tok_Wo", "L0_attn_Wq", "L0_attn_Wkv",
                             "L0_attn_Wout", "L0_attn_Wg", "L0_ffn_wr", "L0_ffn_w1", "L0_ffn_w2", "L1_attn_Wq_comp", "L1_attn_Wkv_comp",
                             "L1_attn_Wqc", "L1_attn_Wqr", "L1_attn_Wkc", "L1_attn_Wkr", "L1_attn_Wv", "L2_attn_qkv_w", "L2_attn_proj_w",
                             "L2_ffn_Wg", "L2_ffn_W1", "L2_ffn_W2")}
    for k in ("L0_tok_bq", "L0_tok_bk", "L0_tok_bv", "L0_tok_bo", "L0_tok_prelu_a", "L0_attn_bout", "L0_attn_bg", "L0_attn_lq1", "L0_attn_lk1",
              "L0_attn_lq2", "L0_attn_lk2", "L0_attn_ln_gamma", "L0_attn_ln_beta", "L0_ffn_br", "L0_ffn_b1", "L0_ffn_b2", "L1_ffn_proj_b",
              "L2_attn_qkv_b", "L2_attn_proj_b", "L2_ffn_bg"):
        out[k] = row(a[k])
    for k in ("cls_tok", "L1_ffn_scale", "L3_ffn_ln1_w", "L3_ffn_ln2_w"):
        out[k] = col(a[k])
    out["L2_ffn_b1"] = np.ascontiguousarray(a["L2_ffn_b1"][:, None, :])
    out["L2_ffn_b2"] = a["L2_ffn_b2"]
    for k in ("L3_attn_Wq", "L3_attn_Wk", "L3_attn_Wv", "L3_ffn_wq", "L3_ffn_wk", "L3_ffn_wv", "L3_ffn_wo", "L1_ffn_proj_w",
              "L3_ffn_w1", "L3_ffn_w2", "L3_ffn_w3"):
        out[k + "T"] = tr(a[k])
    out["L3_ffn_routerT"] = tr(a["L3_ffn_router_w"])
    out["L1_ffn_weightT"] = np.ascontiguousarray(tr(a["L1_ffn_weight"][0]).reshape(8, -1))
    out["rpbT"] = tr(a["L2_attn_rpb_table"])
    out["rpbT_flipped"] = np.ascontiguousarray(out["rpbT"][:, ::-1])
    pair = np.arange(16) ^ 1
    out["L1_attn_Wqr_swapped"] = np.ascontiguousarray(a["L1_attn_Wqr"][:, pair])
    out["L1_attn_Wkr_swapped"] = np.ascontiguousarray(a["L1_attn_Wkr"][:, pair])
    half = lambda n: np.arange(n) ^ 8
    out["L3_ffn_wqT_rotated"] = np.ascontiguousarray(out["L3_ffn_wqT"][:, half(64)])
    out["L3_ffn_wkT_rotated"] = np.ascontiguousarray(out["L3_ffn_wkT"][:, half(32)])
    pos = np.arange(TP, dtype=np.float32)
    f = np.float32
    theta = f(1.0) / f(10000.0) ** (np.arange(8, dtype=f) / f(8))
    rope = np.zeros((64, 4, TP), f)
    rope[:48, 0] = 1.0
    for r in range(16):
        angle = pos * theta[r // 2]
        rope[48 + r, 0] = np.cos(angle)
        rope[48 + r, 1] = np.sin(angle) * (-1.0 if r % 2 == 0 else 1.0)
    for r in range(64):
        angle = pos * theta[r % 8]
        rope[r, 2] = np.cos(angle)
        rope[r, 3] = np.sin(angle) * (-1.0 if r % 16 < 8 else 1.0)
    out["rope"] = rope
    return out


STOP = LAST


def kernel(**inputs):
    import numpy as _np
    import concourse.bacc as _bacc
    from concourse import mybir as _mybir
    from concourse.bass_utils import run_bass_kernel_spmd as _run

    nc = _bacc.Bacc("TRN2", target_bir_lowering=False, num_devices=1)
    arrays, A = {}, {}
    for name, a in _layout(inputs).items():
        arrays["in_" + name] = a
        A[name] = nc.dram_tensor("in_" + name, a.shape, _mybir.dt.from_np(a.dtype), kind="ExternalInput").ap()
    bf = _mybir.dt.bfloat16
    scratch = [nc.dram_tensor(n, s, bf, kind="Internal").ap() for n, s in (
        ("scr_qa", (16, 16, 6, TP)), ("scr_ka", (16, 16, 6, TP)), ("scr_qb", (8, 8, 6, TP)), ("scr_kb", (8, 8, 6, TP)),
        ("scr_qc", (4, 16, 6, TP)), ("scr_kc", (2, 16, 6, TP)))]
    scratch += [nc.dram_tensor("scr_t", (2, 8, 384), _mybir.dt.float32, kind="Internal").ap(),
                nc.dram_tensor("scr_w", (8, TP), _mybir.dt.float32, kind="Internal").ap()]
    out = nc.dram_tensor("out", (B, T, D), _mybir.dt.float32, kind="ExternalOutput").ap()
    build(nc, A, scratch, out, STOP)
    r = _run(nc, [arrays], core_ids=[0])
    return r.results[0]["out"]
```
